# Optimizing a Trainium2 kernel written in Bass

```python
import numpy as np
import jax
import jax.numpy as jnp

def _softmax(x, axis=-1):
    return jax.nn.softmax(x, axis=axis)

def _gelu(x):
    return jax.nn.gelu(x, approximate=True)

def _silu(x):
    return jax.nn.silu(x)

def _sigmoid(x):
    return jax.nn.sigmoid(x)

def _layernorm(x, axis=-1, eps=1e-05):
    m = jnp.mean(x, axis=axis, keepdims=True)
    v = jnp.var(x, axis=axis, keepdims=True)
    return (x - m) / jnp.sqrt(v + eps)

def _scatter_add(tgt, idx, src, axis=0):
    return tgt.at[idx].add(src)

def _segment_sum(src, seg, n):
    return jax.ops.segment_sum(src, seg, n)
kernel_name = 'mk_gnn_ffn_d2_gnn_r8_128244'

def setup_inputs(seed: int=0):
    np.random.seed(seed)
    _w = jnp.asarray

    def _rec_inputs():
        import jax
        import jax.numpy as jnp
        _gk = jax.random.key(seed)
        x = -0.0001394 + 0.9999 * jax.random.normal(jax.random.fold_in(_gk, 1), (1250, 768), jnp.float32)
        _s = jax.random.randint(jax.random.fold_in(_gk, 2), (20000,), 0, 1250, jnp.int32)
        _d = jax.random.randint(jax.random.fold_in(_gk, 3), (20000,), 0, 1250, jnp.int32)
        _loop = jnp.arange(1250, dtype=jnp.int32)
        src = jnp.concatenate([_s, _d, _loop])
        dst = jnp.concatenate([_d, _s, _loop])
        _o = jnp.argsort(dst, stable=True)
        src = src[_o]
        dst = dst[_o]
        edge_weight = jax.random.uniform(jax.random.fold_in(_gk, 12), (41250,), jnp.float32, 0.0, 0.999998)
        return (x, src, dst, edge_weight)
    x, src, dst, edge_weight = _rec_inputs()

    def _L0_gnn_setup():
        import jax, jax.numpy as jnp
        import numpy as np
        N = 6250
        E = 62500
        D = 768
        H = 256
        R = 32

        def _gcn(x, W, b, row, col, ew):
            x = x @ W
            n = x.shape[0]
            deg = jax.ops.segment_sum(ew, col, num_segments=n) + 1.0
            dinv = jax.lax.rsqrt(deg)
            norm = dinv[row] * ew * dinv[col]
            agg = jax.ops.segment_sum(norm[:, None] * x[row], col, num_segments=n)
            return agg + (dinv * dinv)[:, None] * x + b
        key = jax.random.key(seed)
        ks = jax.random.split(key, 8)
        d = D // R
        w = lambda k, sh: jax.random.normal(k, sh, jnp.float32) * 0.05
        return {'x': jax.random.normal(ks[0], (N, D), jnp.float32), 'edge_index': jax.random.randint(ks[1], (2, E), 0, N), 'edge_weight': jax.random.uniform(ks[2], (E,), jnp.float32), 'Wd': w(ks[3], (D, d)), 'bd': jnp.zeros((d,), jnp.float32), 'Wu': w(ks[4], (d, D)), 'bu': jnp.zeros((D,), jnp.float32), 'W1': w(ks[5], (D, H)), 'b1': jnp.zeros((H,), jnp.float32), 'W2': w(ks[6], (H, D)), 'b2': jnp.zeros((D,), jnp.float32)}
    _L0_gnn_all = _L0_gnn_setup()
    _L0_gnn_in = {k: v for k, v in _L0_gnn_all.items() if k in ('Wd', 'bd', 'Wu', 'bu', 'W1', 'b1', 'W2', 'b2')}
    del _L0_gnn_all

    def _L0_ffn_setup():
        import jax, jax.numpy as jnp
        import numpy as np
        B, S, D, F, E = (8, 256, 768, 384, 16)
        CAP = 64
        EPS = 1e-06

        def _switch_moe_block(x, ln_w, w_router, wi, wo):
            var = jnp.mean(jnp.square(x.astype(jnp.float32)), axis=-1, keepdims=True)
            normed = (x * jax.lax.rsqrt(var + EPS)).astype(x.dtype) * ln_w
            logits = jnp.einsum('bsd,de->bse', normed.astype(jnp.float32), w_router.astype(jnp.float32))
            probs = jax.nn.softmax(logits, axis=-1)
            expert_idx = jnp.argmax(probs, axis=-1)
            onehot = jax.nn.one_hot(expert_idx, E, dtype=jnp.float32)
            priority = jnp.cumsum(onehot, axis=1)
            keep = onehot * (priority <= CAP)
            pos = (priority - 1.0).astype(jnp.int32)
            dispatch = keep[..., None] * jax.nn.one_hot(pos, CAP, dtype=jnp.float32)
            expert_in = jnp.einsum('bsec,bsd->becd', dispatch, normed)
            h = jax.nn.relu(jnp.einsum('becd,edf->becf', expert_in, wi))
            expert_out = jnp.einsum('becf,efd->becd', h, wo)
            combined = jnp.einsum('bsec,becd->bsd', dispatch, expert_out)
            routed = jnp.sum(dispatch, axis=(2, 3)) > 0
            next_states = jnp.where(routed[..., None], combined.astype(x.dtype), normed)
            router_prob = jnp.max(probs, axis=-1, keepdims=True).astype(x.dtype)
            return x + router_prob * next_states
        key = jax.random.key(seed)
        k_x, k_r, k_wi, k_wo = jax.random.split(key, 4)
        x = jax.random.normal(k_x, (B, S, D), dtype=jnp.float32)
        ln_w = jnp.ones((D,), dtype=jnp.float32)
        w_router = jax.random.normal(k_r, (D, E), dtype=jnp.float32) * 0.02
        wi = jax.random.normal(k_wi, (E, D, F), dtype=jnp.float32) * D ** (-0.5)
        wo = jax.random.normal(k_wo, (E, F, D), dtype=jnp.float32) * F ** (-0.5)
        return {'x': x, 'ln_w': ln_w, 'w_router': w_router, 'wi': wi, 'wo': wo}
    _L0_ffn_all = _L0_ffn_setup()
    _L0_ffn_in = {k: v for k, v in _L0_ffn_all.items() if k in ('ln_w', 'w_router', 'wi', 'wo')}
    del _L0_ffn_all

    def _L1_gnn_setup():
        import jax, jax.numpy as jnp
        import numpy as np
        N = 2500
        E_RAND = 40000
        NEG_SLOPE = 0.2

        def gat_layer(x, W, a_src, a_dst, bias, src, dst, heads, out_c, concat):
            n = x.shape[0]
            h = (x @ W).reshape(n, heads, out_c)
            al_s = jnp.einsum('nhc,hc->nh', h, a_src)
            al_d = jnp.einsum('nhc,hc->nh', h, a_dst)
            e = jax.nn.leaky_relu(al_s[src] + al_d[dst], NEG_SLOPE)
            m = jax.ops.segment_max(e, dst, num_segments=n)
            ex = jnp.exp(e - m[dst])
            z = jax.ops.segment_sum(ex, dst, num_segments=n)
            alpha = ex / (z[dst] + 1e-16)
            msg = h[src] * alpha[:, :, None]
            out = jax.ops.segment_sum(msg, dst, num_segments=n)
            out = out.reshape(n, heads * out_c) if concat else out.mean(axis=1)
            return out + bias
        key = jax.random.key(seed)
        ks = jax.random.split(key, 10)
        x = jax.random.normal(ks[0], (N, 768), dtype=jnp.float32)
        src = jax.random.randint(ks[1], (E_RAND,), 0, N)
        dst = jax.random.randint(ks[2], (E_RAND,), 0, N)
        loop = jnp.arange(N)
        edge_index = jnp.stack([jnp.concatenate([src, loop]), jnp.concatenate([dst, loop])])
        s = 1.0 / np.sqrt(768.0)
        W1 = jax.random.normal(ks[3], (768, 768), dtype=jnp.float32) * s
        a_src1 = jax.random.normal(ks[4], (8, 96), dtype=jnp.float32) * 0.1
        a_dst1 = jax.random.normal(ks[5], (8, 96), dtype=jnp.float32) * 0.1
        b1 = jnp.zeros((768,), dtype=jnp.float32)
        W2 = jax.random.normal(ks[6], (768, 768), dtype=jnp.float32) * s
        a_src2 = jax.random.normal(ks[7], (1, 768), dtype=jnp.float32) * 0.1
        a_dst2 = jax.random.normal(ks[8], (1, 768), dtype=jnp.float32) * 0.1
        b2 = jnp.zeros((768,), dtype=jnp.float32)
        return {'x': x, 'edge_index': edge_index, 'W1': W1, 'a_src1': a_src1, 'a_dst1': a_dst1, 'b1': b1, 'W2': W2, 'a_src2': a_src2, 'a_dst2': a_dst2, 'b2': b2}
    _L1_gnn_all = _L1_gnn_setup()
    _L1_gnn_in = {k: v for k, v in _L1_gnn_all.items() if k in ('W1', 'a_src1', 'a_dst1', 'b1', 'W2', 'a_src2', 'a_dst2', 'b2')}
    del _L1_gnn_all

    def _L1_ffn_setup():
        import jax, jax.numpy as jnp
        import numpy as np
        import math
        B, T, C = (8, 256, 768)
        E = 3
        HD = C // E
        TOPK = 2
        NGLOB = 4

        def _masked_softmax(att, mask):
            att = jnp.where(mask, -jnp.inf, att)
            return jax.nn.softmax(att, axis=-1)
        key = jax.random.key(seed)
        ks = jax.random.split(key, 16)
        s = 0.02
        return {'x': jax.random.normal(ks[0], (B, T, C), jnp.float32), 'Wqk': jax.random.normal(ks[1], (C, 2 * C), jnp.float32) * s, 'bqk': jnp.zeros((2 * C,), jnp.float32), 'Wv': jax.random.normal(ks[2], (E, C, HD), jnp.float32) * s, 'bv': jnp.zeros((E, HD), jnp.float32), 'conv_w': jax.random.normal(ks[3], (HD, 1, 3), jnp.float32) * s, 'conv_b': jnp.zeros((HD,), jnp.float32), 'glob': jax.random.normal(ks[4], (NGLOB, HD), jnp.float32) * 0.02, 'pos_bias': jnp.zeros((64, 64), jnp.float32), 'Wg1': jax.random.normal(ks[5], (C, 32), jnp.float32) * s, 'bg1': jnp.zeros((32,), jnp.float32), 'Wg2': jax.random.normal(ks[6], (32, E), jnp.float32) * s, 'bg2': jnp.zeros((E,), jnp.float32), 'Wp': jax.random.normal(ks[7], (C, C), jnp.float32) * s, 'bp': jnp.zeros((C,), jnp.float32)}
    _L1_ffn_all = _L1_ffn_setup()
    _L1_ffn_in = {k: v for k, v in _L1_ffn_all.items() if k in ('Wqk', 'bqk', 'Wv', 'bv', 'conv_w', 'conv_b', 'glob', 'pos_bias', 'Wg1', 'bg1', 'Wg2', 'bg2', 'Wp', 'bp')}
    del _L1_ffn_all
    return {'x': x, 'src': src, 'dst': dst, 'edge_weight': edge_weight, 'L0_gnn_Wd': _L0_gnn_in['Wd'], 'L0_gnn_bd': _L0_gnn_in['bd'], 'L0_gnn_Wu': _L0_gnn_in['Wu'], 'L0_gnn_bu': _L0_gnn_in['bu'], 'L0_gnn_W1': _L0_gnn_in['W1'], 'L0_gnn_b1': _L0_gnn_in['b1'], 'L0_gnn_W2': _L0_gnn_in['W2'], 'L0_gnn_b2': _L0_gnn_in['b2'], 'L0_ffn_ln_w': _L0_ffn_in['ln_w'], 'L0_ffn_w_router': _L0_ffn_in['w_router'], 'L0_ffn_wi': _L0_ffn_in['wi'], 'L0_ffn_wo': _L0_ffn_in['wo'], 'L1_gnn_W1': _L1_gnn_in['W1'], 'L1_gnn_a_src1': _L1_gnn_in['a_src1'], 'L1_gnn_a_dst1': _L1_gnn_in['a_dst1'], 'L1_gnn_b1': _L1_gnn_in['b1'], 'L1_gnn_W2': _L1_gnn_in['W2'], 'L1_gnn_a_src2': _L1_gnn_in['a_src2'], 'L1_gnn_a_dst2': _L1_gnn_in['a_dst2'], 'L1_gnn_b2': _L1_gnn_in['b2'], 'L1_ffn_Wqk': _L1_ffn_in['Wqk'], 'L1_ffn_bqk': _L1_ffn_in['bqk'], 'L1_ffn_Wv': _L1_ffn_in['Wv'], 'L1_ffn_bv': _L1_ffn_in['bv'], 'L1_ffn_conv_w': _L1_ffn_in['conv_w'], 'L1_ffn_conv_b': _L1_ffn_in['conv_b'], 'L1_ffn_glob': _L1_ffn_in['glob'], 'L1_ffn_pos_bias': _L1_ffn_in['pos_bias'], 'L1_ffn_Wg1': _L1_ffn_in['Wg1'], 'L1_ffn_bg1': _L1_ffn_in['bg1'], 'L1_ffn_Wg2': _L1_ffn_in['Wg2'], 'L1_ffn_bg2': _L1_ffn_in['bg2'], 'L1_ffn_Wp': _L1_ffn_in['Wp'], 'L1_ffn_bp': _L1_ffn_in['bp']}

def reference(x, src, dst, edge_weight, L0_gnn_Wd, L0_gnn_bd, L0_gnn_Wu, L0_gnn_bu, L0_gnn_W1, L0_gnn_b1, L0_gnn_W2, L0_gnn_b2, L0_ffn_ln_w, L0_ffn_w_router, L0_ffn_wi, L0_ffn_wo, L1_gnn_W1, L1_gnn_a_src1, L1_gnn_a_dst1, L1_gnn_b1, L1_gnn_W2, L1_gnn_a_src2, L1_gnn_a_dst2, L1_gnn_b2, L1_ffn_Wqk, L1_ffn_bqk, L1_ffn_Wv, L1_ffn_bv, L1_ffn_conv_w, L1_ffn_conv_b, L1_ffn_glob, L1_ffn_pos_bias, L1_ffn_Wg1, L1_ffn_bg1, L1_ffn_Wg2, L1_ffn_bg2, L1_ffn_Wp, L1_ffn_bp):
    import jax
    import jax.numpy as jnp

    def _L0_gnn_ref(x, edge_index, edge_weight, Wd, bd, Wu, bu, W1, b1, W2, b2):
        import jax, jax.numpy as jnp
        import numpy as np
        N = 6250
        E = 62500
        D = 768
        H = 256
        R = 32

        def _gcn(x, W, b, row, col, ew):
            x = x @ W
            n = x.shape[0]
            deg = jax.ops.segment_sum(ew, col, num_segments=n) + 1.0
            dinv = jax.lax.rsqrt(deg)
            norm = dinv[row] * ew * dinv[col]
            agg = jax.ops.segment_sum(norm[:, None] * x[row], col, num_segments=n)
            return agg + (dinv * dinv)[:, None] * x + b
        h = jax.nn.relu(x @ Wd + bd) @ Wu + bu + x
        row, col = (edge_index[0], edge_index[1])
        h = jax.nn.relu(_gcn(h, W1, b1, row, col, edge_weight))
        h = _gcn(h, W2, b2, row, col, edge_weight)
        return h

    def _L0_ffn_ref(x, ln_w, w_router, wi, wo):
        import jax, jax.numpy as jnp
        import numpy as np
        B, S, D, F, E = (8, 256, 768, 384, 16)
        CAP = 64
        EPS = 1e-06

        def _switch_moe_block(x, ln_w, w_router, wi, wo):
            var = jnp.mean(jnp.square(x.astype(jnp.float32)), axis=-1, keepdims=True)
            normed = (x * jax.lax.rsqrt(var + EPS)).astype(x.dtype) * ln_w
            logits = jnp.einsum('bsd,de->bse', normed.astype(jnp.float32), w_router.astype(jnp.float32))
            probs = jax.nn.softmax(logits, axis=-1)
            expert_idx = jnp.argmax(probs, axis=-1)
            onehot = jax.nn.one_hot(expert_idx, E, dtype=jnp.float32)
            priority = jnp.cumsum(onehot, axis=1)
            keep = onehot * (priority <= CAP)
            pos = (priority - 1.0).astype(jnp.int32)
            dispatch = keep[..., None] * jax.nn.one_hot(pos, CAP, dtype=jnp.float32)
            expert_in = jnp.einsum('bsec,bsd->becd', dispatch, normed)
            h = jax.nn.relu(jnp.einsum('becd,edf->becf', expert_in, wi))
            expert_out = jnp.einsum('becf,efd->becd', h, wo)
            combined = jnp.einsum('bsec,becd->bsd', dispatch, expert_out)
            routed = jnp.sum(dispatch, axis=(2, 3)) > 0
            next_states = jnp.where(routed[..., None], combined.astype(x.dtype), normed)
            router_prob = jnp.max(probs, axis=-1, keepdims=True).astype(x.dtype)
            return x + router_prob * next_states
        return _switch_moe_block(x, ln_w, w_router, wi, wo)

    def _L1_gnn_ref(x, edge_index, W1, a_src1, a_dst1, b1, W2, a_src2, a_dst2, b2):
        import jax, jax.numpy as jnp
        import numpy as np
        N = 2500
        E_RAND = 40000
        NEG_SLOPE = 0.2

        def gat_layer(x, W, a_src, a_dst, bias, src, dst, heads, out_c, concat):
            n = x.shape[0]
            h = (x @ W).reshape(n, heads, out_c)
            al_s = jnp.einsum('nhc,hc->nh', h, a_src)
            al_d = jnp.einsum('nhc,hc->nh', h, a_dst)
            e = jax.nn.leaky_relu(al_s[src] + al_d[dst], NEG_SLOPE)
            m = jax.ops.segment_max(e, dst, num_segments=n)
            ex = jnp.exp(e - m[dst])
            z = jax.ops.segment_sum(ex, dst, num_segments=n)
            alpha = ex / (z[dst] + 1e-16)
            msg = h[src] * alpha[:, :, None]
            out = jax.ops.segment_sum(msg, dst, num_segments=n)
            out = out.reshape(n, heads * out_c) if concat else out.mean(axis=1)
            return out + bias
        src, dst = (edge_index[0], edge_index[1])
        h = gat_layer(x, W1, a_src1, a_dst1, b1, src, dst, heads=8, out_c=96, concat=True)
        h = jax.nn.elu(h)
        out = gat_layer(h, W2, a_src2, a_dst2, b2, src, dst, heads=1, out_c=768, concat=False)
        return out

    def _L1_ffn_ref(x, Wqk, bqk, Wv, bv, conv_w, conv_b, glob, pos_bias, Wg1, bg1, Wg2, bg2, Wp, bp):
        import jax, jax.numpy as jnp
        import numpy as np
        import math
        B, T, C = (8, 256, 768)
        E = 3
        HD = C // E
        TOPK = 2
        NGLOB = 4

        def _masked_softmax(att, mask):
            att = jnp.where(mask, -jnp.inf, att)
            return jax.nn.softmax(att, axis=-1)
        Bx, Tx, Cx = x.shape
        scale = 1.0 / math.sqrt(HD)
        gate = jax.nn.softmax(jax.nn.relu(x @ Wg1 + bg1) @ Wg2 + bg2, axis=-1)
        top_w, top_i = jax.lax.top_k(gate, TOPK)
        top_w = jax.nn.softmax(top_w, axis=-1)
        qk = x @ Wqk + bqk
        q, k = (qk[..., :Cx], qk[..., Cx:])
        q = q.reshape(Bx, Tx, E, HD)
        k = k.reshape(Bx, Tx, E, HD)
        rows = jnp.arange(Tx)[:, None]
        ys = []
        for e in range(E):
            qe = q[:, :, e]
            ke = k[:, :, e]
            ve = x @ Wv[e] + bv[e]
            if e == 0:
                qc = jnp.transpose(qe, (0, 2, 1))
                qc = jax.lax.conv_general_dilated(qc, conv_w, window_strides=(1,), padding=((1, 1),), feature_group_count=HD, dimension_numbers=('NCH', 'OIH', 'NCH'))
                qe = jnp.transpose(qc + conv_b[None, :, None], (0, 2, 1))
            elif e == 1:
                gb = jnp.broadcast_to(glob[None], (Bx, NGLOB, HD))
                ke = jnp.concatenate([ke, gb], axis=1)
                ve = jnp.concatenate([ve, gb], axis=1)
            att = jnp.einsum('btd,bsd->bts', qe, ke) * scale
            if e == 2 and Tx <= 64:
                att = att + pos_bias[:Tx, :Tx][None]
            S = att.shape[-1]
            mask = jnp.arange(S)[None, :] > rows
            att = _masked_softmax(att, mask[None])
            ys.append(jnp.einsum('bts,bsd->btd', att, ve))
        ys = jnp.stack(ys, axis=2)
        w_e = jnp.sum(jax.nn.one_hot(top_i, E, dtype=x.dtype) * top_w[..., None], axis=-2)
        combined = (ys * w_e[..., None]).reshape(Bx, Tx, Cx)
        return combined @ Wp + bp
    edge_index = jnp.stack([src, dst])
    x = x + _L0_gnn_ref(_layernorm(x, axis=-1), edge_index, edge_weight, L0_gnn_Wd, L0_gnn_bd, L0_gnn_Wu, L0_gnn_bu, L0_gnn_W1, L0_gnn_b1, L0_gnn_W2, L0_gnn_b2)
    x = x + _L0_ffn_ref(_layernorm(x, axis=-1)[None], L0_ffn_ln_w, L0_ffn_w_router, L0_ffn_wi, L0_ffn_wo)[0]
    x = x + _L1_gnn_ref(_layernorm(x, axis=-1), edge_index, L1_gnn_W1, L1_gnn_a_src1, L1_gnn_a_dst1, L1_gnn_b1, L1_gnn_W2, L1_gnn_a_src2, L1_gnn_a_dst2, L1_gnn_b2)
    x = x + _L1_ffn_ref(_layernorm(x, axis=-1)[None], L1_ffn_Wqk, L1_ffn_bqk, L1_ffn_Wv, L1_ffn_bv, L1_ffn_conv_w, L1_ffn_conv_b, L1_ffn_glob, L1_ffn_pos_bias, L1_ffn_Wg1, L1_ffn_bg1, L1_ffn_Wg2, L1_ffn_bg2, L1_ffn_Wp, L1_ffn_bp)[0]
    return x

_drawn_inputs = setup_inputs


def setup_inputs(seed=0):
    import zlib

    import numpy as np

    out = dict(_drawn_inputs(seed))
    spreads = {'L0_gnn_bd': (0.0, 0.735),
     'L0_gnn_bu': (0.0, 0.1),
     'L0_gnn_b1': (0.0, 0.1),
     'L0_gnn_b2': (0.0, 0.1),
     'L0_ffn_ln_w': (1.0, 0.2),
     'L1_gnn_b1': (0.0, 0.1),
     'L1_gnn_b2': (0.0, 0.1),
     'L1_ffn_bqk': (0.0, 0.8),
     'L1_ffn_bv': (0.0, 0.764),
     'L1_ffn_conv_b': (0.0, 0.8),
     'L1_ffn_pos_bias': (0.0, 0.1),
     'L1_ffn_bg1': (0.0, 0.8),
     'L1_ffn_bg2': (0.0, 0.541),
     'L1_ffn_bp': (0.0, 0.1)}
    factors = {'L0_gnn_Wd': 4.505,
     'L1_gnn_a_dst1': 8.0,
     'L1_gnn_a_src2': 6.29,
     'L1_gnn_a_dst2': 8.0,
     'L1_ffn_Wqk': 8.0,
     'L1_ffn_Wv': 4.157,
     'L1_ffn_conv_w': 8.0,
     'L1_ffn_Wg1': 7.794,
     'L1_ffn_Wg2': 8.0,
     'L1_ffn_Wp': 3.383}
    for name, (base, spread) in spreads.items():
        noise = np.random.default_rng([zlib.crc32(name.encode()), seed]).standard_normal(out[name].shape)
        drawn = base * np.exp(spread * noise) if base else spread * noise
        out[name] = jnp.asarray(drawn.astype(out[name].dtype))
    for name, factor in factors.items():
        out[name] = (out[name] * factor).astype(out[name].dtype)
    return out
```

```python
import math
from contextlib import ExitStack

import concourse.bass as bass
from concourse import mybir

F32 = mybir.dt.float32
BF16 = mybir.dt.bfloat16
I16 = mybir.dt.int16
I32 = mybir.dt.int32
ALU = mybir.AluOpType
ACT = mybir.ActivationFunctionType
AX = mybir.AxisListType

N, D = 1250, 768
NT, T = 125, 10
K = D // 128
EPC, NC_E, EROWS = 125, 330, 110
EG = NC_E // EROWS
WIN = 25
NWIN = N // WIN
BIG = 1e30
CHUNKS = [(0, 500), (500, 500), (1000, 250)]
BANKS = 8


def new_sem(nc, c, name):
    s = c.enter_context(nc.semaphore(name))
    c.callback(lambda: nc.sync.sem_clear(s))
    return s


def layernorm(nc, name, src, dst, stat, eps_col):
    with ExitStack() as c:
        stats_done = new_sem(nc, c, name + "_stats")
        std_done = new_sem(nc, c, name + "_std")
        rstd_done = new_sem(nc, c, name + "_rstd")
        bn = c.enter_context(nc.sbuf_tensor(name + "_bn", [NT, T, 2, 6], F32))
        block = c.enter_context(nc.Block(no_gpsimd_drain=True))
        half = D // 2

        @block.vector
        def _(dve):
            for t in range(T):
                for h in range(2):
                    nc.vector.bn_stats(bn[:, t, h, :], src[:, t, h * half:(h + 1) * half]).then_inc(stats_done, 1)
            for t in range(T):
                dve.wait_ge(stats_done, 2 * t + 2)
                nc.vector.bn_aggr(stat[:, t, 0:2], bn[:, t, :, :]).then_inc(stats_done, 1)
            dve.wait_ge(std_done, 1)
            nc.vector.reciprocal(stat[:, :, 2], stat[:, :, 2]).then_inc(rstd_done, 1)
            dve.wait_ge(rstd_done, 1)
            for t in range(T):
                nc.vector.tensor_scalar(dst[:, t, :], src[:, t, :], stat[:, t, 0:1], stat[:, t, 2:3],
                                        ALU.subtract, ALU.mult)

        @block.scalar
        def _(act):
            act.wait_ge(stats_done, 3 * T)
            nc.scalar.activation(stat[:, :, 2], stat[:, :, 1], ACT.Sqrt, bias=eps_col).then_inc(std_done, 1)


def transpose_nodes(nc, name, src, dst, ident, ps):
    with ExitStack() as c:
        turned = new_sem(nc, c, name + "_turned")
        by_act = new_sem(nc, c, name + "_by_act")
        by_dve = new_sem(nc, c, name + "_by_dve")
        block = c.enter_context(nc.Block(no_gpsimd_drain=True))
        groups = [(t, h) for t in range(T) for h in range(2)]

        @block.tensor
        def _(pe):
            for g, (t, h) in enumerate(groups):
                if g >= BANKS:
                    pe.wait_ge(by_dve if h else by_act, (g - BANKS) // 2 + 1)
                for j in range(3):
                    k = 3 * h + j
                    last = nc.tensor.transpose(ps[:, g % BANKS, j * NT:(j + 1) * NT],
                                               src[:, t, k * 128:(k + 1) * 128], ident[:NT, :NT])
                last.then_inc(turned, 1)

        def empty(g):
            t, h = groups[g]
            return (dst[:, 3 * h:3 * h + 3, t * NT:(t + 1) * NT],
                    ps[:, g % BANKS, 0:3 * NT].rearrange("p (j n) -> p j n", j=3))

        @block.scalar
        def _(act):
            for g in range(0, len(groups), 2):
                act.wait_ge(turned, g + 1)
                out, in_ = empty(g)
                nc.scalar.activation(out, in_, ACT.Copy).then_inc(by_act, 1)

        @block.vector
        def _(dve):
            for g in range(1, len(groups), 2):
                dve.wait_ge(turned, g + 1)
                out, in_ = empty(g)
                nc.vector.tensor_copy(out, in_).then_inc(by_dve, 1)


def dense_graph(nc, ins, cst, MT, CT, ps):
    GR = 4
    with ExitStack() as c:
        def sb(name, shape, dt=F32):
            return c.enter_context(nc.sbuf_tensor("g_" + name, shape, dt))

        def sem(name):
            return new_sem(nc, c, "g_" + name)

        ident = cst["ident"]
        raw = sb("raw", [EROWS, 2, EG, EPC], I32)
        row = sb("row", [EROWS, 3, EG, EPC])
        dstf = sb("dstf", [EROWS, EG, EPC])
        srcf = sb("srcf", [EROWS, EG, EPC])
        hi = sb("hi", [EROWS, 2, EG, EPC])
        edge = sb("edge", [EPC, NC_E + GR, 5])
        wrest = sb("wrest", [EPC, NC_E])
        mine = sb("mine", [EPC, GR, 5])
        key = sb("key", [EPC, GR])
        act_edges, pool_edges = sb("act_edges", [EPC, GR, 5]), sb("pool_edges", [EPC, GR, 5])
        wb = sb("wb", [EPC, NC_E], BF16)
        lo_iota = sb("lo_iota", [EPC, 128], I16)
        key_iota = sb("key_iota", [EPC, T, WIN], I16)
        win_start = sb("win_start", [EPC, NWIN])
        chunk_no = sb("chunk_no", [EROWS, EG])
        dlim = sb("dlim", [EROWS, 2, EG])
        meets = sb("meets", [EROWS, EG, NWIN])
        part = sb("part", [EROWS, EG, NWIN])
        marks = sb("marks", [EROWS, 2, EG, NWIN])
        mark = sb("mark", [EROWS, 2, NWIN])
        lim = sb("lim", [NWIN, 2])
        lim1 = sb("lim1", [1, 4, NWIN])
        lim_i = sb("lim_i", [1, 2, NWIN], I32)
        zero_b = sb("zero_b", [EPC, 512], BF16)
        A = sb("A", [EPC, GR, 4, 128], BF16)
        G = sb("G", [EPC, GR, T * WIN], BF16)

        loaded, iotas, v, lims = sem("loaded"), sem("iotas"), sem("v"), sem("lims")
        rows_ready, marks_ready = sem("rows_ready"), sem("marks_ready")
        cols_ready, lim_T, lim_T2, lim_sb = sem("cols_ready"), sem("lim_T"), sem("lim_T2"), sem("lim_sb")
        hot_one, hot_dve, hot_act, hot_pool, used, win_done, win_out = (
            sem("hot_one"), sem("hot_dve"), sem("hot_act"), sem("hot_pool"), sem("used"), sem("win_done"), sem("win_out"))
        copied, copied_act, copied_pool = sem("copied"), sem("copied_act"), sem("copied_pool")
        block = c.enter_context(nc.Block(no_gpsimd_drain=True))

        def limits(eng, w):
            first = eng.value_load(lim_i[0:1, 0, bass.ds(w, 1)], min_val=0, max_val=NC_E - 1)
            return first, eng.value_load(lim_i[0:1, 1, bass.ds(w, 1)], min_val=1, max_val=NC_E)

        def counter(eng, name):
            r = eng.alloc_register(name)
            eng.reg_mov(r, 0)
            return r

        def count(eng, r):
            return eng.snap(r, min_val=0, max_val=NWIN * (NC_E + GR))

        @block.sync
        def _(sp):
            for i, n in enumerate(("src", "dst")):
                sp.dma_start(raw[:, i, :, :], ins[n].rearrange("(j p e) -> p j e", p=EROWS, e=EPC)).then_inc(loaded, 16)
            sp.dma_start(row[:, 2, :, :], ins["edge_weight"].rearrange("(j p e) -> p j e", p=EROWS, e=EPC)).then_inc(loaded, 16)

        @block.gpsimd
        def _(pool):
            nc.gpsimd.memset(cst["ones"][:], 1.0).then_inc(iotas, 1)
            nc.gpsimd.iota(lo_iota[:], [[1, 128]], base=0, channel_multiplier=0).then_inc(iotas, 1)
            nc.gpsimd.iota(key_iota[:], [[N, T], [1, WIN]], base=0, channel_multiplier=0).then_inc(iotas, 1)
            nc.gpsimd.iota(win_start[:], [[WIN, NWIN]], base=0, channel_multiplier=0,
                           allow_small_or_imprecise_dtypes=True).then_inc(iotas, 1)
            nc.gpsimd.iota(chunk_no[:], [[EROWS, EG]], base=0, channel_multiplier=1,
                           allow_small_or_imprecise_dtypes=True).then_inc(iotas, 1)
            nc.gpsimd.memset(zero_b[:], 0.0).then_inc(iotas, 1)
            pool.wait_ge(iotas, 6)
            pool.wait_ge(lims, 1)
            begun = counter(pool, "begun_pool")
            with pool.Fori(0, NWIN) as w:
                first, end = limits(pool, w)
                with pool.Fori(first, end, GR) as ch:
                    at = count(pool, begun)
                    pool.wait_ge(hot_pool, at)
                    nc.gpsimd.tensor_copy(pool_edges[:], edge[:, bass.ds(ch, GR), :]).then_inc(copied_pool, GR)
                    pool.wait_ge(copied_pool, at + GR)
                    for g in range(0, GR, 2):
                        pool.wait_ge(used, at + (g + 1))
                        nc.gpsimd.tensor_scalar(A[:, g, 2, :], lo_iota[:], pool_edges[:, g, 0:1], pool_edges[:, g, 4:5],
                                                ALU.is_equal, ALU.mult).then_inc(hot_pool, 2)
                    pool.reg_add(begun, begun, GR)

        @block.vector
        def _(dve):
            n = [0]

            def link(ins_):
                n[0] += 1
                ins_.then_inc(v, 1)
                dve.wait_ge(v, n[0])

            dve.wait_ge(loaded, 48)
            dve.wait_ge(iotas, 6)
            nc.vector.tensor_copy(srcf[:], raw[:, 0])
            link(nc.vector.tensor_copy(dstf[:], raw[:, 1]))
            link(nc.vector.tensor_scalar(hi[:, 0], srcf[:], float(NT), None, ALU.is_ge))
            for t in range(2, T):
                link(nc.vector.scalar_tensor_tensor(hi[:, (t + 1) % 2], srcf[:], float(NT * t), hi[:, t % 2],
                                                    ALU.is_ge, ALU.add))
            tile = hi[:, 0]
            nc.vector.scalar_tensor_tensor(row[:, 0], tile, -float(NT), srcf[:], ALU.mult, ALU.add)
            nc.vector.tensor_reduce(dlim[:, 0], dstf[:], AX.X, ALU.min)
            nc.vector.tensor_reduce(dlim[:, 1], dstf[:], AX.X, ALU.max)
            nc.vector.scalar_tensor_tensor(row[:, 1], tile, float(N), dstf[:], ALU.mult, ALU.add).then_inc(rows_ready, 1)
            dve.wait_ge(rows_ready, 1)
            for j in range(EG):
                nc.vector.tensor_scalar(part[:, j], win_start[:EROWS], float(WIN - 1), dlim[:, 0, j:j + 1],
                                        ALU.add, ALU.is_ge)
            for j in range(EG):
                link(nc.vector.tensor_scalar(meets[:, j], win_start[:EROWS], dlim[:, 1, j:j + 1], None, ALU.is_le))
            link(nc.vector.tensor_tensor(meets[:], meets[:], part[:], ALU.mult))
            for j in range(EG):
                link(nc.vector.tensor_scalar(marks[:, 1, j], meets[:, j], chunk_no[:, j:j + 1], None, ALU.mult))
            link(nc.vector.scalar_tensor_tensor(marks[:, 0], meets[:], float(NC_E), marks[:, 1], ALU.mult, ALU.subtract))
            link(nc.vector.tensor_tensor(marks[:, 1], marks[:, 1], meets[:], ALU.add))
            link(nc.vector.tensor_tensor(mark[:], marks[:, :, 0], marks[:, :, 1], ALU.max))
            nc.vector.tensor_tensor(mark[:], mark[:], marks[:, :, 2], ALU.max).then_inc(marks_ready, 1)
            dve.wait_ge(cols_ready, 1)
            nc.vector.memset(edge[:, NC_E:, :], -1.0)
            for i in range(2):
                nc.vector.tensor_copy(edge[:, 0:NC_E, i], ps[:EPC, i, 0:NC_E])
            link(nc.vector.tensor_copy(wrest[:], ps[:EPC, 2, 0:NC_E]))
            link(nc.vector.tensor_copy(wb[:], wrest[:]))
            link(nc.vector.tensor_copy(edge[:, 0:NC_E, 2], wb[:]))
            link(nc.vector.tensor_tensor(wrest[:], wrest[:], edge[:, 0:NC_E, 2], ALU.subtract))
            link(nc.vector.tensor_copy(wb[:], wrest[:]))
            link(nc.vector.tensor_copy(edge[:, 0:NC_E, 3], wb[:]))
            link(nc.vector.tensor_tensor(edge[:, 0:NC_E, 4], wrest[:], edge[:, 0:NC_E, 3], ALU.subtract))
            dve.wait_ge(lim_T, 1)
            for i in range(2):
                nc.vector.tensor_reduce(lim[:, i:i + 1], ps[:NWIN, 3, i * 128:i * 128 + EROWS], AX.X, ALU.max).then_inc(lim_sb, 1)
            dve.wait_ge(lim_T2, 1)
            link(nc.vector.tensor_copy(lim1[:, 2:4].rearrange("p a w -> p (a w)"),
                                       ps[0:1, 4, 0:2 * NWIN]))
            link(nc.vector.tensor_scalar(lim1[:, 0], lim1[:, 2], -1.0, float(NC_E), ALU.mult, ALU.add))
            link(nc.vector.tensor_scalar(lim1[:, 0], lim1[:, 0], float(NC_E - 1), None, ALU.min))
            link(nc.vector.scalar_tensor_tensor(lim1[:, 1], lim1[:, 0], 1.0, lim1[:, 3], ALU.add, ALU.max))
            nc.vector.tensor_copy(lim_i[:], lim1[:, 0:2]).then_inc(lims, 1)
            dve.wait_ge(lims, 1)
            begun = counter(dve, "begun_dve")
            with dve.Fori(0, NWIN) as w:
                first, end = limits(dve, w)
                with dve.Fori(first, end, GR) as ch:
                    at = count(dve, begun)
                    dve.wait_ge(hot_dve, at)
                    nc.vector.tensor_copy(mine[:], edge[:, bass.ds(ch, GR), :])
                    nc.vector.tensor_scalar(key[:], edge[:, bass.ds(ch, GR), 1], win_start[:, bass.ds(w, 1)], None,
                                            ALU.subtract).then_inc(copied, GR)
                    dve.wait_ge(copied, at + GR)
                    for g in range(GR):
                        dve.wait_ge(used, at + (g + 1))
                        nc.vector.tensor_scalar(A[:, g, 3, :], lo_iota[:], mine[:, g, 0:1], None,
                                                ALU.is_equal).then_inc(hot_one, 1)
                        nc.vector.tensor_scalar(G[:, g, :], key_iota[:].rearrange("p a w -> p (a w)"), key[:, g:g + 1],
                                                None, ALU.is_equal)
                        nc.vector.tensor_scalar(A[:, g, 0, :], lo_iota[:], mine[:, g, 0:1], mine[:, g, 2:3],
                                                ALU.is_equal, ALU.mult).then_inc(hot_dve, 1)
                    dve.reg_add(begun, begun, GR)

        @block.tensor
        def _(pe):
            pe.wait_ge(rows_ready, 1)
            pe.wait_ge(loaded, 48)
            for i in range(3):
                for j in range(EG):
                    last = nc.tensor.transpose(ps[:EPC, i, j * EROWS:(j + 1) * EROWS], row[:, i, j, :], ident[:EROWS, :EROWS])
            last.then_inc(cols_ready, 1)
            pe.wait_ge(marks_ready, 1)
            for i in range(2):
                last = nc.tensor.transpose(ps[:NWIN, 3, i * 128:i * 128 + EROWS], mark[:, i], ident[:EROWS, :EROWS])
            last.then_inc(lim_T, 1)
            pe.wait_ge(lim_sb, 2)
            for i in range(2):
                last = nc.tensor.transpose(ps[0:1, 4, i * NWIN:(i + 1) * NWIN], lim[:, i:i + 1], ident[:NWIN, :NWIN])
            last.then_inc(lim_T2, 1)
            pe.wait_ge(lims, 1)
            pe.wait_ge(iotas, 6)
            pe.sem_inc(used, GR)
            begun = counter(pe, "begun_pe")
            with pe.Fori(0, NWIN // 2) as w2:
                for half in range(2):
                    w = w2 * 2 + half
                    sums = ps[:, 5 + half, :]
                    first, end = limits(pe, w)
                    pe.wait_ge(win_out, w + 1)
                    nc.tensor.matmul(sums, zero_b[:, 0:128], zero_b[:], start=True, stop=False)
                    with pe.Fori(first, end, GR):
                        at = count(pe, begun)
                        for g in range(GR):
                            pe.wait_ge(hot_dve, at + (g + 1))
                            pe.wait_ge(hot_act, at + (g + 1))
                            if g % 2 == 0:
                                pe.wait_ge(hot_pool, at + (g + 2))
                            for i in range(4):
                                off = 256 * (i == 3)
                                last = nc.tensor.matmul(sums[:, off:off + T * WIN], A[:, g, i, :], G[:, g, :],
                                                        start=False, stop=False, skip_group_check=True)
                            last.then_inc(used, 1)
                        pe.reg_add(begun, begun, GR)
                    nc.tensor.matmul(sums, zero_b[:, 0:128], zero_b[:], start=False, stop=True).then_inc(win_done, 1)

        @block.scalar
        def _(act):
            act.sem_inc(win_out, 2)
            act.wait_ge(lims, 1)
            begun = counter(act, "begun_act")

            def second_parts(w):
                first, end = limits(act, w)
                with act.Fori(first, end, GR) as ch:
                    at = count(act, begun)
                    act.wait_ge(hot_act, at)
                    nc.scalar.activation(act_edges[:, :, 3:5], edge[:, bass.ds(ch, GR), 3:5], ACT.Copy).then_inc(copied_act, GR)
                    act.wait_ge(copied_act, at + GR)
                    for g in range(GR):
                        act.wait_ge(hot_one, at + (g + 1))
                        for part in (1, 2)[:1 + g % 2]:
                            last = nc.scalar.activation(A[:, g, part, :], A[:, g, 3, :], ACT.Copy,
                                                        scale=act_edges[:, g, part + 2:part + 3])
                        last.then_inc(hot_act, 1)
                    act.reg_add(begun, begun, GR)

            def copy_out(w, bank):
                act.wait_ge(win_done, w + 1)
                for i, dense in enumerate((MT, CT)):
                    last = nc.scalar.activation(dense[:, :, bass.ds(w * WIN, WIN)],
                                                ps[:NT, bank, 256 * i:256 * i + T * WIN].rearrange("p (a w) -> p a w", a=T), ACT.Copy)
                last.then_inc(win_out, 1)

            second_parts(0)
            with act.Fori(0, NWIN // 2 - 1) as w2:
                for half in range(2):
                    second_parts(w2 * 2 + half + 1)
                    copy_out(w2 * 2 + half, 5 + half)
            second_parts(NWIN - 1)
            copy_out(NWIN - 2, 5)
            copy_out(NWIN - 1, 6)


def low_rank_and_gcn(nc, ins, XT, MT, X, W, stat, ones, ps):
    H, R = 256, 24
    with ExitStack() as c:
        def sb(name, shape, dt=F32):
            return c.enter_context(nc.sbuf_tensor("c_" + name, shape, dt))

        def sem(name):
            return new_sem(nc, c, "c_" + name)

        ident = W["ident"]
        wd, wu, bd, bu = sb("wd", [128, K, R]), sb("wu", [R, D]), sb("bd", [R, 1]), sb("bu", [128, K])
        w1, w2 = sb("w1", [128, K, H]), sb("w2", [128, 2, D])
        b1, b2 = sb("b1", [NT, H]), sb("b2", [NT, D])
        RT = sb("RT", [R, N])
        hw = sb("hw", [NT, T, H])
        aggT = sb("aggT", [128, 2, N])
        tmp = sb("tmp", [NT, 2, H])
        dinv = stat[:, :, 3]
        hw2 = XT[:NT, :, :].rearrange("p k n -> p (k n)")[:, 0:T * H].rearrange("p (t h) -> p t h", t=T)
        loaded, self_loop, deg_done, std_done, dinv_done = (
            sem("loaded"), sem("self_loop"), sem("deg_done"), sem("std_done"), sem("dinv_done"))
        low_done, low_out, up_done, up_out = sem("low_done"), sem("low_out"), sem("up_done"), sem("up_out")
        hw_done, hw_out, agg_done, agg_out, tmp_done = (
            sem("hw_done"), sem("hw_out"), sem("agg_done"), sem("agg_out"), sem("tmp_done"))
        aggT_done, aggT_out, y_done, y_out, bias_done = (
            sem("aggT_done"), sem("aggT_out"), sem("y_done"), sem("y_out"), sem("bias_done"))
        block = c.enter_context(nc.Block(no_gpsimd_drain=True))

        @block.sync
        def _(sp):
            def load(dst, src, small=False):
                sp.dma_start(dst, src, allow_slow_non_contiguous=small).then_inc(loaded, 16)
            load(wd[:], ins["L0_gnn_Wd"].rearrange("(k p) r -> p k r", p=128))
            load(wu[:], ins["L0_gnn_Wu"])
            load(bd[:], ins["L0_gnn_bd"].rearrange("(r a) -> r a", a=1), True)
            load(bu[:], ins["L0_gnn_bu"].rearrange("(k p) -> p k", p=128), True)
            load(w1[:], ins["L0_gnn_W1"].rearrange("(k p) h -> p k h", p=128))
            load(w2[:], ins["L0_gnn_W2"].rearrange("(k p) d -> p k d", p=128))
            load(b1[:], ins["L0_gnn_b1"].partition_broadcast(NT))
            load(b2[:], ins["L0_gnn_b2"].partition_broadcast(NT))

        @block.gpsimd
        def _(pool):
            pool.wait_ge(loaded, 128)
            for t in range(T):
                nc.gpsimd.tensor_tensor(X[:, t, :], X[:, t, :], b2[:], ALU.add).then_inc(bias_done, 1)
            pool.wait_ge(bias_done, T)

        @block.tensor
        def _(pe):
            pe.wait_ge(self_loop, 1)
            for t in range(T):
                for s in range(T):
                    last = nc.tensor.matmul(ps[:NT, 7, t:t + 1], MT[:, s, t * NT:(t + 1) * NT], ones[:NT, 0:1],
                                            start=(s == 0), stop=(s == T - 1))
            last.then_inc(deg_done, 1)
            pe.wait_ge(loaded, 128)
            for g, (n0, nn) in enumerate(CHUNKS):
                for k in range(K):
                    last = nc.tensor.matmul(ps[:R, g, 0:nn], wd[:, k, :], XT[:, k, n0:n0 + nn],
                                            start=(k == 0), stop=(k == K - 1))
                last.then_inc(low_done, 1)
            for g, (n0, nn) in enumerate(CHUNKS):
                pe.wait_ge(low_out, g + 1)
                for m in range(K):
                    i = g * K + m
                    if i >= 4:
                        pe.wait_ge(up_out, i - 3)
                    nc.tensor.matmul(ps[:, 3 + i % 4, 0:nn], wu[:, m * 128:(m + 1) * 128], RT[:, n0:n0 + nn],
                                     start=True, stop=True).then_inc(up_done, 1)
            pe.wait_ge(up_out, 3 * K)
            for t in range(T):
                if t >= 4:
                    pe.wait_ge(hw_out, t - 3)
                for k in range(K):
                    last = nc.tensor.matmul(ps[:NT, t % 4, 0:H], XT[:, k, t * NT:(t + 1) * NT], w1[:, k, :],
                                            start=(k == 0), stop=(k == K - 1))
                last.then_inc(hw_done, 1)
            pe.wait_ge(hw_out, T)
            for t in range(T):
                if t >= 4:
                    pe.wait_ge(tmp_done, t - 3)
                for s in range(T):
                    last = nc.tensor.matmul(ps[:NT, 4 + t % 4, 0:H], MT[:, s, t * NT:(t + 1) * NT], hw[:, s, :],
                                            start=(s == 0), stop=(s == T - 1))
                last.then_inc(agg_done, 1)
            pe.wait_ge(agg_out, T)
            for m in range(2):
                for g, (n0, nn) in enumerate(CHUNKS):
                    i = m * 3 + g
                    if i >= 4:
                        pe.wait_ge(aggT_out, i - 3)
                    for s in range(T):
                        last = nc.tensor.matmul(ps[:, i % 4, 0:nn], hw2[:, s, m * 128:(m + 1) * 128],
                                                MT[:, s, n0:n0 + nn], start=(s == 0), stop=(s == T - 1))
                    last.then_inc(aggT_done, 1)
            pe.wait_ge(aggT_out, 6)
            for t in range(T):
                for h in range(2):
                    i = 2 * t + h
                    if i >= 4:
                        pe.wait_ge(y_out, i - 3)
                    for k in range(2):
                        last = nc.tensor.matmul(ps[:NT, 4 + i % 4, 0:384], aggT[:, k, t * NT:(t + 1) * NT],
                                                w2[:, k, h * 384:(h + 1) * 384], start=(k == 0), stop=(k == 1))
                    last.then_inc(y_done, 1)

        @block.scalar
        def _(act):
            act.wait_ge(deg_done, 1)
            nc.scalar.activation(dinv, ps[:NT, 7, 0:T], ACT.Sqrt).then_inc(std_done, 1)
            act.wait_ge(loaded, 128)
            for g, (n0, nn) in enumerate(CHUNKS):
                act.wait_ge(low_done, g + 1)
                nc.scalar.activation(RT[:, n0:n0 + nn], ps[:R, g, 0:nn], ACT.Relu, bias=bd[:, 0:1]).then_inc(low_out, 1)
            act.wait_ge(dinv_done, 1)
            for t in range(T):
                act.wait_ge(hw_done, t + 1)
                nc.scalar.activation(hw[:, t, :], ps[:NT, t % 4, 0:H], ACT.Copy, scale=dinv[:, t:t + 1]).then_inc(hw_out, 1)
            for m in range(2):
                for g, (n0, nn) in enumerate(CHUNKS):
                    act.wait_ge(aggT_done, m * 3 + g + 1)
                    nc.scalar.activation(aggT[:, m, n0:n0 + nn], ps[:, (m * 3 + g) % 4, 0:nn], ACT.Copy).then_inc(aggT_out, 1)

        @block.vector
        def _(dve):
            for t in range(T):
                last = nc.vector.tensor_tensor(MT[:, t, t * NT:(t + 1) * NT], MT[:, t, t * NT:(t + 1) * NT],
                                               ident[:NT, :NT], ALU.add)
            last.then_inc(self_loop, 1)
            dve.wait_ge(std_done, 1)
            nc.vector.reciprocal(dinv, dinv).then_inc(dinv_done, 1)
            for g, (n0, nn) in enumerate(CHUNKS):
                for m in range(K):
                    i = g * K + m
                    dve.wait_ge(up_done, i + 1)
                    nc.vector.scalar_tensor_tensor(XT[:, m, n0:n0 + nn], ps[:, 3 + i % 4, 0:nn], bu[:, m:m + 1],
                                                   XT[:, m, n0:n0 + nn], ALU.add, ALU.add).then_inc(up_out, 1)
            dve.wait_ge(dinv_done, 1)
            dve.wait_ge(hw_done, T)
            for t in range(T):
                dve.wait_ge(agg_done, t + 1)
                nc.vector.scalar_tensor_tensor(tmp[:, t % 2, :], ps[:NT, 4 + t % 4, 0:H], dinv[:, t:t + 1], b1[:],
                                               ALU.mult, ALU.add).then_inc(tmp_done, 1)
                dve.wait_ge(tmp_done, t + 1)
                nc.vector.tensor_scalar(hw2[:, t, :], tmp[:, t % 2, :], 0.0, dinv[:, t:t + 1],
                                        ALU.max, ALU.mult).then_inc(agg_out, 1)
            dve.wait_ge(bias_done, T)
            for t in range(T):
                for h in range(2):
                    i = 2 * t + h
                    dve.wait_ge(y_done, i + 1)
                    nc.vector.scalar_tensor_tensor(X[:, t, h * 384:(h + 1) * 384], ps[:NT, 4 + i % 4, 0:384],
                                                   dinv[:, t:t + 1], X[:, t, h * 384:(h + 1) * 384],
                                                   ALU.mult, ALU.add).then_inc(y_out, 1)


E_MOE, CAP, FF = 16, 64, 384


def route(nc, ins, W, X, XN, XT, stat, eps6, moe, ps, normd):
    with ExitStack() as c:
        def sb(name, shape, dt=F32):
            return c.enter_context(nc.sbuf_tensor("r_" + name, shape, dt))

        def sem(name):
            return new_sem(nc, c, "r_" + name)

        ident, ones = W["ident"], W["ones"]
        lnw = sb("lnw", [NT, D])
        wr = sb("wr", [128, K, E_MOE])
        sq = sb("sq", [NT, D])
        ms = sb("ms", [NT, T])
        lg, oh, tmp, base = (sb(x, [NT, T, E_MOE]) for x in ("lg", "oh", "tmp", "base"))
        mx, p1, keep, sc = (sb(x, [NT, T]) for x in ("mx", "p1", "keep", "sc"))
        down = sb("down", [NT, E_MOE])
        slot0 = sb("slot0", [NT, E_MOE])
        rank = sb("rank", [NT, CAP])
        node = sb("node", [NT, T])
        tri = sb("tri", [NT, NT])
        at_rank = sb("at_rank", [NT, T, 2, CAP])
        tok = sb("tok", [128, E_MOE])
        loaded, made, sq_done, v, norm_done, added, stored = (
            sem("loaded"), sem("made"), sem("sq_done"), sem("v"), sem("norm_done"), sem("added"), sem("stored"))
        normed, t_done, t_act, t_dve, lg_done, exp_in, exp_out, oh_done, cum_done, inv_in, inv_done = (
            sem("normed"), sem("t_done"), sem("t_act"), sem("t_dve"), sem("lg_done"), sem("exp_in"),
            sem("exp_out"), sem("oh_done"), sem("cum_done"), sem("inv_in"), sem("inv_done"))
        rms_in, rms_out = sem("rms_in"), sem("rms_out")
        block = c.enter_context(nc.Block(no_gpsimd_drain=True))
        rp, slot_i, tok_i, ka, kb = moe["rp"], moe["slot"], moe["tok"], moe["ka"], moe["kb"]

        @block.sync
        def _(sp):
            sp.dma_start(lnw[:], ins["L0_ffn_ln_w"].partition_broadcast(NT)).then_inc(loaded, 16)
            sp.dma_start(wr[:], ins["L0_ffn_w_router"].rearrange("(k p) e -> p k e", p=128)).then_inc(loaded, 16)
            sp.wait_ge(norm_done, T)
            sp.dma_start(normd.rearrange("(t p) d -> p t d", p=NT), XN[:]).then_inc(stored, 16)
            sp.wait_ge(stored, 16)

        @block.gpsimd
        def _(pool):
            nc.gpsimd.iota(down[:], [[-1, E_MOE]], base=E_MOE, channel_multiplier=0, allow_small_or_imprecise_dtypes=True)
            nc.gpsimd.iota(slot0[:], [[CAP, E_MOE]], base=-1, channel_multiplier=0, allow_small_or_imprecise_dtypes=True)
            nc.gpsimd.iota(rank[:], [[1, CAP]], base=1, channel_multiplier=0, allow_small_or_imprecise_dtypes=True)
            nc.gpsimd.iota(node[:], [[NT, T]], base=0, channel_multiplier=1, allow_small_or_imprecise_dtypes=True)
            nc.gpsimd.memset(tri[:], 1.0).then_inc(made, 1)
            pool.wait_ge(made, 1)
            nc.gpsimd.affine_select(out=tri[:], in_=tri[:], compare_op=ALU.is_ge, fill=0.0, base=0,
                                    pattern=[[1, NT]], channel_multiplier=-1).then_inc(made, 1)
            for t in range(T):
                nc.gpsimd.tensor_tensor(X[:, t, :], X[:, t, :], XN[:, t, :], ALU.add).then_inc(added, 1)
            pool.wait_ge(added, T)

        @block.scalar
        def _(act):
            for t in range(T):
                nc.scalar.activation(sq[:], XN[:, t, :], ACT.Square, accum_out=ms[:, t:t + 1]).then_inc(sq_done, 1)
                act.wait_ge(sq_done, t + 1)
            nc.scalar.activation(mx[:], ms[:], ACT.Sqrt, scale=1.0 / D, bias=eps6).then_inc(rms_in, 1)
            for g in range(0, 2 * T, 2):
                act.wait_ge(t_done, g + 1)
                nc.scalar.activation(XT[:, 0:3, (g // 2) * NT:(g // 2 + 1) * NT],
                                     ps[:, g % 6, 0:3 * NT].rearrange("p (j n) -> p j n", j=3), ACT.Copy).then_inc(t_act, 1)
            act.wait_ge(exp_in, 1)
            nc.scalar.activation(tmp[:], lg[:], ACT.Exp).then_inc(exp_out, 1)

        @block.tensor
        def _(pe):
            for t in range(T):
                pe.wait_ge(norm_done, t + 1)
                for h in range(2):
                    g = 2 * t + h
                    if g >= 6:
                        pe.wait_ge(t_dve if h else t_act, (g - 6) // 2 + 1)
                    for j in range(3):
                        k = 3 * h + j
                        last = nc.tensor.transpose(ps[:, g % 6, j * NT:(j + 1) * NT],
                                                   XN[:, t, k * 128:(k + 1) * 128], ident[:NT, :NT])
                    last.then_inc(t_done, 1)
            pe.wait_ge(loaded, 32)
            for t in range(T):
                pe.wait_ge(t_act, t + 1)
                pe.wait_ge(t_dve, t + 1)
                for k in range(K):
                    last = nc.tensor.matmul(ps[:NT, 6, t * E_MOE:(t + 1) * E_MOE], XT[:, k, t * NT:(t + 1) * NT],
                                            wr[:, k, :], start=(k == 0), stop=(k == K - 1))
            last.then_inc(lg_done, 1)
            pe.wait_ge(made, 2)
            pe.wait_ge(oh_done, 1)
            flat = oh[:].rearrange("p t e -> p (t e)")
            nc.tensor.matmul(ps[:NT, 7, 0:T * E_MOE], tri[:], flat, start=True, stop=True)
            nc.tensor.matmul(ps[:NT, 0, 0:T * E_MOE], ones[:NT, :NT], flat, start=True, stop=True).then_inc(cum_done, 1)
            pe.wait_ge(inv_in, 1)
            for t in range(T):
                last = nc.tensor.matmul(ps[:, 1, 0:E_MOE], at_rank[:, t, :, :].rearrange("p a c -> p (a c)"), oh[:, t, :],
                                        start=(t == 0), stop=(t == T - 1))
            last.then_inc(inv_done, 1)

        @block.vector
        def _(dve):
            n = [0]

            def link(ins_):
                n[0] += 1
                ins_.then_inc(v, 1)
                dve.wait_ge(v, n[0])

            def wide(a, m=E_MOE):
                return a.unsqueeze(2).broadcast_to([NT, T, m])

            def each(a):
                return a.unsqueeze(1).broadcast_to([NT, T, E_MOE])

            dve.wait_ge(rms_in, 1)
            dve.wait_ge(loaded, 32)
            link(nc.vector.reciprocal(ms[:], mx[:]))
            for t in range(T):
                dve.wait_ge(added, t + 1)
                nc.vector.scalar_tensor_tensor(XN[:, t, :], XN[:, t, :], ms[:, t:t + 1], lnw[:], ALU.mult,
                                               ALU.mult).then_inc(norm_done, 1)
            for g in range(1, 2 * T, 2):
                dve.wait_ge(t_done, g + 1)
                nc.vector.tensor_copy(XT[:, 3:6, (g // 2) * NT:(g // 2 + 1) * NT],
                                      ps[:, g % 6, 0:3 * NT].rearrange("p (j n) -> p j n", j=3)).then_inc(t_dve, 1)
            dve.wait_ge(lg_done, 1)
            link(nc.vector.tensor_copy(lg[:], ps[:NT, 6, 0:T * E_MOE].rearrange("p (t e) -> p t e", t=T)))
            link(nc.vector.tensor_reduce(mx[:], lg[:], AX.X, ALU.max))
            link(nc.vector.tensor_tensor(oh[:], lg[:], wide(mx[:]), ALU.is_ge))
            nc.vector.tensor_tensor(lg[:], lg[:], wide(mx[:]), ALU.subtract).then_inc(exp_in, 1)
            dve.wait_ge(made, 2)
            link(nc.vector.tensor_tensor(oh[:], oh[:], each(down[:]), ALU.mult))
            link(nc.vector.tensor_reduce(sc[:], oh[:], AX.X, ALU.max))
            nc.vector.tensor_tensor(oh[:], each(down[:]), wide(sc[:]), ALU.is_equal).then_inc(oh_done, 1)
            dve.wait_ge(exp_out, 1)
            link(nc.vector.tensor_reduce(rp[:], tmp[:], AX.X, ALU.add))
            link(nc.vector.reciprocal(rp[:], rp[:]))
            dve.wait_ge(cum_done, 1)
            link(nc.vector.memset(base[:, 0, :], 0.0))
            for t in range(1, T):
                link(nc.vector.tensor_tensor(base[:, t, :], base[:, t - 1, :],
                                             ps[:NT, 0, (t - 1) * E_MOE:t * E_MOE], ALU.add))
            link(nc.vector.tensor_tensor(base[:], base[:],
                                         ps[:NT, 7, 0:T * E_MOE].rearrange("p (t e) -> p t e", t=T), ALU.add))
            link(nc.vector.tensor_tensor(base[:], base[:], oh[:], ALU.mult))
            link(nc.vector.tensor_reduce(p1[:], base[:], AX.X, ALU.add))
            link(nc.vector.tensor_scalar(keep[:], p1[:], float(CAP), None, ALU.is_le))
            link(nc.vector.tensor_tensor(tmp[:], oh[:], each(slot0[:]), ALU.mult))
            link(nc.vector.tensor_reduce(sc[:], tmp[:], AX.X, ALU.add))
            link(nc.vector.tensor_tensor(sc[:], sc[:], p1[:], ALU.add))
            link(nc.vector.tensor_tensor(sc[:], sc[:], keep[:], ALU.mult))
            nc.vector.tensor_copy(slot_i[:], sc[:])
            link(nc.vector.tensor_tensor(ka[:], rp[:], keep[:], ALU.mult))
            nc.vector.tensor_tensor(kb[:], rp[:], ka[:], ALU.subtract)
            link(nc.vector.tensor_tensor(mx[:], node[:], keep[:], ALU.mult))
            link(nc.vector.tensor_tensor(oh[:], oh[:], wide(mx[:]), ALU.mult))
            for h in range(2):
                last = nc.vector.tensor_tensor(at_rank[:, :, h, :], rank[:].unsqueeze(1).broadcast_to([NT, T, CAP]),
                                               wide(p1[:], CAP), ALU.is_equal)
            last.then_inc(inv_in, 1)
            dve.wait_ge(inv_done, 1)
            pair = ps[:, 1, 0:E_MOE].rearrange("p (q a) -> p q a", a=2)
            nc.vector.tensor_copy(tok_i[0:CAP, :], pair[0:CAP, :, 0])
            nc.vector.tensor_copy(tok_i[CAP:128, :], pair[CAP:128, :, 1])


def experts(nc, ins, W, X, XN, XT, moe, ps, normd, eo):
    RING = 3
    with ExitStack() as c:
        def sb(name, shape, dt=F32):
            return c.enter_context(nc.sbuf_tensor("e_" + name, shape, dt))

        def sem(name):
            return new_sem(nc, c, "e_" + name)

        ident = W["ident"]
        wi = sb("wi", [128, RING, K, FF])
        wo = sb("wo", [128, RING, 3, D])
        room = XT[:].rearrange("p k n -> p (k n)")
        xg = room[:, 0:2 * D].rearrange("p (a d) -> p a d", a=2)
        xgT = room[:, 2 * D:4 * D].rearrange("p (a k n) -> p a k n", a=2, k=K)
        y = room[:CAP, 4 * D:6 * D].rearrange("p (a d) -> p a d", a=2)
        back = room[:NT, 6 * D:8 * D].rearrange("p (a d) -> p a d", a=2)
        hT = room[:, 8 * D:8 * D + 6 * CAP].rearrange("p (a f c) -> p a f c", a=2, f=3)
        wl = [sem(f"wl{i}") for i in range(RING)]
        gl = [sem(f"gl{i}") for i in range(2)]
        st = [sem(f"st{i}") for i in range(2)]
        bl = [sem(f"bl{i}") for i in range(2)]
        turned, xgT_out, up_done, up_out, dn_done, dn_out, comb, comb1 = (
            sem("turned"), sem("xgT_out"), sem("up_done"), sem("up_out"), sem("dn_done"),
            sem("dn_out"), sem("comb"), sem("comb1"))
        block = c.enter_context(nc.Block(no_gpsimd_drain=True))
        slot_i, tok_i, ka, kb = moe["slot"], moe["tok"], moe["ka"], moe["kb"]
        PAIRS = E_MOE // 2

        @block.sync
        def _(sp):
            for e in range(E_MOE):
                if e >= RING:
                    sp.wait_ge(dn_done, 2 * (e - RING + 1))
                sp.dma_start(wi[:, e % RING], ins["L0_ffn_wi"][e].rearrange("(k p) f -> p k f", p=128)).then_inc(wl[e % RING], 16)
                sp.dma_start(wo[:, e % RING], ins["L0_ffn_wo"][e].rearrange("(k p) d -> p k d", p=128)).then_inc(wl[e % RING], 16)

        @block.gpsimd
        def _(pool):
            for q in range(PAIRS):
                if q >= 2:
                    pool.wait_ge(turned, 2 * (q - 1))
                nc.gpsimd.indirect_dma_start(out=xg[:, q % 2, :], out_offset=None, in_=normd[:, :],
                                             in_offset=bass.IndirectOffsetOnAxis(ap=tok_i[:, q:q + 1], axis=0)).then_inc(gl[q % 2], 16)
            for i in range(2):
                pool.wait_ge(st[i], 16 * PAIRS)
            for t in range(T):
                if t >= 2:
                    pool.wait_ge(comb1, t - 1)
                nc.gpsimd.indirect_dma_start(out=back[:, t % 2, :], out_offset=None, in_=eo[:, :],
                                             in_offset=bass.IndirectOffsetOnAxis(ap=slot_i[:, t:t + 1], axis=0)).then_inc(bl[t % 2], 16)

        @block.tensor
        def _(pe):
            for q in range(PAIRS):
                pe.wait_ge(gl[q % 2], 16 * (q // 2 + 1))
                if q >= 1:
                    pe.wait_ge(xgT_out, 2 * q)
                for h in range(2):
                    for j in range(3):
                        k = 3 * h + j
                        last = nc.tensor.transpose(ps[:, h, j * 128:(j + 1) * 128], xg[:, q % 2, k * 128:(k + 1) * 128], ident[:])
                    last.then_inc(turned, 1)
                pe.wait_ge(xgT_out, 2 * q + 2)
                for i in range(2):
                    e = 2 * q + i
                    pe.wait_ge(wl[e % RING], 32 * (e // RING + 1))
                    if e >= 2:
                        pe.wait_ge(up_out, e - 1)
                    for f in range(3):
                        for k in range(K):
                            last = nc.tensor.matmul(ps[:, 2 + i, f * CAP:(f + 1) * CAP], wi[:, e % RING, k, f * 128:(f + 1) * 128],
                                                    xgT[:, q % 2, k, i * CAP:(i + 1) * CAP], start=(k == 0), stop=(k == K - 1))
                    last.then_inc(up_done, 1)
                    pe.wait_ge(up_out, e + 1)
                    for h in range(2):
                        if e >= 2:
                            pe.wait_ge(dn_out, 2 * (e - 2) + h + 1)
                        for f in range(3):
                            last = nc.tensor.matmul(ps[:CAP, 4 + 2 * i + h, 0:384], hT[:, i, f, :],
                                                    wo[:, e % RING, f, h * 384:(h + 1) * 384], start=(f == 0), stop=(f == 2))
                        last.then_inc(dn_done, 1)

        @block.scalar
        def _(act):
            for q in range(PAIRS):
                act.wait_ge(turned, 2 * q + 1)
                nc.scalar.activation(xgT[:, q % 2, 0:3, :], ps[:, 0, 0:384].rearrange("p (j n) -> p j n", j=3), ACT.Copy).then_inc(xgT_out, 1)
                act.wait_ge(turned, 2 * q + 2)
                nc.scalar.activation(xgT[:, q % 2, 3:6, :], ps[:, 1, 0:384].rearrange("p (j n) -> p j n", j=3), ACT.Copy).then_inc(xgT_out, 1)
                for i in range(2):
                    e = 2 * q + i
                    act.wait_ge(up_done, e + 1)
                    if e >= 2:
                        act.wait_ge(dn_done, 2 * (e - 1))
                    nc.scalar.activation(hT[:, i, :, :].rearrange("p f c -> p (f c)"), ps[:, 2 + i, 0:3 * CAP], ACT.Relu).then_inc(up_out, 1)
                    act.wait_ge(dn_out, 2 * (e + 1))
                    act.dma_start(eo[e * CAP:(e + 1) * CAP, :], y[:, i, :]).then_inc(st[i], 16)

        @block.vector
        def _(dve):
            for e in range(E_MOE):
                i = e % 2
                if e >= 2:
                    dve.wait_ge(st[i], 16 * (e // 2))
                for h in range(2):
                    dve.wait_ge(dn_done, 2 * e + h + 1)
                    last = nc.vector.tensor_copy(y[:, i, h * 384:(h + 1) * 384], ps[:CAP, 4 + 2 * i + h, 0:384]).then_inc(dn_out, 1)
            for t in range(T):
                nc.vector.scalar_tensor_tensor(X[:, t, :], XN[:, t, :], kb[:, t:t + 1], X[:, t, :], ALU.mult, ALU.add).then_inc(comb, 1)
            for t in range(T):
                dve.wait_ge(bl[t % 2], 16 * (t // 2 + 1))
                dve.wait_ge(comb, t + 1)
                nc.vector.scalar_tensor_tensor(X[:, t, :], back[:, t % 2, :], ka[:, t:t + 1], X[:, t, :], ALU.mult, ALU.add).then_inc(comb1, 1)


def gat_project(nc, name, ins, keys, XT, hx, al, heads, MN, CT, ident, ps, make_mask):
    wkey, skey, dkey = keys
    C = D // heads
    HALF = D // 2
    WIDE = HALF + heads
    with ExitStack() as c:
        def sb(n, shape, dt=F32):
            return c.enter_context(nc.sbuf_tensor(name + n, shape, dt))

        def sem(n):
            return new_sem(nc, c, name + n)

        w = sb("w", [128, K, 2, WIDE])
        a = sb("a", [128, 2, D])
        prod = sb("prod", [128, 2, D])
        loaded, prod_done, folded, ones_done = sem("loaded"), sem("prod_done"), sem("folded"), sem("ones_done")
        h_done, h_out, m_done, m_act, m_dve = sem("h_done"), sem("h_out"), sem("m_done"), sem("m_act"), sem("m_dve")
        block = c.enter_context(nc.Block(no_gpsimd_drain=True))
        MB = 4

        @block.sync
        def _(sp):
            for h in range(2):
                sp.dma_start(w[:, :, h, 0:HALF], ins[wkey].rearrange("(k p) (h n) -> p k h n", p=128, h=2)[:, :, h, :]).then_inc(loaded, 16)
            for i, key in enumerate((skey, dkey)):
                sp.dma_start(a[:, i, :], ins[key].rearrange("h c -> (h c)").partition_broadcast(128)).then_inc(loaded, 16)

        @block.gpsimd
        def _(pool):
            nc.gpsimd.memset(hx[:, :, :, C:C + 1], 1.0).then_inc(ones_done, 1)
            pool.wait_ge(ones_done, 1)

        @block.vector
        def _(dve):
            dve.wait_ge(loaded, 64)
            for k in range(K):
                for i in range(2):
                    j = 2 * k + i
                    nc.vector.tensor_tensor(prod[:, j % 2, :].rearrange("p (h n) -> p h n", h=2), w[:, k, :, 0:HALF],
                                            a[:, i, :].rearrange("p (h n) -> p h n", h=2), ALU.mult).then_inc(prod_done, 1)
                    dve.wait_ge(prod_done, j + 1)
                    nc.vector.tensor_reduce(w[:, k, i, HALF:WIDE], prod[:, j % 2, :].rearrange("p (h c) -> p h c", h=heads),
                                            AX.X, ALU.add).then_inc(folded, 1)
            if make_mask:
                for t in range(T):
                    for q, n in ((0, 4), (1, 4), (2, 2)):
                        i = 3 * t + q
                        dve.wait_ge(m_done, i + 1)
                        nc.vector.tensor_scalar(MN[:, t, q * 500:q * 500 + n * NT], ps[:NT, 4 + i % MB, 0:n * NT],
                                                0.0, -BIG, ALU.is_equal, ALU.mult).then_inc(m_dve, 1)

        @block.scalar
        def _(act):
            for t in range(T):
                for h in range(2):
                    i = 2 * t + h
                    act.wait_ge(h_done, i + 1)
                    if heads > 1:
                        hh = heads // 2
                        out = hx[:, t, h * hh:(h + 1) * hh, 0:C]
                        in_ = ps[:NT, i % 4, 0:HALF].rearrange("p (g c) -> p g c", g=hh)
                    else:
                        out, in_ = hx[:, t, 0, h * HALF:(h + 1) * HALF], ps[:NT, i % 4, 0:HALF]
                    nc.scalar.activation(out, in_, ACT.Copy)
                    nc.scalar.activation(al[:, t, h * heads:(h + 1) * heads], ps[:NT, i % 4, HALF:WIDE], ACT.Copy).then_inc(h_out, 1)

        @block.tensor
        def _(pe):
            if make_mask:
                for t in range(T):
                    for q, n in ((0, 4), (1, 4), (2, 2)):
                        i = 3 * t + q
                        if i >= MB:
                            pe.wait_ge(m_dve, i - MB + 1)
                        for j in range(n):
                            last = nc.tensor.transpose(ps[:NT, 4 + i % MB, j * NT:(j + 1) * NT],
                                                       CT[:, 4 * q + j, t * NT:(t + 1) * NT], ident[:NT, :NT])
                        last.then_inc(m_done, 1)
            pe.wait_ge(folded, 2 * K)
            for t in range(T):
                for h in range(2):
                    i = 2 * t + h
                    if i >= 4:
                        pe.wait_ge(h_out, i - 3)
                    for k in range(K):
                        last = nc.tensor.matmul(ps[:NT, i % 4, 0:WIDE], XT[:, k, t * NT:(t + 1) * NT], w[:, k, h, :],
                                                start=(k == 0), stop=(k == K - 1))
                    last.then_inc(h_done, 1)


def gat_attention(nc, name, ins, hx, al, heads, MN, CT, ident, ps, ald, out, P_in_CT):
    C = D // heads
    ER, PR = 3, 2
    with ExitStack() as c:
        def sb(n, shape, dt=F32):
            return c.enter_context(nc.sbuf_tensor(name + n, shape, dt))

        def sem(n):
            return new_sem(nc, c, name + n)

        srow = sb("srow", [NT, 2, N])
        fifth = sb("fifth", [NT, N])
        d08 = sb("d08", [NT, T, heads])
        junk = sb("junk", [NT, N], BF16)
        mx = sb("mx", [NT, 2, T])
        shift = sb("shift", [NT, 2, 2, T])
        E = sb("E", [NT, ER, N])
        alr = E[0:16, 0, :]
        P = None if P_in_CT else sb("P", [NT, PR, T, NT])
        r_done, d_done, fifth_done = sem("r_done"), sem("d_done"), sem("fifth_done")
        rz = sb("rz", [NT, 2, T])
        al_T, al_sb, al_st, s_ld = sem("al_T"), sem("al_sb"), sem("al_st"), [sem("s_ld0"), sem("s_ld1")]
        mx_done, v, shift_done, y_done, e_done, eT_done, p_done, o_done, o_out, e_used = (
            sem("mx_done"), sem("v"), sem("shift_done"), sem("y_done"), sem("e_done"), sem("eT_done"), sem("p_done"),
            sem("o_done"), sem("o_out"), sem("e_used"))
        block = c.enter_context(nc.Block(no_gpsimd_drain=True))

        @block.sync
        def _(sp):
            sp.wait_ge(al_sb, 3)
            sp.dma_start(ald[0:2 * heads, :], alr[0:2 * heads, :]).then_inc(al_st, 16)
            sp.wait_ge(al_st, 16)
            for h in range(heads):
                if h >= 2:
                    sp.wait_ge(r_done, T * (h - 1))
                    sp.wait_ge(mx_done, T * (h - 1))
                sp.dma_start(srow[:, h % 2, :], ald[h:h + 1, :].rearrange("a n -> (a n)").partition_broadcast(NT)).then_inc(s_ld[h % 2], 16)

        @block.tensor
        def _(pe):
            for q, n in ((0, 4), (1, 4), (2, 2)):
                for j in range(n):
                    last = nc.tensor.transpose(ps[:2 * heads, q, j * NT:(j + 1) * NT], al[:, 4 * q + j, :], ident[:NT, :NT])
                last.then_inc(al_T, 1)
            pe.wait_ge(al_sb, 3)

            def turn(h, t):
                i = h * T + t
                pe.wait_ge(e_done, i + 1)
                for q, n in ((0, 4), (1, 4), (2, 2)):
                    g = 3 * i + q
                    if g >= 4:
                        pe.wait_ge(p_done, g - 3)
                    for j in range(n):
                        last = nc.tensor.transpose(ps[:NT, g % 4, j * NT:(j + 1) * NT], E[:, i % ER, (4 * q + j) * NT:(4 * q + j + 1) * NT],
                                                   ident[:NT, :NT])
                    last.then_inc(eT_done, 1)

            def weigh(h, t):
                i = h * T + t
                pe.wait_ge(p_done, 3 * i + 3)
                if heads > 1:
                    if i >= 4:
                        pe.wait_ge(o_out, i - 3)
                    for s in range(T):
                        last = nc.tensor.matmul(ps[:NT, 4 + i % 4, 0:C + 1], P[:, i % PR, s, 0:NT], hx[:, s, h, :],
                                                start=(s == 0), stop=(s == T - 1))
                    last.then_inc(o_done, 1)
                else:
                    for half in range(2):
                        g = 2 * i + half
                        if g >= 4:
                            pe.wait_ge(o_out, g - 3)
                        for s in range(T):
                            c0, c1 = (D // 2, D + 1) if half == 0 else (0, D // 2)
                            last = nc.tensor.matmul(ps[:NT, 4 + g % 4, 0:c1 - c0], CT[:, s, t * NT:(t + 1) * NT],
                                                    hx[:, s, 0, c0:c1], start=(s == 0), stop=(s == T - 1))
                        last.then_inc(o_done, 1)

            steps = [(h, t) for h in range(heads) for t in range(T)]
            turn(*steps[0])
            for i, (h, t) in enumerate(steps):
                if i + 1 < len(steps):
                    turn(*steps[i + 1])
                weigh(h, t)

        @block.scalar
        def _(act):
            for q, n in ((0, 500), (1, 500), (2, 250)):
                act.wait_ge(al_T, q + 1)
                nc.scalar.activation(alr[0:2 * heads, q * 500:q * 500 + n], ps[:2 * heads, q, 0:n], ACT.Copy).then_inc(al_sb, 1)

            act.wait_ge(d_done, 1)

            def relu(h, t):
                i = h * T + t
                if t == 0:
                    act.wait_ge(s_ld[h % 2], 16 * (h // 2 + 1))
                    if h:
                        act.wait_ge(y_done, T * h)
                    nc.scalar.activation(fifth[:], srow[:, h % 2, :], ACT.Copy, scale=0.2).then_inc(fifth_done, 1)
                if i >= ER:
                    act.wait_ge(eT_done, 3 * (i - ER + 1))
                nc.scalar.activation(E[:, i % ER, :], srow[:, h % 2, :], ACT.Relu, bias=d08[:, t, h:h + 1],
                                     scale=0.8).then_inc(r_done, 1)

            def expo(h, t):
                i = h * T + t
                act.wait_ge(y_done, i + 1)
                act.wait_ge(shift_done, h + 1)
                nc.scalar.activation(E[:, i % ER, :], E[:, i % ER, :], ACT.Exp, bias=shift[:, h % 2, 1, t:t + 1]).then_inc(e_done, 1)

            steps = [(h, t) for h in range(heads) for t in range(T)]
            relu(*steps[0])
            relu(*steps[1])
            for i, (h, t) in enumerate(steps):
                expo(h, t)
                if i + 2 < len(steps):
                    relu(*steps[i + 2])

        @block.gpsimd
        def _(pool):
            for i in range(heads * T):
                pool.wait_ge(r_done, i + 1)
                pool.wait_ge(fifth_done, i // T + 1)
                nc.gpsimd.tensor_tensor(E[:, i % ER, :], E[:, i % ER, :], fifth[:], ALU.add).then_inc(y_done, 1)

        @block.vector
        def _(dve):
            n = [0]

            def link(ins_):
                n[0] += 1
                ins_.then_inc(v, 1)
                dve.wait_ge(v, n[0])

            def maxima(h, t):
                if t == 0:
                    dve.wait_ge(s_ld[h % 2], 16 * (h // 2 + 1))
                k = h * T + t
                if k:
                    dve.wait_ge(mx_done, k)
                nc.vector.tensor_tensor_reduce(out=junk[:], in0=srow[:, h % 2, :], in1=MN[:, t, :], scale=1.0, scalar=-BIG,
                                               op0=ALU.add, op1=ALU.max, accum_out=mx[:, h % 2, t:t + 1]).then_inc(mx_done, 1)

            def shifts(h):
                a, b = shift[:, h % 2, 0], shift[:, h % 2, 1]
                dve.wait_ge(mx_done, T * (h + 1))
                if h >= 2:
                    dve.wait_ge(e_done, T * (h - 1))
                link(nc.vector.tensor_tensor(a, mx[:, h % 2], al[:, :, heads + h], ALU.add))
                link(nc.vector.tensor_scalar(a, a, 0.0, -0.8, ALU.max, ALU.mult))
                nc.vector.scalar_tensor_tensor(b, mx[:, h % 2], -0.2, a, ALU.mult, ALU.add).then_inc(shift_done, 1)

            def masked(h, t):
                i = h * T + t
                for q, m in ((0, 4), (1, 4), (2, 2)):
                    g = 3 * i + q
                    dve.wait_ge(eT_done, g + 1)
                    if not P_in_CT and i >= PR:
                        dve.wait_ge(o_done, i - PR + 1)
                    ct = CT[:, 4 * q:4 * q + m, t * NT:(t + 1) * NT]
                    dst = ct if P_in_CT else P[:, i % PR, 4 * q:4 * q + m, 0:NT]
                    nc.vector.scalar_tensor_tensor(dst, ps[:NT, g % 4, 0:m * NT].rearrange("p (j n) -> p j n", j=m), 2.0, ct,
                                                   ALU.min, ALU.mult).then_inc(p_done, 1)

            finish = finish_gat2(out) if P_in_CT else finish_gat1(out)
            nc.vector.tensor_scalar(d08[:], al[:, :, heads:2 * heads], 0.8, None, ALU.mult).then_inc(d_done, 1)
            for t in range(T):
                maxima(0, t)
            shifts(0)
            for h in range(heads):
                for t in range(T):
                    masked(h, t)
                    if h + 1 < heads:
                        maxima(h + 1, t)
                    if t == T - 1 and h + 1 < heads:
                        shifts(h + 1)
                    if t >= 1:
                        finish(dve, nc, ps, o_done, o_out, rz, link, h, t - 1)
                finish(dve, nc, ps, o_done, o_out, rz, link, h, T - 1)


def finish_gat1(out):
    C = 96

    def finish(dve, nc, ps, o_done, o_out, rz, link, h, t):
        i = h * T + t
        dve.wait_ge(o_done, i + 1)
        acc = ps[:NT, 4 + i % 4, :]
        link(nc.vector.tensor_scalar(rz[:, h % 2, t:t + 1], acc[:, C:C + 1], 1e-16, None, ALU.add))
        link(nc.vector.reciprocal(rz[:, h % 2, t:t + 1], rz[:, h % 2, t:t + 1]))
        nc.vector.tensor_scalar(out[:, t, h * C:(h + 1) * C], acc[:, 0:C], rz[:, h % 2, t:t + 1], None,
                                ALU.mult).then_inc(o_out, 1)
    return finish


def finish_gat2(X):
    def finish(dve, nc, ps, o_done, o_out, rz, link, h, t):
        half = D // 2
        for part in range(2):
            g = 2 * t + part
            dve.wait_ge(o_done, g + 1)
            acc = ps[:NT, 4 + g % 4, :]
            if part == 0:
                link(nc.vector.tensor_scalar(rz[:, 0, t:t + 1], acc[:, half:half + 1], 1e-16, None, ALU.add))
                link(nc.vector.reciprocal(rz[:, 0, t:t + 1], rz[:, 0, t:t + 1]))
            dst = X[:, t, half:D] if part == 0 else X[:, t, 0:half]
            nc.vector.scalar_tensor_tensor(dst, acc[:, 0:half], rz[:, 0, t:t + 1], dst, ALU.mult, ALU.add).then_inc(o_out, 1)
    return finish


def elu_and_bias(nc, ins, O1, X):
    with ExitStack() as c:
        b2 = c.enter_context(nc.sbuf_tensor("elu_b2", [NT, D], F32))
        b1 = c.enter_context(nc.sbuf_tensor("elu_b1", [NT, D], F32))
        tmp = c.enter_context(nc.sbuf_tensor("elu_tmp", [NT, 3, D], F32))
        biased = new_sem(nc, c, "elu_biased")
        loaded, low, ex, added, out = (new_sem(nc, c, "elu_" + n) for n in ("loaded", "low", "ex", "added", "out"))
        block = c.enter_context(nc.Block(no_gpsimd_drain=True))

        @block.sync
        def _(sp):
            sp.dma_start(b2[:], ins["L1_gnn_b2"].partition_broadcast(NT)).then_inc(loaded, 16)
            sp.dma_start(b1[:], ins["L1_gnn_b1"].partition_broadcast(NT)).then_inc(loaded, 16)

        @block.gpsimd
        def _(pool):
            pool.wait_ge(loaded, 32)
            for t in range(T):
                nc.gpsimd.tensor_tensor(X[:, t, :], X[:, t, :], b2[:], ALU.add).then_inc(added, 1)
            pool.wait_ge(added, T)

        @block.scalar
        def _(act):
            for t in range(T):
                act.wait_ge(low, t + 1)
                nc.scalar.activation(tmp[:, t % 3, :], tmp[:, t % 3, :], ACT.Exp).then_inc(ex, 1)

        @block.vector
        def _(dve):
            def lower(t):
                if t >= 3:
                    dve.wait_ge(out, 2 * (t - 2))
                nc.vector.tensor_tensor(O1[:, t, :], O1[:, t, :], b1[:], ALU.add).then_inc(biased, 1)
                dve.wait_ge(biased, t + 1)
                nc.vector.tensor_scalar(tmp[:, t % 3, :], O1[:, t, :], 0.0, None, ALU.min).then_inc(low, 1)
            dve.wait_ge(loaded, 32)
            lower(0)
            lower(1)
            for t in range(T):
                if t + 2 < T:
                    lower(t + 2)
                nc.vector.tensor_scalar(O1[:, t, :], O1[:, t, :], 0.0, -1.0, ALU.max, ALU.add).then_inc(out, 1)
                dve.wait_ge(ex, t + 1)
                dve.wait_ge(out, 2 * t + 1)
                nc.vector.tensor_tensor(O1[:, t, :], O1[:, t, :], tmp[:, t % 3, :], ALU.add).then_inc(out, 1)


HD, E_ATT = 256, 3


def ffn_project(nc, ins, XT, QK, V, we, ident, ps, X):
    RING = 4
    M = 2 * D // 128
    with ExitStack() as c:
        def sb(n, shape, dt=F32):
            return c.enter_context(nc.sbuf_tensor("p_" + n, shape, dt))

        def sem(n):
            return new_sem(nc, c, "p_" + n)

        wqk = sb("wqk", [128, RING, K, 128])
        wv = sb("wv", [128, K, E_ATT, HD])
        bv, bp = sb("bv", [NT, D]), sb("bp", [NT, D])
        bqk = sb("bqk", [128, M])
        wg1, wg2 = sb("wg1", [128, K, 32]), sb("wg2", [32, E_ATT])
        bg1, bg2 = sb("bg1", [32, 1]), sb("bg2", [NT, E_ATT])
        g1 = sb("g1", [32, N])
        lg = sb("lg", [NT, T, E_ATT])
        p = sb("p", [NT, T, E_ATT])
        c1, c2, mx = sb("c1", [NT, T]), sb("c2", [NT, T]), sb("mx", [NT, T])
        loaded, wl, bpl, added = sem("loaded"), [sem(f"wl{i}") for i in range(RING)], sem("bpl"), sem("added")
        q_done, q_out, v_done, v_out, g1_done, g1_out, g2_done, e_in, e_out, v = (
            sem("q_done"), sem("q_out"), sem("v_done"), sem("v_out"), sem("g1_done"), sem("g1_out"), sem("g2_done"),
            sem("e_in"), sem("e_out"), sem("v"))
        block = c.enter_context(nc.Block(no_gpsimd_drain=True))
        NLOAD = 7 + E_ATT

        @block.sync
        def _(sp):
            def load(dst, src, small=False):
                sp.dma_start(dst, src, allow_slow_non_contiguous=small).then_inc(loaded, 16)
            load(wg1[:], ins["L1_ffn_Wg1"].rearrange("(k p) g -> p k g", p=128))
            load(wg2[:], ins["L1_ffn_Wg2"])
            load(bg1[:], ins["L1_ffn_bg1"].rearrange("(g a) -> g a", a=1), True)
            load(bg2[:], ins["L1_ffn_bg2"].partition_broadcast(NT))
            load(bqk[:], ins["L1_ffn_bqk"].rearrange("(m p) -> p m", p=128), True)
            load(bv[:], ins["L1_ffn_bv"].rearrange("e d -> (e d)").partition_broadcast(NT))
            for e in range(E_ATT):
                load(wv[:, :, e, :], ins["L1_ffn_Wv"][e].rearrange("(k p) d -> p k d", p=128))
            load(bp[:], ins["L1_ffn_bp"].partition_broadcast(NT))
            for m in range(M):
                if m >= RING:
                    sp.wait_ge(q_done, 3 * (m - RING + 1))
                sp.dma_start(wqk[:, m % RING], ins["L1_ffn_Wqk"][:, m * 128:(m + 1) * 128].rearrange("(k p) n -> p k n", p=128)).then_inc(wl[m % RING], 16)

        @block.gpsimd
        def _(pool):
            pool.wait_ge(loaded, 16 * NLOAD)
            for t in range(T):
                nc.gpsimd.tensor_tensor(X[:, t, :], X[:, t, :], bp[:], ALU.add).then_inc(added, 1)
            pool.wait_ge(added, T)

        @block.tensor
        def _(pe):
            pe.wait_ge(loaded, 16 * NLOAD)
            for g, (n0, nn) in enumerate(CHUNKS):
                for k in range(K):
                    last = nc.tensor.matmul(ps[:32, g, 0:nn], wg1[:, k, :], XT[:, k, n0:n0 + nn], start=(k == 0), stop=(k == K - 1))
                last.then_inc(g1_done, 1)
            pe.wait_ge(g1_out, 3)
            for t in range(T):
                last = nc.tensor.matmul(ps[:NT, 7, t * E_ATT:(t + 1) * E_ATT], g1[:, t * NT:(t + 1) * NT], wg2[:], start=True, stop=True)
            last.then_inc(g2_done, 1)
            for m in range(M):
                pe.wait_ge(wl[m % RING], 16 * (m // RING + 1))
                for g, (n0, nn) in enumerate(CHUNKS):
                    i = 3 * m + g
                    if i >= 4:
                        pe.wait_ge(q_out, i - 3)
                    for k in range(K):
                        last = nc.tensor.matmul(ps[:, i % 4, 0:nn], wqk[:, m % RING, k, :], XT[:, k, n0:n0 + nn],
                                                start=(k == 0), stop=(k == K - 1))
                    last.then_inc(q_done, 1)
            for t in range(T):
                for h in range(2):
                    i = 2 * t + h
                    if i >= 3:
                        pe.wait_ge(v_out, i - 2)
                    for k in range(K):
                        last = nc.tensor.matmul(ps[:NT, 4 + i % 3, 0:384], XT[:, k, t * NT:(t + 1) * NT],
                                                wv[:, k, :, :].rearrange("p e d -> p (e d)")[:, h * 384:(h + 1) * 384],
                                                start=(k == 0), stop=(k == K - 1))
                    last.then_inc(v_done, 1)

        @block.scalar
        def _(act):
            act.wait_ge(loaded, 16 * NLOAD)
            for g, (n0, nn) in enumerate(CHUNKS):
                act.wait_ge(g1_done, g + 1)
                nc.scalar.activation(g1[:, n0:n0 + nn], ps[:32, g, 0:nn], ACT.Relu, bias=bg1[:, 0:1]).then_inc(g1_out, 1)
            act.wait_ge(e_in, 1)
            nc.scalar.activation(p[:], lg[:], ACT.Exp).then_inc(e_out, 1)
            act.wait_ge(e_in, 2)
            nc.scalar.activation(lg[:], p[:], ACT.Exp).then_inc(e_out, 1)
            for m in range(M):
                for g, (n0, nn) in enumerate(CHUNKS):
                    i = 3 * m + g
                    act.wait_ge(q_done, i + 1)
                    nc.scalar.activation(QK[:, m, n0:n0 + nn], ps[:, i % 4, 0:nn], ACT.Identity, bias=bqk[:, m:m + 1]).then_inc(q_out, 1)

        @block.vector
        def _(dve):
            n = [0]

            def link(ins_):
                n[0] += 1
                ins_.then_inc(v, 1)
                dve.wait_ge(v, n[0])

            def each(a):
                return a.unsqueeze(2).broadcast_to([NT, T, E_ATT])

            dve.wait_ge(loaded, 16 * NLOAD)
            dve.wait_ge(g2_done, 1)
            link(nc.vector.tensor_tensor(lg[:], ps[:NT, 7, 0:T * E_ATT].rearrange("p (t e) -> p t e", t=T),
                                         bg2[:].unsqueeze(1).broadcast_to([NT, T, E_ATT]), ALU.add))
            link(nc.vector.tensor_reduce(mx[:], lg[:], AX.X, ALU.max))
            nc.vector.tensor_tensor(lg[:], lg[:], each(mx[:]), ALU.subtract).then_inc(e_in, 1)
            dve.wait_ge(e_out, 1)
            link(nc.vector.tensor_reduce(mx[:], p[:], AX.X, ALU.add))
            link(nc.vector.reciprocal(mx[:], mx[:]))
            nc.vector.tensor_tensor(p[:], p[:], each(mx[:]), ALU.mult).then_inc(e_in, 1)
            dve.wait_ge(e_out, 2)
            for e in range(E_ATT):
                a, b = [x for x in range(E_ATT) if x != e]
                link(nc.vector.tensor_tensor(c1[:], p[:, :, a], p[:, :, e], ALU.is_ge if a < e else ALU.is_gt))
                link(nc.vector.tensor_tensor(c2[:], p[:, :, b], p[:, :, e], ALU.is_ge if b < e else ALU.is_gt))
                link(nc.vector.tensor_tensor(c1[:], c1[:], c2[:], ALU.mult))
                link(nc.vector.tensor_scalar(c1[:], c1[:], -1.0, 1.0, ALU.mult, ALU.add))
                link(nc.vector.tensor_tensor(we[:, :, e], lg[:, :, e], c1[:], ALU.mult))
            link(nc.vector.tensor_reduce(mx[:], we[:], AX.X, ALU.add))
            link(nc.vector.reciprocal(mx[:], mx[:]))
            link(nc.vector.tensor_tensor(we[:], we[:], each(mx[:]), ALU.mult))
            for t in range(T):
                for h in range(2):
                    i = 2 * t + h
                    dve.wait_ge(v_done, i + 1)
                    nc.vector.tensor_tensor(V[:, t, h * 384:(h + 1) * 384], ps[:NT, 4 + i % 3, 0:384], bv[:, h * 384:(h + 1) * 384],
                                            ALU.add).then_inc(v_out, 1)


def ffn_attention(nc, ins, QK, V, we, YT, X, ident, ps, out):
    SCALE = 1.0 / math.sqrt(HD)
    with ExitStack() as c:
        def sb(n, shape, dt=F32):
            return c.enter_context(nc.sbuf_tensor("a_" + n, shape, dt))

        def sem(n):
            return new_sem(nc, c, "a_" + n)

        wp = sb("wp", [128, K, D])
        cw, cb = sb("cw", [128, 2, 3]), sb("cb", [128, 2])
        causal = sb("causal", [NT, NT])
        E = sb("E", [NT, 2, N])
        PT = sb("PT", [NT, 2, T, NT])
        qc = sb("qc", [128, N])
        mx = sb("mx", [NT, 2, 4])
        rs = sb("rs", [NT, 2, 4])
        loaded, made, v, conv_done, s_done, m_done, x_done, e_done, n_done, t_done, pt_act, pt_dve, y_done, y_out = (
            sem("loaded"), sem("made"), sem("v"), sem("conv_done"), sem("s_done"), sem("m_done"), sem("x_done"), sem("e_done"),
            sem("n_done"), sem("t_done"), sem("pt_act"), sem("pt_dve"), sem("y_done"), sem("y_out"))
        o_done, o_out, stored = sem("o_done"), sem("o_out"), sem("stored")
        block = c.enter_context(nc.Block(no_gpsimd_drain=True))
        steps = [(e, i) for e in (1, 2, 0) for i in range(T)]

        def blocks(i):
            return [(q, min(4, i + 1 - 4 * q)) for q in range(i // 4 + 1)]

        turned = [0]
        for _, i in steps:
            turned.append(turned[-1] + len(blocks(i)))

        @block.sync
        def _(sp):
            sp.dma_start(cw[:], ins["L1_ffn_conv_w"].rearrange("(k p) a w -> p k (a w)", p=128), allow_slow_non_contiguous=True).then_inc(loaded, 16)
            sp.dma_start(cb[:], ins["L1_ffn_conv_b"].rearrange("(k p) -> p k", p=128), allow_slow_non_contiguous=True).then_inc(loaded, 16)
            sp.dma_start(wp[:], ins["L1_ffn_Wp"].rearrange("(k p) d -> p k d", p=128)).then_inc(loaded, 16)
            for t in range(T):
                sp.wait_ge(o_out, 2 * t + 2)
                sp.dma_start(out[t * NT:(t + 1) * NT, :], X[:, t, :]).then_inc(stored, 16)
            sp.wait_ge(stored, 16 * T)

        @block.gpsimd
        def _(pool):
            nc.gpsimd.memset(causal[:], 0.0).then_inc(made, 1)
            pool.wait_ge(made, 1)
            nc.gpsimd.affine_select(out=causal[:], in_=causal[:], compare_op=ALU.is_ge, fill=-BIG, base=0,
                                    pattern=[[-1, NT]], channel_multiplier=1).then_inc(made, 1)
            pool.wait_ge(made, 2)

        @block.tensor
        def _(pe):
            def scores(z):
                e, i = steps[z]
                if e == 0:
                    pe.wait_ge(conv_done, 2)
                if z:
                    pe.wait_ge(x_done, z)
                for q, n in blocks(i):
                    for m in range(2):
                        last = nc.tensor.matmul(ps[:NT, q, 0:n * NT], QK[:, 2 * e + m, i * NT:(i + 1) * NT],
                                                QK[:, 6 + 2 * e + m, q * 500:q * 500 + n * NT], start=(m == 0), stop=(m == 1))
                last.then_inc(s_done, 1)

            def turn(z):
                e, i = steps[z]
                pe.wait_ge(n_done, z + 1)
                for q, n in blocks(i):
                    g = turned[z] + q
                    if g >= 3:
                        pe.wait_ge(pt_dve, g - 2)
                    for j in range(n):
                        s = 4 * q + j
                        last = nc.tensor.transpose(ps[:NT, 3 + g % 3, j * NT:(j + 1) * NT], E[:, z % 2, s * NT:(s + 1) * NT], ident[:NT, :NT])
                    last.then_inc(t_done, 1)

            def values(z):
                e, i = steps[z]
                pe.wait_ge(pt_dve, turned[z + 1])
                if z >= 2:
                    pe.wait_ge(y_out, z - 1)
                for m in range(2):
                    for s in range(i + 1):
                        last = nc.tensor.matmul(ps[:, 6 + z % 2, m * NT:(m + 1) * NT], V[:, s, e * HD + m * 128:e * HD + (m + 1) * 128],
                                                PT[:, z % 2, s, :], start=(s == 0), stop=(s == i))
                last.then_inc(y_done, 1)

            Z = len(steps)
            scores(0)
            for z in range(Z):
                if z + 1 < Z:
                    scores(z + 1)
                turn(z)
                values(z)
            pe.wait_ge(y_out, Z)
            pe.wait_ge(loaded, 48)
            for t in range(T):
                for h in range(2):
                    i = 2 * t + h
                    if i >= 4:
                        pe.wait_ge(o_out, i - 3)
                    for k in range(K):
                        last = nc.tensor.matmul(ps[:NT, i % 4, 0:384], YT[:, k, t * NT:(t + 1) * NT], wp[:, k, h * 384:(h + 1) * 384],
                                                start=(k == 0), stop=(k == K - 1))
                    last.then_inc(o_done, 1)

        @block.scalar
        def _(act):
            for z, (e, i) in enumerate(steps):
                act.wait_ge(m_done, z + 1)
                if z >= 2:
                    act.wait_ge(t_done, turned[z - 1])
                for q, n in blocks(i):
                    last = nc.scalar.activation(E[:, z % 2, q * 500:q * 500 + n * NT], ps[:NT, q, 0:n * NT], ACT.Exp,
                                                bias=mx[:, z % 2, 3:4], scale=SCALE, accum_out=rs[:, z % 2, q:q + 1])
                last.then_inc(x_done, 1)
                if z >= 1:
                    act.wait_ge(y_done, z)
                    pe_, pi = steps[z - 1]
                    nc.scalar.activation(YT[:, 2 * pe_:2 * pe_ + 2, pi * NT:(pi + 1) * NT],
                                         ps[:, 6 + (z - 1) % 2, 0:2 * NT].rearrange("p (m n) -> p m n", m=2), ACT.Copy).then_inc(y_out, 1)
            z = len(steps)
            act.wait_ge(y_done, z)
            pe_, pi = steps[z - 1]
            nc.scalar.activation(YT[:, 2 * pe_:2 * pe_ + 2, pi * NT:(pi + 1) * NT],
                                 ps[:, 6 + (z - 1) % 2, 0:2 * NT].rearrange("p (m n) -> p m n", m=2), ACT.Copy).then_inc(y_out, 1)

        @block.vector
        def _(dve):
            n = [0]

            def link(ins_):
                n[0] += 1
                ins_.then_inc(v, 1)
                dve.wait_ge(v, n[0])

            dve.wait_ge(loaded, 48)
            for m in range(2):
                q = QK[:, m, :]
                link(nc.vector.tensor_scalar(qc[:], q, cw[:, m, 1:2], cb[:, m:m + 1], ALU.mult, ALU.add))
                link(nc.vector.scalar_tensor_tensor(qc[:, 1:N], q[:, 0:N - 1], cw[:, m, 0:1], qc[:, 1:N], ALU.mult, ALU.add))
                link(nc.vector.scalar_tensor_tensor(qc[:, 0:N - 1], q[:, 1:N], cw[:, m, 2:3], qc[:, 0:N - 1], ALU.mult, ALU.add))
                nc.vector.tensor_copy(q, qc[:]).then_inc(conv_done, 1)
                dve.wait_ge(conv_done, m + 1)
            dve.wait_ge(made, 2)

            def maxima(z):
                e, i = steps[z]
                dve.wait_ge(s_done, z + 1)
                q0 = i // 4
                diag = ps[:NT, q0, (i - 4 * q0) * NT:(i - 4 * q0 + 1) * NT]
                link(nc.vector.tensor_tensor(diag, diag, causal[:], ALU.add))
                for q, m in blocks(i):
                    link(nc.vector.tensor_reduce(mx[:, z % 2, q:q + 1], ps[:NT, q, 0:m * NT], AX.X, ALU.max))
                nq = len(blocks(i))
                if nq > 1:
                    link(nc.vector.tensor_reduce(mx[:, z % 2, 3:4], mx[:, z % 2, 0:nq], AX.X, ALU.max))
                src = mx[:, z % 2, 3:4] if nq > 1 else mx[:, z % 2, 0:1]
                nc.vector.tensor_scalar(mx[:, z % 2, 3:4], src, -SCALE, None, ALU.mult).then_inc(m_done, 1)

            def normalise(z):
                e, i = steps[z]
                dve.wait_ge(x_done, z + 1)
                nq = len(blocks(i))
                r = rs[:, z % 2, 3:4]
                if nq > 1:
                    link(nc.vector.tensor_reduce(r, rs[:, z % 2, 0:nq], AX.X, ALU.add))
                    link(nc.vector.reciprocal(r, r))
                else:
                    link(nc.vector.reciprocal(r, rs[:, z % 2, 0:1]))
                link(nc.vector.tensor_tensor(r, r, we[:, i, e:e + 1], ALU.mult))
                L = (i + 1) * NT
                nc.vector.tensor_scalar(E[:, z % 2, 0:L], E[:, z % 2, 0:L], r, None, ALU.mult).then_inc(n_done, 1)

            def copy_turned(z):
                e, i = steps[z]
                if z >= 2:
                    dve.wait_ge(y_done, z - 1)
                for q, m in blocks(i):
                    g = turned[z] + q
                    dve.wait_ge(t_done, g + 1)
                    nc.vector.tensor_copy(PT[:, z % 2, 4 * q:4 * q + m, :],
                                          ps[:NT, 3 + g % 3, 0:m * NT].rearrange("p (j n) -> p j n", j=m)).then_inc(pt_dve, 1)

            Z = len(steps)
            maxima(0)
            for z in range(Z):
                normalise(z)
                if z + 1 < Z:
                    maxima(z + 1)
                copy_turned(z)
            for t in range(T):
                for h in range(2):
                    i = 2 * t + h
                    dve.wait_ge(o_done, i + 1)
                    nc.vector.tensor_tensor(X[:, t, h * 384:(h + 1) * 384], X[:, t, h * 384:(h + 1) * 384], ps[:NT, i % 4, 0:384],
                                            ALU.add).then_inc(o_out, 1)


def program(nc, ins, out):
    with ExitStack() as c:
        X = c.enter_context(nc.sbuf_tensor("X", [NT, T, D], F32))
        ident = c.enter_context(nc.sbuf_tensor("ident", [128, 128], F32))
        stat = c.enter_context(nc.sbuf_tensor("stat", [NT, T, 4], F32))
        eps = c.enter_context(nc.sbuf_tensor("eps", [128, 2], F32))
        ps = c.enter_context(nc.psum_tensor("ps", [128, BANKS, 512], F32))
        normd = nc.dram_tensor("normd", [N, D], F32).ap()
        eo = nc.dram_tensor("eo", [E_MOE * CAP, D], F32).ap()
        with ExitStack() as s:
            loaded = new_sem(nc, s, "x_loaded")
            made = new_sem(nc, s, "consts_made")
            block = s.enter_context(nc.Block(no_gpsimd_drain=True))

            @block.sync
            def _(sp):
                sp.dma_start(X[:], ins["x"].rearrange("(t p) d -> p t d", p=NT)).then_inc(loaded, 16)
                sp.wait_ge(loaded, 16)

            @block.gpsimd
            def _(pool):
                nc.gpsimd.memset(eps[:, 0:1], 1e-5)
                nc.gpsimd.memset(eps[:, 1:2], 1e-6)
                nc.gpsimd.memset(ident[:], 0.0).then_inc(made, 1)
                pool.wait_ge(made, 1)
                nc.gpsimd.affine_select(out=ident[:], in_=ident[:], compare_op=ALU.not_equal, fill=1.0,
                                        base=0, pattern=[[-1, 128]], channel_multiplier=1).then_inc(made, 1)
                pool.wait_ge(made, 2)
        A = c.enter_context(nc.sbuf_tensor("A", [128, T * 8 * 97], F32))
        XT = A[:, 0:K * N].rearrange("p (k n) -> p k n", k=K)
        ald = nc.dram_tensor("ald", [16, N], F32).ap()

        def by_node(area, width=D):
            return area[:NT, 0:T * width].rearrange("p (t d) -> p t d", t=T)

        with ExitStack() as graph:
            CT = graph.enter_context(nc.sbuf_tensor("CT", [NT, T, N], F32))
            with ExitStack() as early:
                ones = early.enter_context(nc.sbuf_tensor("ones", [128, 128], F32))
                cst = {"ident": ident, "ones": ones}
                moe = {n: early.enter_context(nc.sbuf_tensor("moe_" + n, [NT, T], F32)) for n in ("rp", "ka", "kb")}
                moe["slot"] = early.enter_context(nc.sbuf_tensor("moe_slot", [NT, T], I32))
                moe["tok"] = early.enter_context(nc.sbuf_tensor("moe_tok", [128, E_MOE // 2], I32))
                with ExitStack() as s:
                    XN = s.enter_context(nc.sbuf_tensor("XN0", [NT, T, D], F32))
                    layernorm(nc, "ln0", X, XN, stat, eps[:NT, 0:1])
                    transpose_nodes(nc, "t0", XN, XT, ident, ps)
                with ExitStack() as s:
                    MT = s.enter_context(nc.sbuf_tensor("MT", [NT, T, N], F32))
                    dense_graph(nc, ins, cst, MT, CT, ps)
                    low_rank_and_gcn(nc, ins, XT, MT, X, cst, stat, ones, ps)
                with ExitStack() as s:
                    XN = s.enter_context(nc.sbuf_tensor("XN1", [NT, T, D], F32))
                    layernorm(nc, "ln1", X, XN, stat, eps[:NT, 0:1])
                    route(nc, ins, cst, X, XN, XT, stat, eps[:NT, 1:2], moe, ps, normd)
                    experts(nc, ins, cst, X, XN, XT, moe, ps, normd, eo)
            B = graph.enter_context(nc.sbuf_tensor("B", [128, T * 8 * 97], F32))
            MN = graph.enter_context(nc.sbuf_tensor("MN", [NT, T, N], BF16))
            layernorm(nc, "ln2", X, by_node(B), stat, eps[:NT, 0:1])
            transpose_nodes(nc, "t2", by_node(B), XT, ident, ps)
            hx = B[:NT].rearrange("p (t h c) -> p t h c", t=T, h=8)
            O1 = by_node(A)
            with ExitStack() as s:
                al = s.enter_context(nc.sbuf_tensor("al1", [NT, T, 16], F32))
                gat_project(nc, "h1_", ins, ("L1_gnn_W1", "L1_gnn_a_src1", "L1_gnn_a_dst1"), XT, hx, al, 8, MN, CT, ident, ps, True)
                gat_attention(nc, "g1_", ins, hx, al, 8, MN, CT, ident, ps, ald, O1, False)
                elu_and_bias(nc, ins, O1, X)
            h1T = B[:, 0:K * N].rearrange("p (k n) -> p k n", k=K)
            transpose_nodes(nc, "t3", O1, h1T, ident, ps)
            hx = by_node(A, D + 1).unsqueeze(2)
            with ExitStack() as s:
                al = s.enter_context(nc.sbuf_tensor("al2", [NT, T, 2], F32))
                gat_project(nc, "h2_", ins, ("L1_gnn_W2", "L1_gnn_a_src2", "L1_gnn_a_dst2"), h1T, hx, al, 1, MN, CT, ident, ps, False)
                gat_attention(nc, "g2_", ins, hx, al, 1, MN, CT, ident, ps, ald, X, True)
        QK = c.enter_context(nc.sbuf_tensor("QK", [128, 2 * K, N], F32))
        V = c.enter_context(nc.sbuf_tensor("V", [NT, T, D], F32))
        we = c.enter_context(nc.sbuf_tensor("we", [NT, T, E_ATT], F32))
        layernorm(nc, "ln3", X, V, stat, eps[:NT, 0:1])
        transpose_nodes(nc, "t4", V, XT, ident, ps)
        ffn_project(nc, ins, XT, QK, V, we, ident, ps, X)
        ffn_attention(nc, ins, QK, V, we, XT, X, ident, ps, out)


_INS = ['x', 'src', 'dst', 'edge_weight', 'L0_gnn_Wd', 'L0_gnn_bd', 'L0_gnn_Wu', 'L0_gnn_bu', 'L0_gnn_W1',
        'L0_gnn_b1', 'L0_gnn_W2', 'L0_gnn_b2', 'L0_ffn_ln_w', 'L0_ffn_w_router', 'L0_ffn_wi', 'L0_ffn_wo',
        'L1_gnn_W1', 'L1_gnn_a_src1', 'L1_gnn_a_dst1', 'L1_gnn_b1', 'L1_gnn_W2', 'L1_gnn_a_src2',
        'L1_gnn_a_dst2', 'L1_gnn_b2', 'L1_ffn_Wqk', 'L1_ffn_bqk', 'L1_ffn_Wv', 'L1_ffn_bv', 'L1_ffn_conv_w',
        'L1_ffn_conv_b', 'L1_ffn_glob', 'L1_ffn_pos_bias', 'L1_ffn_Wg1', 'L1_ffn_bg1', 'L1_ffn_Wg2',
        'L1_ffn_bg2', 'L1_ffn_Wp', 'L1_ffn_bp']


def kernel(**inputs):
    import numpy as _np
    import concourse.bacc as _bacc
    from concourse import mybir as _mybir
    from concourse.bass_utils import run_bass_kernel_spmd as _run

    nc = _bacc.Bacc("TRN2", target_bir_lowering=False, num_devices=1)
    arrays, args = {}, {}
    for name in _INS:
        a = _np.ascontiguousarray(inputs[name])
        arrays[f"in_{name}_dram"] = a
        args[name] = nc.dram_tensor(f"in_{name}_dram", a.shape, _mybir.dt.from_np(a.dtype), kind="ExternalInput").ap()
    out = nc.dram_tensor("out_0_dram", (1250, 768), _mybir.dt.from_np(_np.dtype("float32")), kind="ExternalOutput").ap()
    program(nc, args, out)
    r = _run(nc, [arrays], core_ids=[0])
    return r.results[0]["out_0_dram"]
```

```python
import math
from contextlib import ExitStack

import concourse.bass as bass
from concourse import mybir

F32 = mybir.dt.float32
BF16 = mybir.dt.bfloat16
I16 = mybir.dt.int16
I32 = mybir.dt.int32
ALU = mybir.AluOpType
ACT = mybir.ActivationFunctionType
AX = mybir.AxisListType

N, D = 1250, 768
NT, T = 125, 10
K = D // 128
EPC, NC_E, EROWS = 125, 330, 110
EG = NC_E // EROWS
WIN = 25
NWIN = N // WIN
BIG = 1e30
CHUNKS = [(0, 500), (500, 500), (1000, 250)]
BANKS = 8


def new_sem(nc, c, name):
    s = c.enter_context(nc.semaphore(name))
    c.callback(lambda: nc.sync.sem_clear(s))
    return s


def layernorm(nc, name, src, dst, stat, eps_col):
    with ExitStack() as c:
        stats_done = new_sem(nc, c, name + "_stats")
        std_done = new_sem(nc, c, name + "_std")
        rstd_done = new_sem(nc, c, name + "_rstd")
        bn = c.enter_context(nc.sbuf_tensor(name + "_bn", [NT, T, 2, 6], F32))
        block = c.enter_context(nc.Block(no_gpsimd_drain=True))
        half = D // 2

        @block.vector
        def _(dve):
            for t in range(T):
                for h in range(2):
                    nc.vector.bn_stats(bn[:, t, h, :], src[:, t, h * half:(h + 1) * half]).then_inc(stats_done, 1)
            for t in range(T):
                dve.wait_ge(stats_done, 2 * t + 2)
                nc.vector.bn_aggr(stat[:, t, 0:2], bn[:, t, :, :]).then_inc(stats_done, 1)
            dve.wait_ge(std_done, 1)
            nc.vector.reciprocal(stat[:, :, 2], stat[:, :, 2]).then_inc(rstd_done, 1)
            dve.wait_ge(rstd_done, 1)
            for t in range(T):
                nc.vector.tensor_scalar(dst[:, t, :], src[:, t, :], stat[:, t, 0:1], stat[:, t, 2:3],
                                        ALU.subtract, ALU.mult)

        @block.scalar
        def _(act):
            act.wait_ge(stats_done, 3 * T)
            nc.scalar.activation(stat[:, :, 2], stat[:, :, 1], ACT.Sqrt, bias=eps_col).then_inc(std_done, 1)


def transpose_nodes(nc, name, src, dst, ident, ps):
    with ExitStack() as c:
        turned = new_sem(nc, c, name + "_turned")
        by_act = new_sem(nc, c, name + "_by_act")
        by_dve = new_sem(nc, c, name + "_by_dve")
        block = c.enter_context(nc.Block(no_gpsimd_drain=True))
        groups = [(t, h) for t in range(T) for h in range(2)]

        @block.tensor
        def _(pe):
            for g, (t, h) in enumerate(groups):
                if g >= BANKS:
                    pe.wait_ge(by_dve if h else by_act, (g - BANKS) // 2 + 1)
                for j in range(3):
                    k = 3 * h + j
                    last = nc.tensor.transpose(ps[:, g % BANKS, j * NT:(j + 1) * NT],
                                               src[:, t, k * 128:(k + 1) * 128], ident[:NT, :NT])
                last.then_inc(turned, 1)

        def empty(g):
            t, h = groups[g]
            return (dst[:, 3 * h:3 * h + 3, t * NT:(t + 1) * NT],
                    ps[:, g % BANKS, 0:3 * NT].rearrange("p (j n) -> p j n", j=3))

        @block.scalar
        def _(act):
            for g in range(0, len(groups), 2):
                act.wait_ge(turned, g + 1)
                out, in_ = empty(g)
                nc.scalar.activation(out, in_, ACT.Copy).then_inc(by_act, 1)

        @block.vector
        def _(dve):
            for g in range(1, len(groups), 2):
                dve.wait_ge(turned, g + 1)
                out, in_ = empty(g)
                nc.vector.tensor_copy(out, in_).then_inc(by_dve, 1)


def dense_graph(nc, ins, cst, MT, CT, ps):
    GR = 4
    with ExitStack() as c:
        def sb(name, shape, dt=F32):
            return c.enter_context(nc.sbuf_tensor("g_" + name, shape, dt))

        def sem(name):
            return new_sem(nc, c, "g_" + name)

        ident = cst["ident"]
        raw = sb("raw", [EROWS, 2, EG, EPC], I32)
        row = sb("row", [EROWS, 3, EG, EPC])
        dstf = sb("dstf", [EROWS, EG, EPC])
        srcf = sb("srcf", [EROWS, EG, EPC])
        hi = sb("hi", [EROWS, 2, EG, EPC])
        edge = sb("edge", [EPC, NC_E + GR, 5])
        wrest = sb("wrest", [EPC, NC_E])
        mine = sb("mine", [EPC, GR, 5])
        key = sb("key", [EPC, GR])
        act_edges, pool_edges = sb("act_edges", [EPC, GR, 5]), sb("pool_edges", [EPC, GR, 5])
        wb = sb("wb", [EPC, NC_E], BF16)
        lo_iota = sb("lo_iota", [EPC, 128], I16)
        key_iota = sb("key_iota", [EPC, T, WIN], I16)
        win_start = sb("win_start", [EPC, NWIN])
        chunk_no = sb("chunk_no", [EROWS, EG])
        dlim = sb("dlim", [EROWS, 2, EG])
        meets = sb("meets", [EROWS, EG, NWIN])
        part = sb("part", [EROWS, EG, NWIN])
        marks = sb("marks", [EROWS, 2, EG, NWIN])
        mark = sb("mark", [EROWS, 2, NWIN])
        lim = sb("lim", [NWIN, 2])
        lim1 = sb("lim1", [1, 4, NWIN])
        lim_i = sb("lim_i", [1, 2, NWIN], I32)
        zero_b = sb("zero_b", [EPC, 512], BF16)
        A = sb("A", [EPC, GR, 4, 128], BF16)
        G = sb("G", [EPC, GR, T * WIN], BF16)

        loaded, iotas, v, lims = sem("loaded"), sem("iotas"), sem("v"), sem("lims")
        rows_ready, marks_ready = sem("rows_ready"), sem("marks_ready")
        cols_ready, lim_T, lim_T2, lim_sb = sem("cols_ready"), sem("lim_T"), sem("lim_T2"), sem("lim_sb")
        hot_one, hot_dve, hot_act, hot_pool, used, win_done, win_out = (
            sem("hot_one"), sem("hot_dve"), sem("hot_act"), sem("hot_pool"), sem("used"), sem("win_done"), sem("win_out"))
        copied, copied_act, copied_pool = sem("copied"), sem("copied_act"), sem("copied_pool")
        block = c.enter_context(nc.Block(no_gpsimd_drain=True))

        def limits(eng, w):
            first = eng.value_load(lim_i[0:1, 0, bass.ds(w, 1)], min_val=0, max_val=NC_E - 1)
            return first, eng.value_load(lim_i[0:1, 1, bass.ds(w, 1)], min_val=1, max_val=NC_E)

        def counter(eng, name):
            r = eng.alloc_register(name)
            eng.reg_mov(r, 0)
            return r

        def count(eng, r):
            return eng.snap(r, min_val=0, max_val=NWIN * (NC_E + GR))

        @block.sync
        def _(sp):
            for i, n in enumerate(("src", "dst")):
                sp.dma_start(raw[:, i, :, :], ins[n].rearrange("(j p e) -> p j e", p=EROWS, e=EPC)).then_inc(loaded, 16)
            sp.dma_start(row[:, 2, :, :], ins["edge_weight"].rearrange("(j p e) -> p j e", p=EROWS, e=EPC)).then_inc(loaded, 16)

        @block.gpsimd
        def _(pool):
            nc.gpsimd.memset(cst["ones"][:], 1.0).then_inc(iotas, 1)
            nc.gpsimd.iota(lo_iota[:], [[1, 128]], base=0, channel_multiplier=0).then_inc(iotas, 1)
            nc.gpsimd.iota(key_iota[:], [[N, T], [1, WIN]], base=0, channel_multiplier=0).then_inc(iotas, 1)
            nc.gpsimd.iota(win_start[:], [[WIN, NWIN]], base=0, channel_multiplier=0,
                           allow_small_or_imprecise_dtypes=True).then_inc(iotas, 1)
            nc.gpsimd.iota(chunk_no[:], [[EROWS, EG]], base=0, channel_multiplier=1,
                           allow_small_or_imprecise_dtypes=True).then_inc(iotas, 1)
            nc.gpsimd.memset(zero_b[:], 0.0).then_inc(iotas, 1)
            pool.wait_ge(iotas, 6)
            pool.wait_ge(lims, 1)
            begun = counter(pool, "begun_pool")
            with pool.Fori(0, NWIN) as w:
                first, end = limits(pool, w)
                with pool.Fori(first, end, GR) as ch:
                    at = count(pool, begun)
                    pool.wait_ge(hot_pool, at)
                    nc.gpsimd.tensor_copy(pool_edges[:], edge[:, bass.ds(ch, GR), :]).then_inc(copied_pool, GR)
                    pool.wait_ge(copied_pool, at + GR)
                    for g in range(0, GR, 2):
                        pool.wait_ge(used, at + (g + 1))
                        nc.gpsimd.tensor_scalar(A[:, g, 2, :], lo_iota[:], pool_edges[:, g, 0:1], pool_edges[:, g, 4:5],
                                                ALU.is_equal, ALU.mult).then_inc(hot_pool, 2)
                    pool.reg_add(begun, begun, GR)

        @block.vector
        def _(dve):
            n = [0]

            def link(ins_):
                n[0] += 1
                ins_.then_inc(v, 1)
                dve.wait_ge(v, n[0])

            dve.wait_ge(loaded, 48)
            dve.wait_ge(iotas, 6)
            nc.vector.tensor_copy(srcf[:], raw[:, 0])
            link(nc.vector.tensor_copy(dstf[:], raw[:, 1]))
            link(nc.vector.tensor_scalar(hi[:, 0], srcf[:], float(NT), None, ALU.is_ge))
            for t in range(2, T):
                link(nc.vector.scalar_tensor_tensor(hi[:, (t + 1) % 2], srcf[:], float(NT * t), hi[:, t % 2],
                                                    ALU.is_ge, ALU.add))
            tile = hi[:, 0]
            nc.vector.scalar_tensor_tensor(row[:, 0], tile, -float(NT), srcf[:], ALU.mult, ALU.add)
            nc.vector.tensor_reduce(dlim[:, 0], dstf[:], AX.X, ALU.min)
            nc.vector.tensor_reduce(dlim[:, 1], dstf[:], AX.X, ALU.max)
            nc.vector.scalar_tensor_tensor(row[:, 1], tile, float(N), dstf[:], ALU.mult, ALU.add).then_inc(rows_ready, 1)
            dve.wait_ge(rows_ready, 1)
            for j in range(EG):
                nc.vector.tensor_scalar(part[:, j], win_start[:EROWS], float(WIN - 1), dlim[:, 0, j:j + 1],
                                        ALU.add, ALU.is_ge)
            for j in range(EG):
                link(nc.vector.tensor_scalar(meets[:, j], win_start[:EROWS], dlim[:, 1, j:j + 1], None, ALU.is_le))
            link(nc.vector.tensor_tensor(meets[:], meets[:], part[:], ALU.mult))
            for j in range(EG):
                link(nc.vector.tensor_scalar(marks[:, 1, j], meets[:, j], chunk_no[:, j:j + 1], None, ALU.mult))
            link(nc.vector.scalar_tensor_tensor(marks[:, 0], meets[:], float(NC_E), marks[:, 1], ALU.mult, ALU.subtract))
            link(nc.vector.tensor_tensor(marks[:, 1], marks[:, 1], meets[:], ALU.add))
            link(nc.vector.tensor_tensor(mark[:], marks[:, :, 0], marks[:, :, 1], ALU.max))
            nc.vector.tensor_tensor(mark[:], mark[:], marks[:, :, 2], ALU.max).then_inc(marks_ready, 1)
            dve.wait_ge(cols_ready, 1)
            nc.vector.memset(edge[:, NC_E:, :], -1.0)
            for i in range(2):
                nc.vector.tensor_copy(edge[:, 0:NC_E, i], ps[:EPC, i, 0:NC_E])
            link(nc.vector.tensor_copy(wrest[:], ps[:EPC, 2, 0:NC_E]))
            link(nc.vector.tensor_copy(wb[:], wrest[:]))
            link(nc.vector.tensor_copy(edge[:, 0:NC_E, 2], wb[:]))
            link(nc.vector.tensor_tensor(wrest[:], wrest[:], edge[:, 0:NC_E, 2], ALU.subtract))
            link(nc.vector.tensor_copy(wb[:], wrest[:]))
            link(nc.vector.tensor_copy(edge[:, 0:NC_E, 3], wb[:]))
            link(nc.vector.tensor_tensor(edge[:, 0:NC_E, 4], wrest[:], edge[:, 0:NC_E, 3], ALU.subtract))
            dve.wait_ge(lim_T, 1)
            for i in range(2):
                nc.vector.tensor_reduce(lim[:, i:i + 1], ps[:NWIN, 3, i * 128:i * 128 + EROWS], AX.X, ALU.max).then_inc(lim_sb, 1)
            dve.wait_ge(lim_T2, 1)
            link(nc.vector.tensor_copy(lim1[:, 2:4].rearrange("p a w -> p (a w)"),
                                       ps[0:1, 4, 0:2 * NWIN]))
            link(nc.vector.tensor_scalar(lim1[:, 0], lim1[:, 2], -1.0, float(NC_E), ALU.mult, ALU.add))
            link(nc.vector.tensor_scalar(lim1[:, 0], lim1[:, 0], float(NC_E - 1), None, ALU.min))
            link(nc.vector.scalar_tensor_tensor(lim1[:, 1], lim1[:, 0], 1.0, lim1[:, 3], ALU.add, ALU.max))
            nc.vector.tensor_copy(lim_i[:], lim1[:, 0:2]).then_inc(lims, 1)
            dve.wait_ge(lims, 1)
            begun = counter(dve, "begun_dve")
            with dve.Fori(0, NWIN) as w:
                first, end = limits(dve, w)
                with dve.Fori(first, end, GR) as ch:
                    at = count(dve, begun)
                    dve.wait_ge(hot_dve, at)
                    nc.vector.tensor_copy(mine[:], edge[:, bass.ds(ch, GR), :])
                    nc.vector.tensor_scalar(key[:], edge[:, bass.ds(ch, GR), 1], win_start[:, bass.ds(w, 1)], None,
                                            ALU.subtract).then_inc(copied, GR)
                    dve.wait_ge(copied, at + GR)
                    for g in range(GR):
                        dve.wait_ge(used, at + (g + 1))
                        nc.vector.tensor_scalar(A[:, g, 3, :], lo_iota[:], mine[:, g, 0:1], None,
                                                ALU.is_equal).then_inc(hot_one, 1)
                        nc.vector.tensor_scalar(G[:, g, :], key_iota[:].rearrange("p a w -> p (a w)"), key[:, g:g + 1],
                                                None, ALU.is_equal)
                        nc.vector.tensor_scalar(A[:, g, 0, :], lo_iota[:], mine[:, g, 0:1], mine[:, g, 2:3],
                                                ALU.is_equal, ALU.mult).then_inc(hot_dve, 1)
                    dve.reg_add(begun, begun, GR)

        @block.tensor
        def _(pe):
            pe.wait_ge(rows_ready, 1)
            pe.wait_ge(loaded, 48)
            for i in range(3):
                for j in range(EG):
                    last = nc.tensor.transpose(ps[:EPC, i, j * EROWS:(j + 1) * EROWS], row[:, i, j, :], ident[:EROWS, :EROWS])
            last.then_inc(cols_ready, 1)
            pe.wait_ge(marks_ready, 1)
            for i in range(2):
                last = nc.tensor.transpose(ps[:NWIN, 3, i * 128:i * 128 + EROWS], mark[:, i], ident[:EROWS, :EROWS])
            last.then_inc(lim_T, 1)
            pe.wait_ge(lim_sb, 2)
            for i in range(2):
                last = nc.tensor.transpose(ps[0:1, 4, i * NWIN:(i + 1) * NWIN], lim[:, i:i + 1], ident[:NWIN, :NWIN])
            last.then_inc(lim_T2, 1)
            pe.wait_ge(lims, 1)
            pe.wait_ge(iotas, 6)
            pe.sem_inc(used, GR)
            begun = counter(pe, "begun_pe")
            with pe.Fori(0, NWIN // 2) as w2:
                for half in range(2):
                    w = w2 * 2 + half
                    sums = ps[:, 5 + half, :]
                    first, end = limits(pe, w)
                    pe.wait_ge(win_out, w + 1)
                    nc.tensor.matmul(sums, zero_b[:, 0:128], zero_b[:], start=True, stop=False)
                    with pe.Fori(first, end, GR):
                        at = count(pe, begun)
                        for g in range(GR):
                            pe.wait_ge(hot_dve, at + (g + 1))
                            pe.wait_ge(hot_act, at + (g + 1))
                            if g % 2 == 0:
                                pe.wait_ge(hot_pool, at + (g + 2))
                            for i in range(4):
                                off = 256 * (i == 3)
                                last = nc.tensor.matmul(sums[:, off:off + T * WIN], A[:, g, i, :], G[:, g, :],
                                                        start=False, stop=False, skip_group_check=True)
                            last.then_inc(used, 1)
                        pe.reg_add(begun, begun, GR)
                    nc.tensor.matmul(sums, zero_b[:, 0:128], zero_b[:], start=False, stop=True).then_inc(win_done, 1)

        @block.scalar
        def _(act):
            act.sem_inc(win_out, 2)
            act.wait_ge(lims, 1)
            begun = counter(act, "begun_act")

            def second_parts(w):
                first, end = limits(act, w)
                with act.Fori(first, end, GR) as ch:
                    at = count(act, begun)
                    act.wait_ge(hot_act, at)
                    nc.scalar.activation(act_edges[:, :, 3:5], edge[:, bass.ds(ch, GR), 3:5], ACT.Copy).then_inc(copied_act, GR)
                    act.wait_ge(copied_act, at + GR)
                    for g in range(GR):
                        act.wait_ge(hot_one, at + (g + 1))
                        for part in (1, 2)[:1 + g % 2]:
                            last = nc.scalar.activation(A[:, g, part, :], A[:, g, 3, :], ACT.Copy,
                                                        scale=act_edges[:, g, part + 2:part + 3])
                        last.then_inc(hot_act, 1)
                    act.reg_add(begun, begun, GR)

            def copy_out(w, bank):
                act.wait_ge(win_done, w + 1)
                for i, dense in enumerate((MT, CT)):
                    last = nc.scalar.activation(dense[:, :, bass.ds(w * WIN, WIN)],
                                                ps[:NT, bank, 256 * i:256 * i + T * WIN].rearrange("p (a w) -> p a w", a=T), ACT.Copy)
                last.then_inc(win_out, 1)

            second_parts(0)
            with act.Fori(0, NWIN // 2 - 1) as w2:
                for half in range(2):
                    second_parts(w2 * 2 + half + 1)
                    copy_out(w2 * 2 + half, 5 + half)
            second_parts(NWIN - 1)
            copy_out(NWIN - 2, 5)
            copy_out(NWIN - 1, 6)


def low_rank_and_gcn(nc, ins, XT, MT, X, W, stat, ones, ps):
    H, R = 256, 24
    with ExitStack() as c:
        def sb(name, shape, dt=F32):
            return c.enter_context(nc.sbuf_tensor("c_" + name, shape, dt))

        def sem(name):
            return new_sem(nc, c, "c_" + name)

        ident = W["ident"]
        wd, wu, bd, bu = sb("wd", [128, K, R]), sb("wu", [R, D]), sb("bd", [R, 1]), sb("bu", [128, K])
        w1, w2 = sb("w1", [128, K, H]), sb("w2", [128, 2, D])
        b1, b2 = sb("b1", [NT, H]), sb("b2", [NT, D])
        RT = sb("RT", [R, N])
        hw = sb("hw", [NT, T, H])
        aggT = sb("aggT", [128, 2, N])
        tmp = sb("tmp", [NT, 2, H])
        dinv = stat[:, :, 3]
        hw2 = XT[:NT, :, :].rearrange("p k n -> p (k n)")[:, 0:T * H].rearrange("p (t h) -> p t h", t=T)
        loaded, self_loop, deg_done, std_done, dinv_done = (
            sem("loaded"), sem("self_loop"), sem("deg_done"), sem("std_done"), sem("dinv_done"))
        low_done, low_out, up_done, up_out = sem("low_done"), sem("low_out"), sem("up_done"), sem("up_out")
        hw_done, hw_out, agg_done, agg_out, tmp_done = (
            sem("hw_done"), sem("hw_out"), sem("agg_done"), sem("agg_out"), sem("tmp_done"))
        aggT_done, aggT_out, y_done, y_out, bias_done = (
            sem("aggT_done"), sem("aggT_out"), sem("y_done"), sem("y_out"), sem("bias_done"))
        block = c.enter_context(nc.Block(no_gpsimd_drain=True))

        @block.sync
        def _(sp):
            def load(dst, src, small=False):
                sp.dma_start(dst, src, allow_slow_non_contiguous=small).then_inc(loaded, 16)
            load(wd[:], ins["L0_gnn_Wd"].rearrange("(k p) r -> p k r", p=128))
            load(wu[:], ins["L0_gnn_Wu"])
            load(bd[:], ins["L0_gnn_bd"].rearrange("(r a) -> r a", a=1), True)
            load(bu[:], ins["L0_gnn_bu"].rearrange("(k p) -> p k", p=128), True)
            load(w1[:], ins["L0_gnn_W1"].rearrange("(k p) h -> p k h", p=128))
            load(w2[:], ins["L0_gnn_W2"].rearrange("(k p) d -> p k d", p=128))
            load(b1[:], ins["L0_gnn_b1"].partition_broadcast(NT))
            load(b2[:], ins["L0_gnn_b2"].partition_broadcast(NT))

        @block.gpsimd
        def _(pool):
            pool.wait_ge(loaded, 128)
            for t in range(T):
                nc.gpsimd.tensor_tensor(X[:, t, :], X[:, t, :], b2[:], ALU.add).then_inc(bias_done, 1)
            pool.wait_ge(bias_done, T)

        @block.tensor
        def _(pe):
            pe.wait_ge(self_loop, 1)
            for t in range(T):
                for s in range(T):
                    last = nc.tensor.matmul(ps[:NT, 7, t:t + 1], MT[:, s, t * NT:(t + 1) * NT], ones[:NT, 0:1],
                                            start=(s == 0), stop=(s == T - 1))
            last.then_inc(deg_done, 1)
            pe.wait_ge(loaded, 128)
            for g, (n0, nn) in enumerate(CHUNKS):
                for k in range(K):
                    last = nc.tensor.matmul(ps[:R, g, 0:nn], wd[:, k, :], XT[:, k, n0:n0 + nn],
                                            start=(k == 0), stop=(k == K - 1))
                last.then_inc(low_done, 1)
            for g, (n0, nn) in enumerate(CHUNKS):
                pe.wait_ge(low_out, g + 1)
                for m in range(K):
                    i = g * K + m
                    if i >= 4:
                        pe.wait_ge(up_out, i - 3)
                    nc.tensor.matmul(ps[:, 3 + i % 4, 0:nn], wu[:, m * 128:(m + 1) * 128], RT[:, n0:n0 + nn],
                                     start=True, stop=True).then_inc(up_done, 1)
            pe.wait_ge(up_out, 3 * K)
            for t in range(T):
                if t >= 4:
                    pe.wait_ge(hw_out, t - 3)
                for k in range(K):
                    last = nc.tensor.matmul(ps[:NT, t % 4, 0:H], XT[:, k, t * NT:(t + 1) * NT], w1[:, k, :],
                                            start=(k == 0), stop=(k == K - 1))
                last.then_inc(hw_done, 1)
            pe.wait_ge(hw_out, T)
            for t in range(T):
                if t >= 4:
                    pe.wait_ge(tmp_done, t - 3)
                for s in range(T):
                    last = nc.tensor.matmul(ps[:NT, 4 + t % 4, 0:H], MT[:, s, t * NT:(t + 1) * NT], hw[:, s, :],
                                            start=(s == 0), stop=(s == T - 1))
                last.then_inc(agg_done, 1)
            pe.wait_ge(agg_out, T)
            for m in range(2):
                for g, (n0, nn) in enumerate(CHUNKS):
                    i = m * 3 + g
                    if i >= 4:
                        pe.wait_ge(aggT_out, i - 3)
                    for s in range(T):
                        last = nc.tensor.matmul(ps[:, i % 4, 0:nn], hw2[:, s, m * 128:(m + 1) * 128],
                                                MT[:, s, n0:n0 + nn], start=(s == 0), stop=(s == T - 1))
                    last.then_inc(aggT_done, 1)
            pe.wait_ge(aggT_out, 6)
            for t in range(T):
                for h in range(2):
                    i = 2 * t + h
                    if i >= 4:
                        pe.wait_ge(y_out, i - 3)
                    for k in range(2):
                        last = nc.tensor.matmul(ps[:NT, 4 + i % 4, 0:384], aggT[:, k, t * NT:(t + 1) * NT],
                                                w2[:, k, h * 384:(h + 1) * 384], start=(k == 0), stop=(k == 1))
                    last.then_inc(y_done, 1)

        @block.scalar
        def _(act):
            act.wait_ge(deg_done, 1)
            nc.scalar.activation(dinv, ps[:NT, 7, 0:T], ACT.Sqrt).then_inc(std_done, 1)
            act.wait_ge(loaded, 128)
            for g, (n0, nn) in enumerate(CHUNKS):
                act.wait_ge(low_done, g + 1)
                nc.scalar.activation(RT[:, n0:n0 + nn], ps[:R, g, 0:nn], ACT.Relu, bias=bd[:, 0:1]).then_inc(low_out, 1)
            act.wait_ge(dinv_done, 1)
            for t in range(T):
                act.wait_ge(hw_done, t + 1)
                nc.scalar.activation(hw[:, t, :], ps[:NT, t % 4, 0:H], ACT.Copy, scale=dinv[:, t:t + 1]).then_inc(hw_out, 1)
            for m in range(2):
                for g, (n0, nn) in enumerate(CHUNKS):
                    act.wait_ge(aggT_done, m * 3 + g + 1)
                    nc.scalar.activation(aggT[:, m, n0:n0 + nn], ps[:, (m * 3 + g) % 4, 0:nn], ACT.Copy).then_inc(aggT_out, 1)

        @block.vector
        def _(dve):
            for t in range(T):
                last = nc.vector.tensor_tensor(MT[:, t, t * NT:(t + 1) * NT], MT[:, t, t * NT:(t + 1) * NT],
                                               ident[:NT, :NT], ALU.add)
            last.then_inc(self_loop, 1)
            dve.wait_ge(std_done, 1)
            nc.vector.reciprocal(dinv, dinv).then_inc(dinv_done, 1)
            for g, (n0, nn) in enumerate(CHUNKS):
                for m in range(K):
                    i = g * K + m
                    dve.wait_ge(up_done, i + 1)
                    nc.vector.scalar_tensor_tensor(XT[:, m, n0:n0 + nn], ps[:, 3 + i % 4, 0:nn], bu[:, m:m + 1],
                                                   XT[:, m, n0:n0 + nn], ALU.add, ALU.add).then_inc(up_out, 1)
            dve.wait_ge(dinv_done, 1)
            dve.wait_ge(hw_done, T)
            for t in range(T):
                dve.wait_ge(agg_done, t + 1)
                nc.vector.scalar_tensor_tensor(tmp[:, t % 2, :], ps[:NT, 4 + t % 4, 0:H], dinv[:, t:t + 1], b1[:],
                                               ALU.mult, ALU.add).then_inc(tmp_done, 1)
                dve.wait_ge(tmp_done, t + 1)
                nc.vector.tensor_scalar(hw2[:, t, :], tmp[:, t % 2, :], 0.0, dinv[:, t:t + 1],
                                        ALU.max, ALU.mult).then_inc(agg_out, 1)
            dve.wait_ge(bias_done, T)
            for t in range(T):
                for h in range(2):
                    i = 2 * t + h
                    dve.wait_ge(y_done, i + 1)
                    nc.vector.scalar_tensor_tensor(X[:, t, h * 384:(h + 1) * 384], ps[:NT, 4 + i % 4, 0:384],
                                                   dinv[:, t:t + 1], X[:, t, h * 384:(h + 1) * 384],
                                                   ALU.mult, ALU.add).then_inc(y_out, 1)


E_MOE, CAP, FF = 16, 64, 384


def route(nc, ins, W, X, XN, XT, stat, eps6, moe, ps, normd):
    with ExitStack() as c:
        def sb(name, shape, dt=F32):
            return c.enter_context(nc.sbuf_tensor("r_" + name, shape, dt))

        def sem(name):
            return new_sem(nc, c, "r_" + name)

        ident, ones = W["ident"], W["ones"]
        lnw = sb("lnw", [NT, D])
        wr = sb("wr", [128, K, E_MOE])
        sq = sb("sq", [NT, D])
        ms = sb("ms", [NT, T])
        lg, oh, tmp, base = (sb(x, [NT, T, E_MOE]) for x in ("lg", "oh", "tmp", "base"))
        mx, p1, keep, sc = (sb(x, [NT, T]) for x in ("mx", "p1", "keep", "sc"))
        down = sb("down", [NT, E_MOE])
        slot0 = sb("slot0", [NT, E_MOE])
        rank = sb("rank", [NT, CAP])
        node = sb("node", [NT, T])
        tri = sb("tri", [NT, NT])
        at_rank = sb("at_rank", [NT, T, 2, CAP])
        tok = sb("tok", [128, E_MOE])
        loaded, made, sq_done, v, norm_done, added, stored = (
            sem("loaded"), sem("made"), sem("sq_done"), sem("v"), sem("norm_done"), sem("added"), sem("stored"))
        normed, t_done, t_act, t_dve, lg_done, exp_in, exp_out, oh_done, cum_done, inv_in, inv_done = (
            sem("normed"), sem("t_done"), sem("t_act"), sem("t_dve"), sem("lg_done"), sem("exp_in"),
            sem("exp_out"), sem("oh_done"), sem("cum_done"), sem("inv_in"), sem("inv_done"))
        rms_in, rms_out = sem("rms_in"), sem("rms_out")
        block = c.enter_context(nc.Block(no_gpsimd_drain=True))
        rp, slot_i, tok_i, ka, kb = moe["rp"], moe["slot"], moe["tok"], moe["ka"], moe["kb"]

        @block.sync
        def _(sp):
            sp.dma_start(lnw[:], ins["L0_ffn_ln_w"].partition_broadcast(NT)).then_inc(loaded, 16)
            sp.dma_start(wr[:], ins["L0_ffn_w_router"].rearrange("(k p) e -> p k e", p=128)).then_inc(loaded, 16)
            sp.wait_ge(norm_done, T)
            sp.dma_start(normd.rearrange("(t p) d -> p t d", p=NT), XN[:]).then_inc(stored, 16)
            sp.wait_ge(stored, 16)

        @block.gpsimd
        def _(pool):
            nc.gpsimd.iota(down[:], [[-1, E_MOE]], base=E_MOE, channel_multiplier=0, allow_small_or_imprecise_dtypes=True)
            nc.gpsimd.iota(slot0[:], [[CAP, E_MOE]], base=-1, channel_multiplier=0, allow_small_or_imprecise_dtypes=True)
            nc.gpsimd.iota(rank[:], [[1, CAP]], base=1, channel_multiplier=0, allow_small_or_imprecise_dtypes=True)
            nc.gpsimd.iota(node[:], [[NT, T]], base=0, channel_multiplier=1, allow_small_or_imprecise_dtypes=True)
            nc.gpsimd.memset(tri[:], 1.0).then_inc(made, 1)
            pool.wait_ge(made, 1)
            nc.gpsimd.affine_select(out=tri[:], in_=tri[:], compare_op=ALU.is_ge, fill=0.0, base=0,
                                    pattern=[[1, NT]], channel_multiplier=-1).then_inc(made, 1)
            for t in range(T):
                nc.gpsimd.tensor_tensor(X[:, t, :], X[:, t, :], XN[:, t, :], ALU.add).then_inc(added, 1)
            pool.wait_ge(added, T)

        @block.scalar
        def _(act):
            for t in range(T):
                nc.scalar.activation(sq[:], XN[:, t, :], ACT.Square, accum_out=ms[:, t:t + 1]).then_inc(sq_done, 1)
                act.wait_ge(sq_done, t + 1)
            nc.scalar.activation(mx[:], ms[:], ACT.Sqrt, scale=1.0 / D, bias=eps6).then_inc(rms_in, 1)
            for g in range(0, 2 * T, 2):
                act.wait_ge(t_done, g + 1)
                nc.scalar.activation(XT[:, 0:3, (g // 2) * NT:(g // 2 + 1) * NT],
                                     ps[:, g % 6, 0:3 * NT].rearrange("p (j n) -> p j n", j=3), ACT.Copy).then_inc(t_act, 1)
            act.wait_ge(exp_in, 1)
            nc.scalar.activation(tmp[:], lg[:], ACT.Exp).then_inc(exp_out, 1)

        @block.tensor
        def _(pe):
            for t in range(T):
                pe.wait_ge(norm_done, t + 1)
                for h in range(2):
                    g = 2 * t + h
                    if g >= 6:
                        pe.wait_ge(t_dve if h else t_act, (g - 6) // 2 + 1)
                    for j in range(3):
                        k = 3 * h + j
                        last = nc.tensor.transpose(ps[:, g % 6, j * NT:(j + 1) * NT],
                                                   XN[:, t, k * 128:(k + 1) * 128], ident[:NT, :NT])
                    last.then_inc(t_done, 1)
            pe.wait_ge(loaded, 32)
            for t in range(T):
                pe.wait_ge(t_act, t + 1)
                pe.wait_ge(t_dve, t + 1)
                for k in range(K):
                    last = nc.tensor.matmul(ps[:NT, 6, t * E_MOE:(t + 1) * E_MOE], XT[:, k, t * NT:(t + 1) * NT],
                                            wr[:, k, :], start=(k == 0), stop=(k == K - 1))
            last.then_inc(lg_done, 1)
            pe.wait_ge(made, 2)
            pe.wait_ge(oh_done, 1)
            flat = oh[:].rearrange("p t e -> p (t e)")
            nc.tensor.matmul(ps[:NT, 7, 0:T * E_MOE], tri[:], flat, start=True, stop=True)
            nc.tensor.matmul(ps[:NT, 0, 0:T * E_MOE], ones[:NT, :NT], flat, start=True, stop=True).then_inc(cum_done, 1)
            pe.wait_ge(inv_in, 1)
            for t in range(T):
                last = nc.tensor.matmul(ps[:, 1, 0:E_MOE], at_rank[:, t, :, :].rearrange("p a c -> p (a c)"), oh[:, t, :],
                                        start=(t == 0), stop=(t == T - 1))
            last.then_inc(inv_done, 1)

        @block.vector
        def _(dve):
            n = [0]

            def link(ins_):
                n[0] += 1
                ins_.then_inc(v, 1)
                dve.wait_ge(v, n[0])

            def wide(a, m=E_MOE):
                return a.unsqueeze(2).broadcast_to([NT, T, m])

            def each(a):
                return a.unsqueeze(1).broadcast_to([NT, T, E_MOE])

            dve.wait_ge(rms_in, 1)
            dve.wait_ge(loaded, 32)
            link(nc.vector.reciprocal(ms[:], mx[:]))
            for t in range(T):
                dve.wait_ge(added, t + 1)
                nc.vector.scalar_tensor_tensor(XN[:, t, :], XN[:, t, :], ms[:, t:t + 1], lnw[:], ALU.mult,
                                               ALU.mult).then_inc(norm_done, 1)
            for g in range(1, 2 * T, 2):
                dve.wait_ge(t_done, g + 1)
                nc.vector.tensor_copy(XT[:, 3:6, (g // 2) * NT:(g // 2 + 1) * NT],
                                      ps[:, g % 6, 0:3 * NT].rearrange("p (j n) -> p j n", j=3)).then_inc(t_dve, 1)
            dve.wait_ge(lg_done, 1)
            link(nc.vector.tensor_copy(lg[:], ps[:NT, 6, 0:T * E_MOE].rearrange("p (t e) -> p t e", t=T)))
            link(nc.vector.tensor_reduce(mx[:], lg[:], AX.X, ALU.max))
            link(nc.vector.tensor_tensor(oh[:], lg[:], wide(mx[:]), ALU.is_ge))
            nc.vector.tensor_tensor(lg[:], lg[:], wide(mx[:]), ALU.subtract).then_inc(exp_in, 1)
            dve.wait_ge(made, 2)
            link(nc.vector.tensor_tensor(oh[:], oh[:], each(down[:]), ALU.mult))
            link(nc.vector.tensor_reduce(sc[:], oh[:], AX.X, ALU.max))
            nc.vector.tensor_tensor(oh[:], each(down[:]), wide(sc[:]), ALU.is_equal).then_inc(oh_done, 1)
            dve.wait_ge(exp_out, 1)
            link(nc.vector.tensor_reduce(rp[:], tmp[:], AX.X, ALU.add))
            link(nc.vector.reciprocal(rp[:], rp[:]))
            dve.wait_ge(cum_done, 1)
            link(nc.vector.memset(base[:, 0, :], 0.0))
            for t in range(1, T):
                link(nc.vector.tensor_tensor(base[:, t, :], base[:, t - 1, :],
                                             ps[:NT, 0, (t - 1) * E_MOE:t * E_MOE], ALU.add))
            link(nc.vector.tensor_tensor(base[:], base[:],
                                         ps[:NT, 7, 0:T * E_MOE].rearrange("p (t e) -> p t e", t=T), ALU.add))
            link(nc.vector.tensor_tensor(base[:], base[:], oh[:], ALU.mult))
            link(nc.vector.tensor_reduce(p1[:], base[:], AX.X, ALU.add))
            link(nc.vector.tensor_scalar(keep[:], p1[:], float(CAP), None, ALU.is_le))
            link(nc.vector.tensor_tensor(tmp[:], oh[:], each(slot0[:]), ALU.mult))
            link(nc.vector.tensor_reduce(sc[:], tmp[:], AX.X, ALU.add))
            link(nc.vector.tensor_tensor(sc[:], sc[:], p1[:], ALU.add))
            link(nc.vector.tensor_tensor(sc[:], sc[:], keep[:], ALU.mult))
            nc.vector.tensor_copy(slot_i[:], sc[:])
            link(nc.vector.tensor_tensor(ka[:], rp[:], keep[:], ALU.mult))
            nc.vector.tensor_tensor(kb[:], rp[:], ka[:], ALU.subtract)
            link(nc.vector.tensor_tensor(mx[:], node[:], keep[:], ALU.mult))
            link(nc.vector.tensor_tensor(oh[:], oh[:], wide(mx[:]), ALU.mult))
            for h in range(2):
                last = nc.vector.tensor_tensor(at_rank[:, :, h, :], rank[:].unsqueeze(1).broadcast_to([NT, T, CAP]),
                                               wide(p1[:], CAP), ALU.is_equal)
            last.then_inc(inv_in, 1)
            dve.wait_ge(inv_done, 1)
            pair = ps[:, 1, 0:E_MOE].rearrange("p (q a) -> p q a", a=2)
            nc.vector.tensor_copy(tok_i[0:CAP, :], pair[0:CAP, :, 0])
            nc.vector.tensor_copy(tok_i[CAP:128, :], pair[CAP:128, :, 1])


def experts(nc, ins, W, X, XN, XT, moe, ps, normd, eo):
    RING = 3
    with ExitStack() as c:
        def sb(name, shape, dt=F32):
            return c.enter_context(nc.sbuf_tensor("e_" + name, shape, dt))

        def sem(name):
            return new_sem(nc, c, "e_" + name)

        ident = W["ident"]
        wi = sb("wi", [128, RING, K, FF])
        wo = sb("wo", [128, RING, 3, D])
        room = XT[:].rearrange("p k n -> p (k n)")
        xg = room[:, 0:2 * D].rearrange("p (a d) -> p a d", a=2)
        xgT = room[:, 2 * D:4 * D].rearrange("p (a k n) -> p a k n", a=2, k=K)
        y = room[:CAP, 4 * D:6 * D].rearrange("p (a d) -> p a d", a=2)
        back = room[:NT, 6 * D:8 * D].rearrange("p (a d) -> p a d", a=2)
        hT = room[:, 8 * D:8 * D + 6 * CAP].rearrange("p (a f c) -> p a f c", a=2, f=3)
        wl = [sem(f"wl{i}") for i in range(RING)]
        gl = [sem(f"gl{i}") for i in range(2)]
        st = [sem(f"st{i}") for i in range(2)]
        bl = [sem(f"bl{i}") for i in range(2)]
        turned, xgT_out, up_done, up_out, dn_done, dn_out, comb, comb1 = (
            sem("turned"), sem("xgT_out"), sem("up_done"), sem("up_out"), sem("dn_done"),
            sem("dn_out"), sem("comb"), sem("comb1"))
        block = c.enter_context(nc.Block(no_gpsimd_drain=True))
        slot_i, tok_i, ka, kb = moe["slot"], moe["tok"], moe["ka"], moe["kb"]
        PAIRS = E_MOE // 2

        @block.sync
        def _(sp):
            for e in range(E_MOE):
                if e >= RING:
                    sp.wait_ge(dn_done, 2 * (e - RING + 1))
                sp.dma_start(wi[:, e % RING], ins["L0_ffn_wi"][e].rearrange("(k p) f -> p k f", p=128)).then_inc(wl[e % RING], 16)
                sp.dma_start(wo[:, e % RING], ins["L0_ffn_wo"][e].rearrange("(k p) d -> p k d", p=128)).then_inc(wl[e % RING], 16)

        @block.gpsimd
        def _(pool):
            for q in range(PAIRS):
                if q >= 2:
                    pool.wait_ge(turned, 2 * (q - 1))
                nc.gpsimd.indirect_dma_start(out=xg[:, q % 2, :], out_offset=None, in_=normd[:, :],
                                             in_offset=bass.IndirectOffsetOnAxis(ap=tok_i[:, q:q + 1], axis=0)).then_inc(gl[q % 2], 16)
            for i in range(2):
                pool.wait_ge(st[i], 16 * PAIRS)
            for t in range(T):
                if t >= 2:
                    pool.wait_ge(comb1, t - 1)
                nc.gpsimd.indirect_dma_start(out=back[:, t % 2, :], out_offset=None, in_=eo[:, :],
                                             in_offset=bass.IndirectOffsetOnAxis(ap=slot_i[:, t:t + 1], axis=0)).then_inc(bl[t % 2], 16)

        @block.tensor
        def _(pe):
            for q in range(PAIRS):
                pe.wait_ge(gl[q % 2], 16 * (q // 2 + 1))
                if q >= 1:
                    pe.wait_ge(xgT_out, 2 * q)
                for h in range(2):
                    for j in range(3):
                        k = 3 * h + j
                        last = nc.tensor.transpose(ps[:, h, j * 128:(j + 1) * 128], xg[:, q % 2, k * 128:(k + 1) * 128], ident[:])
                    last.then_inc(turned, 1)
                pe.wait_ge(xgT_out, 2 * q + 2)
                for i in range(2):
                    e = 2 * q + i
                    pe.wait_ge(wl[e % RING], 32 * (e // RING + 1))
                    if e >= 2:
                        pe.wait_ge(up_out, e - 1)
                    for f in range(3):
                        for k in range(K):
                            last = nc.tensor.matmul(ps[:, 2 + i, f * CAP:(f + 1) * CAP], wi[:, e % RING, k, f * 128:(f + 1) * 128],
                                                    xgT[:, q % 2, k, i * CAP:(i + 1) * CAP], start=(k == 0), stop=(k == K - 1))
                    last.then_inc(up_done, 1)
                    pe.wait_ge(up_out, e + 1)
                    for h in range(2):
                        if e >= 2:
                            pe.wait_ge(dn_out, 2 * (e - 2) + h + 1)
                        for f in range(3):
                            last = nc.tensor.matmul(ps[:CAP, 4 + 2 * i + h, 0:384], hT[:, i, f, :],
                                                    wo[:, e % RING, f, h * 384:(h + 1) * 384], start=(f == 0), stop=(f == 2))
                        last.then_inc(dn_done, 1)

        @block.scalar
        def _(act):
            for q in range(PAIRS):
                act.wait_ge(turned, 2 * q + 1)
                nc.scalar.activation(xgT[:, q % 2, 0:3, :], ps[:, 0, 0:384].rearrange("p (j n) -> p j n", j=3), ACT.Copy).then_inc(xgT_out, 1)
                act.wait_ge(turned, 2 * q + 2)
                nc.scalar.activation(xgT[:, q % 2, 3:6, :], ps[:, 1, 0:384].rearrange("p (j n) -> p j n", j=3), ACT.Copy).then_inc(xgT_out, 1)
                for i in range(2):
                    e = 2 * q + i
                    act.wait_ge(up_done, e + 1)
                    if e >= 2:
                        act.wait_ge(dn_done, 2 * (e - 1))
                    nc.scalar.activation(hT[:, i, :, :].rearrange("p f c -> p (f c)"), ps[:, 2 + i, 0:3 * CAP], ACT.Relu).then_inc(up_out, 1)
                    act.wait_ge(dn_out, 2 * (e + 1))
                    act.dma_start(eo[e * CAP:(e + 1) * CAP, :], y[:, i, :]).then_inc(st[i], 16)

        @block.vector
        def _(dve):
            for e in range(E_MOE):
                i = e % 2
                if e >= 2:
                    dve.wait_ge(st[i], 16 * (e // 2))
                for h in range(2):
                    dve.wait_ge(dn_done, 2 * e + h + 1)
                    last = nc.vector.tensor_copy(y[:, i, h * 384:(h + 1) * 384], ps[:CAP, 4 + 2 * i + h, 0:384]).then_inc(dn_out, 1)
            for t in range(T):
                nc.vector.scalar_tensor_tensor(X[:, t, :], XN[:, t, :], kb[:, t:t + 1], X[:, t, :], ALU.mult, ALU.add).then_inc(comb, 1)
            for t in range(T):
                dve.wait_ge(bl[t % 2], 16 * (t // 2 + 1))
                dve.wait_ge(comb, t + 1)
                nc.vector.scalar_tensor_tensor(X[:, t, :], back[:, t % 2, :], ka[:, t:t + 1], X[:, t, :], ALU.mult, ALU.add).then_inc(comb1, 1)


def gat_project(nc, name, ins, keys, XT, hx, al, heads, MN, CT, ident, ps, make_mask):
    wkey, skey, dkey = keys
    C = D // heads
    HALF = D // 2
    WIDE = HALF + heads
    with ExitStack() as c:
        def sb(n, shape, dt=F32):
            return c.enter_context(nc.sbuf_tensor(name + n, shape, dt))

        def sem(n):
            return new_sem(nc, c, name + n)

        w = sb("w", [128, K, 2, WIDE])
        a = sb("a", [128, 2, D])
        prod = sb("prod", [128, 2, D])
        loaded, prod_done, folded, ones_done = sem("loaded"), sem("prod_done"), sem("folded"), sem("ones_done")
        h_done, h_out, m_done, m_act, m_dve = sem("h_done"), sem("h_out"), sem("m_done"), sem("m_act"), sem("m_dve")
        block = c.enter_context(nc.Block(no_gpsimd_drain=True))
        MB = 4

        @block.sync
        def _(sp):
            for h in range(2):
                sp.dma_start(w[:, :, h, 0:HALF], ins[wkey].rearrange("(k p) (h n) -> p k h n", p=128, h=2)[:, :, h, :]).then_inc(loaded, 16)
            for i, key in enumerate((skey, dkey)):
                sp.dma_start(a[:, i, :], ins[key].rearrange("h c -> (h c)").partition_broadcast(128)).then_inc(loaded, 16)

        @block.gpsimd
        def _(pool):
            nc.gpsimd.memset(hx[:, :, :, C:C + 1], 1.0).then_inc(ones_done, 1)
            pool.wait_ge(ones_done, 1)

        @block.vector
        def _(dve):
            dve.wait_ge(loaded, 64)
            for k in range(K):
                for i in range(2):
                    j = 2 * k + i
                    nc.vector.tensor_tensor(prod[:, j % 2, :].rearrange("p (h n) -> p h n", h=2), w[:, k, :, 0:HALF],
                                            a[:, i, :].rearrange("p (h n) -> p h n", h=2), ALU.mult).then_inc(prod_done, 1)
                    dve.wait_ge(prod_done, j + 1)
                    nc.vector.tensor_reduce(w[:, k, i, HALF:WIDE], prod[:, j % 2, :].rearrange("p (h c) -> p h c", h=heads),
                                            AX.X, ALU.add).then_inc(folded, 1)
            if make_mask:
                for t in range(T):
                    for q, n in ((0, 4), (1, 4), (2, 2)):
                        i = 3 * t + q
                        dve.wait_ge(m_done, i + 1)
                        nc.vector.tensor_scalar(MN[:, t, q * 500:q * 500 + n * NT], ps[:NT, 4 + i % MB, 0:n * NT],
                                                0.0, -BIG, ALU.is_equal, ALU.mult).then_inc(m_dve, 1)

        @block.scalar
        def _(act):
            for t in range(T):
                for h in range(2):
                    i = 2 * t + h
                    act.wait_ge(h_done, i + 1)
                    if heads > 1:
                        hh = heads // 2
                        out = hx[:, t, h * hh:(h + 1) * hh, 0:C]
                        in_ = ps[:NT, i % 4, 0:HALF].rearrange("p (g c) -> p g c", g=hh)
                    else:
                        out, in_ = hx[:, t, 0, h * HALF:(h + 1) * HALF], ps[:NT, i % 4, 0:HALF]
                    nc.scalar.activation(out, in_, ACT.Copy)
                    nc.scalar.activation(al[:, t, h * heads:(h + 1) * heads], ps[:NT, i % 4, HALF:WIDE], ACT.Copy).then_inc(h_out, 1)

        @block.tensor
        def _(pe):
            if make_mask:
                for t in range(T):
                    for q, n in ((0, 4), (1, 4), (2, 2)):
                        i = 3 * t + q
                        if i >= MB:
                            pe.wait_ge(m_dve, i - MB + 1)
                        for j in range(n):
                            last = nc.tensor.transpose(ps[:NT, 4 + i % MB, j * NT:(j + 1) * NT],
                                                       CT[:, 4 * q + j, t * NT:(t + 1) * NT], ident[:NT, :NT])
                        last.then_inc(m_done, 1)
            pe.wait_ge(folded, 2 * K)
            for t in range(T):
                for h in range(2):
                    i = 2 * t + h
                    if i >= 4:
                        pe.wait_ge(h_out, i - 3)
                    for k in range(K):
                        last = nc.tensor.matmul(ps[:NT, i % 4, 0:WIDE], XT[:, k, t * NT:(t + 1) * NT], w[:, k, h, :],
                                                start=(k == 0), stop=(k == K - 1))
                    last.then_inc(h_done, 1)


def gat_attention(nc, name, ins, hx, al, heads, MN, CT, ident, ps, ald, out, P_in_CT):
    C = D // heads
    ER, PR = 3, 2
    with ExitStack() as c:
        def sb(n, shape, dt=F32):
            return c.enter_context(nc.sbuf_tensor(name + n, shape, dt))

        def sem(n):
            return new_sem(nc, c, name + n)

        srow = sb("srow", [NT, 2, N])
        fifth = sb("fifth", [NT, N])
        d08 = sb("d08", [NT, T, heads])
        junk = sb("junk", [NT, N], BF16)
        mx = sb("mx", [NT, 2, T])
        shift = sb("shift", [NT, 2, 2, T])
        E = sb("E", [NT, ER, N])
        alr = E[0:16, 0, :]
        P = None if P_in_CT else sb("P", [NT, PR, T, NT])
        r_done, d_done, fifth_done = sem("r_done"), sem("d_done"), sem("fifth_done")
        rz = sb("rz", [NT, 2, T])
        al_T, al_sb, al_st, s_ld = sem("al_T"), sem("al_sb"), sem("al_st"), [sem("s_ld0"), sem("s_ld1")]
        mx_done, v, shift_done, y_done, e_done, eT_done, p_done, o_done, o_out, e_used = (
            sem("mx_done"), sem("v"), sem("shift_done"), sem("y_done"), sem("e_done"), sem("eT_done"), sem("p_done"),
            sem("o_done"), sem("o_out"), sem("e_used"))
        block = c.enter_context(nc.Block(no_gpsimd_drain=True))

        @block.sync
        def _(sp):
            sp.wait_ge(al_sb, 3)
            sp.dma_start(ald[0:2 * heads, :], alr[0:2 * heads, :]).then_inc(al_st, 16)
            sp.wait_ge(al_st, 16)
            for h in range(heads):
                if h >= 2:
                    sp.wait_ge(r_done, T * (h - 1))
                    sp.wait_ge(mx_done, T * (h - 1))
                sp.dma_start(srow[:, h % 2, :], ald[h:h + 1, :].rearrange("a n -> (a n)").partition_broadcast(NT)).then_inc(s_ld[h % 2], 16)

        @block.tensor
        def _(pe):
            for q, n in ((0, 4), (1, 4), (2, 2)):
                for j in range(n):
                    last = nc.tensor.transpose(ps[:2 * heads, q, j * NT:(j + 1) * NT], al[:, 4 * q + j, :], ident[:NT, :NT])
                last.then_inc(al_T, 1)
            pe.wait_ge(al_sb, 3)

            def turn(h, t):
                i = h * T + t
                pe.wait_ge(e_done, i + 1)
                for q, n in ((0, 4), (1, 4), (2, 2)):
                    g = 3 * i + q
                    if g >= 4:
                        pe.wait_ge(p_done, g - 3)
                    for j in range(n):
                        last = nc.tensor.transpose(ps[:NT, g % 4, j * NT:(j + 1) * NT], E[:, i % ER, (4 * q + j) * NT:(4 * q + j + 1) * NT],
                                                   ident[:NT, :NT])
                    last.then_inc(eT_done, 1)

            def weigh(h, t):
                i = h * T + t
                pe.wait_ge(p_done, 3 * i + 3)
                if heads > 1:
                    if i >= 4:
                        pe.wait_ge(o_out, i - 3)
                    for s in range(T):
                        last = nc.tensor.matmul(ps[:NT, 4 + i % 4, 0:C + 1], P[:, i % PR, s, 0:NT], hx[:, s, h, :],
                                                start=(s == 0), stop=(s == T - 1))
                    last.then_inc(o_done, 1)
                else:
                    for half in range(2):
                        g = 2 * i + half
                        if g >= 4:
                            pe.wait_ge(o_out, g - 3)
                        for s in range(T):
                            c0, c1 = (D // 2, D + 1) if half == 0 else (0, D // 2)
                            last = nc.tensor.matmul(ps[:NT, 4 + g % 4, 0:c1 - c0], CT[:, s, t * NT:(t + 1) * NT],
                                                    hx[:, s, 0, c0:c1], start=(s == 0), stop=(s == T - 1))
                        last.then_inc(o_done, 1)

            steps = [(h, t) for h in range(heads) for t in range(T)]
            turn(*steps[0])
            for i, (h, t) in enumerate(steps):
                if i + 1 < len(steps):
                    turn(*steps[i + 1])
                weigh(h, t)

        @block.scalar
        def _(act):
            for q, n in ((0, 500), (1, 500), (2, 250)):
                act.wait_ge(al_T, q + 1)
                nc.scalar.activation(alr[0:2 * heads, q * 500:q * 500 + n], ps[:2 * heads, q, 0:n], ACT.Copy).then_inc(al_sb, 1)

            act.wait_ge(d_done, 1)

            def relu(h, t):
                i = h * T + t
                if t == 0:
                    act.wait_ge(s_ld[h % 2], 16 * (h // 2 + 1))
                    if h:
                        act.wait_ge(y_done, T * h)
                    nc.scalar.activation(fifth[:], srow[:, h % 2, :], ACT.Copy, scale=0.2).then_inc(fifth_done, 1)
                if i >= ER:
                    act.wait_ge(eT_done, 3 * (i - ER + 1))
                nc.scalar.activation(E[:, i % ER, :], srow[:, h % 2, :], ACT.Relu, bias=d08[:, t, h:h + 1],
                                     scale=0.8).then_inc(r_done, 1)

            def expo(h, t):
                i = h * T + t
                act.wait_ge(y_done, i + 1)
                act.wait_ge(shift_done, h + 1)
                nc.scalar.activation(E[:, i % ER, :], E[:, i % ER, :], ACT.Exp, bias=shift[:, h % 2, 1, t:t + 1]).then_inc(e_done, 1)

            steps = [(h, t) for h in range(heads) for t in range(T)]
            relu(*steps[0])
            relu(*steps[1])
            for i, (h, t) in enumerate(steps):
                expo(h, t)
                if i + 2 < len(steps):
                    relu(*steps[i + 2])

        @block.gpsimd
        def _(pool):
            for i in range(heads * T):
                pool.wait_ge(r_done, i + 1)
                pool.wait_ge(fifth_done, i // T + 1)
                nc.gpsimd.tensor_tensor(E[:, i % ER, :], E[:, i % ER, :], fifth[:], ALU.add).then_inc(y_done, 1)

        @block.vector
        def _(dve):
            n = [0]

            def link(ins_):
                n[0] += 1
                ins_.then_inc(v, 1)
                dve.wait_ge(v, n[0])

            def maxima(h, t):
                if t == 0:
                    dve.wait_ge(s_ld[h % 2], 16 * (h // 2 + 1))
                k = h * T + t
                if k:
                    dve.wait_ge(mx_done, k)
                nc.vector.tensor_tensor_reduce(out=junk[:], in0=srow[:, h % 2, :], in1=MN[:, t, :], scale=1.0, scalar=-BIG,
                                               op0=ALU.add, op1=ALU.max, accum_out=mx[:, h % 2, t:t + 1]).then_inc(mx_done, 1)

            def shifts(h):
                a, b = shift[:, h % 2, 0], shift[:, h % 2, 1]
                dve.wait_ge(mx_done, T * (h + 1))
                if h >= 2:
                    dve.wait_ge(e_done, T * (h - 1))
                link(nc.vector.tensor_tensor(a, mx[:, h % 2], al[:, :, heads + h], ALU.add))
                link(nc.vector.tensor_scalar(a, a, 0.0, -0.8, ALU.max, ALU.mult))
                nc.vector.scalar_tensor_tensor(b, mx[:, h % 2], -0.2, a, ALU.mult, ALU.add).then_inc(shift_done, 1)

            def masked(h, t):
                i = h * T + t
                for q, m in ((0, 4), (1, 4), (2, 2)):
                    g = 3 * i + q
                    dve.wait_ge(eT_done, g + 1)
                    if not P_in_CT and i >= PR:
                        dve.wait_ge(o_done, i - PR + 1)
                    ct = CT[:, 4 * q:4 * q + m, t * NT:(t + 1) * NT]
                    dst = ct if P_in_CT else P[:, i % PR, 4 * q:4 * q + m, 0:NT]
                    nc.vector.scalar_tensor_tensor(dst, ps[:NT, g % 4, 0:m * NT].rearrange("p (j n) -> p j n", j=m), 2.0, ct,
                                                   ALU.min, ALU.mult).then_inc(p_done, 1)

            finish = finish_gat2(out) if P_in_CT else finish_gat1(out)
            nc.vector.tensor_scalar(d08[:], al[:, :, heads:2 * heads], 0.8, None, ALU.mult).then_inc(d_done, 1)
            for t in range(T):
                maxima(0, t)
            shifts(0)
            for h in range(heads):
                for t in range(T):
                    masked(h, t)
                    if h + 1 < heads:
                        maxima(h + 1, t)
                    if t == T - 1 and h + 1 < heads:
                        shifts(h + 1)
                    if t >= 1:
                        finish(dve, nc, ps, o_done, o_out, rz, link, h, t - 1)
                finish(dve, nc, ps, o_done, o_out, rz, link, h, T - 1)


def finish_gat1(out):
    C = 96

    def finish(dve, nc, ps, o_done, o_out, rz, link, h, t):
        i = h * T + t
        dve.wait_ge(o_done, i + 1)
        acc = ps[:NT, 4 + i % 4, :]
        link(nc.vector.tensor_scalar(rz[:, h % 2, t:t + 1], acc[:, C:C + 1], 1e-16, None, ALU.add))
        link(nc.vector.reciprocal(rz[:, h % 2, t:t + 1], rz[:, h % 2, t:t + 1]))
        nc.vector.tensor_scalar(out[:, t, h * C:(h + 1) * C], acc[:, 0:C], rz[:, h % 2, t:t + 1], None,
                                ALU.mult).then_inc(o_out, 1)
    return finish


def finish_gat2(X):
    def finish(dve, nc, ps, o_done, o_out, rz, link, h, t):
        half = D // 2
        for part in range(2):
            g = 2 * t + part
            dve.wait_ge(o_done, g + 1)
            acc = ps[:NT, 4 + g % 4, :]
            if part == 0:
                link(nc.vector.tensor_scalar(rz[:, 0, t:t + 1], acc[:, half:half + 1], 1e-16, None, ALU.add))
                link(nc.vector.reciprocal(rz[:, 0, t:t + 1], rz[:, 0, t:t + 1]))
            dst = X[:, t, half:D] if part == 0 else X[:, t, 0:half]
            nc.vector.scalar_tensor_tensor(dst, acc[:, 0:half], rz[:, 0, t:t + 1], dst, ALU.mult, ALU.add).then_inc(o_out, 1)
    return finish


def elu_and_bias(nc, ins, O1, X):
    with ExitStack() as c:
        b2 = c.enter_context(nc.sbuf_tensor("elu_b2", [NT, D], F32))
        b1 = c.enter_context(nc.sbuf_tensor("elu_b1", [NT, D], F32))
        tmp = c.enter_context(nc.sbuf_tensor("elu_tmp", [NT, 3, D], F32))
        biased = new_sem(nc, c, "elu_biased")
        loaded, low, ex, added, out = (new_sem(nc, c, "elu_" + n) for n in ("loaded", "low", "ex", "added", "out"))
        block = c.enter_context(nc.Block(no_gpsimd_drain=True))

        @block.sync
        def _(sp):
            sp.dma_start(b2[:], ins["L1_gnn_b2"].partition_broadcast(NT)).then_inc(loaded, 16)
            sp.dma_start(b1[:], ins["L1_gnn_b1"].partition_broadcast(NT)).then_inc(loaded, 16)

        @block.gpsimd
        def _(pool):
            pool.wait_ge(loaded, 32)
            for t in range(T):
                nc.gpsimd.tensor_tensor(X[:, t, :], X[:, t, :], b2[:], ALU.add).then_inc(added, 1)
            pool.wait_ge(added, T)

        @block.scalar
        def _(act):
            for t in range(T):
                act.wait_ge(low, t + 1)
                nc.scalar.activation(tmp[:, t % 3, :], tmp[:, t % 3, :], ACT.Exp).then_inc(ex, 1)

        @block.vector
        def _(dve):
            def lower(t):
                if t >= 3:
                    dve.wait_ge(out, 2 * (t - 2))
                nc.vector.tensor_tensor(O1[:, t, :], O1[:, t, :], b1[:], ALU.add).then_inc(biased, 1)
                dve.wait_ge(biased, t + 1)
                nc.vector.tensor_scalar(tmp[:, t % 3, :], O1[:, t, :], 0.0, None, ALU.min).then_inc(low, 1)
            dve.wait_ge(loaded, 32)
            lower(0)
            lower(1)
            for t in range(T):
                if t + 2 < T:
                    lower(t + 2)
                nc.vector.tensor_scalar(O1[:, t, :], O1[:, t, :], 0.0, -1.0, ALU.max, ALU.add).then_inc(out, 1)
                dve.wait_ge(ex, t + 1)
                dve.wait_ge(out, 2 * t + 1)
                nc.vector.tensor_tensor(O1[:, t, :], O1[:, t, :], tmp[:, t % 3, :], ALU.add).then_inc(out, 1)


HD, E_ATT = 256, 3
F32R = mybir.dt.float32r


def expert_attention(nc, ins, XT, X, ident, ps, out):
    SCALE = 1.0 / math.sqrt(HD)
    WT = 8
    WR = 3
    PR = 2
    xh, xl = XT
    with ExitStack() as c:
        def sb(n, shape, dt=F32):
            return c.enter_context(nc.sbuf_tensor("a_" + n, shape, dt))

        def sem(n):
            return new_sem(nc, c, "a_" + n)

        raw = sb("raw", [128, 2, D])
        wh, wl = sb("wh", [128, WR, D], F32R), sb("wl", [128, WR, D], F32R)
        bqk = sb("bqk", [128, 2 * K])
        bv, bp = sb("bv", [NT, E_ATT, HD]), sb("bp", [NT, D])
        cw, cb = sb("cw", [128, 2, 3]), sb("cb", [128, 2])
        wg1, bg1 = sb("wg1", [128, K, 32]), sb("bg1", [32, 1])
        g1h, g1l = sb("g1h", [128, K, 32], F32R), sb("g1l", [128, K, 32], F32R)
        wg2, bg2 = sb("wg2", [32, E_ATT]), sb("bg2", [NT, E_ATT])
        lg, p, we = (sb(x, [NT, T, E_ATT]) for x in ("lg", "p", "we"))
        c1, c2, mg = (sb(x, [NT, T]) for x in ("c1", "c2", "mg"))
        qkh, qkl = sb("qkh", [128, 4, N + 2], F32R), sb("qkl", [128, 4, N + 2], F32R)
        vh, vl = sb("vh", [NT, T, HD], F32R), sb("vl", [NT, T, HD], F32R)
        E = sb("E", [128, 2, N])
        g1 = E[:32, 1, :]
        PTh, PTl = sb("PTh", [NT, PR, 4, NT + 1], F32R), sb("PTl", [NT, PR, 4, NT + 1], F32R)
        YTh, YTl = sb("YTh", [128, 2, 2, NT + 1], F32R), sb("YTl", [128, 2, 2, NT + 1], F32R)
        Y = sb("Y", [NT, 2, HD])
        wbv = sb("wbv", [NT, HD])
        eye_b, causal_b = sb("eye_b", [NT, NT], BF16), sb("causal_b", [NT, NT], BF16)
        mx, rs = sb("mx", [NT, 2, 5]), sb("rs", [NT, 2, 5])

        loaded, wraw, split_h, split, biased = (
            sem("loaded"), [sem("wraw0"), sem("wraw1")], sem("split_h"), sem("split"), sem("biased"))
        wg1_loaded, bg1_loaded, g2_done = sem("wg1_loaded"), sem("bg1_loaded"), sem("g2_done")
        masks, gsplit, g1_done, g1_out, e_in, e_out, v = (
            sem("masks"), sem("gsplit"), sem("g1_done"), sem("g1_out"), sem("e_in"), sem("e_out"), sem("v"))
        pj_done, pj_hi, pj_lo, conv_in, conv_done = sem("pj_done"), sem("pj_hi"), sem("pj_lo"), sem("conv_in"), sem("conv_done")
        s_done, m_done, x_done, tr_done, tr_hi, tr_lo, pv_done, y_out, o_done, o_out, stored = (
            sem("s_done"), sem("m_done"), sem("x_done"), sem("tr_done"), sem("tr_hi"), sem("tr_lo"), sem("pv_done"),
            sem("y_out"), sem("o_done"), sem("o_out"), sem("stored"))
        block = c.enter_context(nc.Block(no_gpsimd_drain=True))

        def blocks(i):
            return [(q, min(4, i + 1 - 4 * q)) for q in range(i // 4 + 1)]

        PJ = 12 + T
        order, pt_no, yt_at, pt_at = [], 0, {}, {}
        for e in range(E_ATT):
            for i in range(T + 1):
                if i < T:
                    for q, n in blocks(i):
                        pt_at[e, i, q] = (len(order), pt_no)
                        order.append(("P", e, i, q, n, pt_no))
                        pt_no += 1
                if i >= 1:
                    yt_at[e, i - 1] = len(order)
                    order.append(("Y", e, i - 1))

        @block.sync
        def _(sp):
            def load(dst, src, small=False):
                sp.dma_start(dst, src, allow_slow_non_contiguous=small).then_inc(loaded, 16)
            sp.dma_start(wg1[:], ins["L1_ffn_Wg1"].rearrange("(k p) g -> p k g", p=128)).then_inc(wg1_loaded, 16)
            sp.dma_start(bg1[:], ins["L1_ffn_bg1"].rearrange("(g a) -> g a", a=1), allow_slow_non_contiguous=True).then_inc(bg1_loaded, 16)

            def tile_source(n):
                e, j = divmod(n, WT)
                if j < 4:
                    col = (j // 2) * D + e * HD + (j % 2) * 128
                    return ins["L1_ffn_Wqk"][:, col:col + 128].rearrange("(k p) n -> p k n", p=128)
                if j < 6:
                    return ins["L1_ffn_Wv"][e][(j - 4) * 384:(j - 3) * 384, :].rearrange("(k p) n -> p k n", p=128)
                row = e * HD + (j - 6) * 128
                return ins["L1_ffn_Wp"][row:row + 128, :]

            for n in range(E_ATT * WT):
                if n >= 2:
                    sp.wait_ge(split, n - 1)
                dst = raw[:, n % 2, :]
                if n % WT < 6:
                    dst = dst.rearrange("p (k n) -> p k n", k=K if n % WT < 4 else K // 2)
                sp.dma_start(dst, tile_source(n)).then_inc(wraw[n % 2], 16)
                if n == 1:
                    load(wg2[:], ins["L1_ffn_Wg2"])
                    load(bg2[:], ins["L1_ffn_bg2"].partition_broadcast(NT))
                    load(bqk[:], ins["L1_ffn_bqk"].rearrange("(m p) -> p m", p=128), True)
                    load(bv[:], ins["L1_ffn_bv"].partition_broadcast(NT))
                    load(bp[:], ins["L1_ffn_bp"].partition_broadcast(NT))
                    load(cw[:], ins["L1_ffn_conv_w"].rearrange("(k p) a w -> p k (a w)", p=128), True)
                    load(cb[:], ins["L1_ffn_conv_b"].rearrange("(k p) -> p k", p=128), True)
            for t in range(T):
                sp.wait_ge(o_out, 2 * T * (E_ATT - 1) + 2 * t + 2)
                sp.dma_start(out[t * NT:(t + 1) * NT, :], X[:, t, :]).then_inc(stored, 16)
            sp.wait_ge(stored, 16 * T)

        @block.gpsimd
        def _(pool):
            def split_tile(n):
                pool.wait_ge(wraw[n % 2], 16 * (n // 2 + 1))
                if n >= WR:
                    e, j = divmod(n - WR, WT)
                    if j < 6:
                        pool.wait_ge(pj_done, e * PJ + (3 * j + 3 if j < 4 else PJ))
                    else:
                        pool.wait_ge(o_done, 2 * T * (e + 1))
                nc.gpsimd.tensor_copy(wh[:, n % WR, :], raw[:, n % 2, :]).then_inc(split_h, 1)
                pool.wait_ge(split_h, n + 1)
                nc.gpsimd.tensor_tensor(wl[:, n % WR, :], raw[:, n % 2, :], wh[:, n % WR, :].bitcast(F32),
                                        ALU.subtract).then_inc(split, 1)
            split_tile(0)
            split_tile(1)
            nc.gpsimd.memset(eye_b[:], 0.0).then_inc(masks, 1)
            nc.gpsimd.memset(causal_b[:], 0.0).then_inc(masks, 1)
            pool.wait_ge(masks, 2)
            nc.gpsimd.affine_select(out=eye_b[:], in_=eye_b[:], compare_op=ALU.not_equal, fill=1.0, base=0,
                                    pattern=[[-1, NT]], channel_multiplier=1).then_inc(masks, 1)
            nc.gpsimd.affine_select(out=causal_b[:], in_=causal_b[:], compare_op=ALU.is_ge, fill=-BIG, base=0,
                                    pattern=[[-1, NT]], channel_multiplier=1).then_inc(masks, 1)
            split_tile(2)
            pool.wait_ge(loaded, 16 * 7)
            for t in range(T):
                nc.gpsimd.tensor_tensor(X[:, t, :], X[:, t, :], bp[:], ALU.add).then_inc(biased, 1)
                if t % 4 == 3:
                    split_tile(3 + t // 4)
            for n in range(5, E_ATT * WT):
                split_tile(n)
            pool.wait_ge(split, E_ATT * WT)

        @block.tensor
        def _(pe):
            def three(out_, a, b, first, last):
                nc.tensor.matmul(out_, a[0], b[0], start=first, stop=False)
                nc.tensor.matmul(out_, a[0], b[1], start=False, stop=False)
                return nc.tensor.matmul(out_, a[1], b[0], start=False, stop=last)

            pe.wait_ge(gsplit, 2)
            for g, (n0, nn) in enumerate(CHUNKS):
                for k in range(K):
                    last = three(ps[:32, 3 + g, 0:nn], (g1h[:, k, :], g1l[:, k, :]),
                                 (xh[:, k, n0:n0 + nn], xl[:, k, n0:n0 + nn]), k == 0, k == K - 1)
                last.then_inc(g1_done, 1)

            def gate_scores():
                pe.wait_ge(g1_out, len(CHUNKS))
                pe.wait_ge(loaded, 16 * 7)
                for t in range(T):
                    last = nc.tensor.matmul(ps[:NT, 6, t * E_ATT:(t + 1) * E_ATT], g1[:, t * NT:(t + 1) * NT], wg2[:],
                                            start=True, stop=True)
                last.then_inc(g2_done, 1)

            def project(e):
                for m in range(4):
                    n = e * WT + m
                    pe.wait_ge(split, n + 1)
                    w = [a[:, n % WR, :].rearrange("p (k n) -> p k n", k=K) for a in (wh, wl)]
                    if e == 0 and m == 1:
                        gate_scores()
                    for g, (n0, nn) in enumerate(CHUNKS):
                        i = e * PJ + 3 * m + g
                        if i >= 3:
                            pe.wait_ge(pj_hi, i - 2)
                        if i >= 9:
                            pe.wait_ge(pj_lo, i - 2)
                        for k in range(K):
                            last = three(ps[:, i % 3, 0:nn], (w[0][:, k, :], w[1][:, k, :]),
                                         (xh[:, k, n0:n0 + nn], xl[:, k, n0:n0 + nn]), k == 0, k == K - 1)
                        last.then_inc(pj_done, 1)
                n = e * WT + 4
                pe.wait_ge(split, n + 2)
                for t in range(T):
                    i = e * PJ + 12 + t
                    pe.wait_ge(pj_hi, i - 2)
                    pe.wait_ge(pj_lo, i - 2)
                    for k in range(K):
                        j, row = divmod(k, K // 2)
                        w = [a[:, (n + j) % WR, row * HD:(row + 1) * HD] for a in (wh, wl)]
                        a = (xh[:, k, t * NT:(t + 1) * NT], xl[:, k, t * NT:(t + 1) * NT])
                        last = three(ps[:NT, i % 3, 0:HD], a, w, k == 0, k == K - 1)
                    last.then_inc(pj_done, 1)

            def scores(e, i):
                z = e * T + i
                if i == 0:
                    pe.wait_ge(pj_hi, (e + 1) * PJ)
                    pe.wait_ge(pj_lo, (e + 1) * PJ)
                elif z:
                    pe.wait_ge(x_done, z)
                for q, n in blocks(i):
                    width = n * NT + n % 2
                    for m in range(2):
                        a = (qkh[:, m, i * NT:(i + 1) * NT], qkl[:, m, i * NT:(i + 1) * NT])
                        b = (qkh[:, 2 + m, q * 500:q * 500 + width], qkl[:, 2 + m, q * 500:q * 500 + width])
                        last = three(ps[:NT, q, 0:width], a, b, m == 0, m == 1)
                        if m == 0 and q == i // 4:
                            at = (i - 4 * q) * NT
                            nc.tensor.matmul(ps[:NT, q, at:at + NT], eye_b[:], causal_b[:], start=False, stop=False,
                                             skip_group_check=True)
                last.then_inc(s_done, 1)

            def ring(g):
                if g >= 2:
                    pe.wait_ge(tr_hi, g - 1)
                    pe.wait_ge(tr_lo, g - 1)
                return ps[:, 3 + g % 2, :]

            def turn(e, i):
                pe.wait_ge(x_done, e * T + i + 1)
                for q, n in blocks(i):
                    g, _ = pt_at[e, i, q]
                    bank = ring(g)
                    for j in range(n):
                        s = 4 * q + j
                        last = nc.tensor.transpose(bank[:NT, j * NT:(j + 1) * NT],
                                                   E[:NT, (e * T + i) % 2, s * NT:(s + 1) * NT], ident[:NT, :NT])
                    last.then_inc(tr_done, 1)

            def values(e, i):
                z = e * T + i
                if z:
                    pe.wait_ge(y_out, z)
                for q, n in blocks(i):
                    g, no = pt_at[e, i, q]
                    pe.wait_ge(tr_hi, g + 1)
                    pe.wait_ge(tr_lo, g + 1)
                    for j in range(n):
                        s = 4 * q + j
                        a = (PTh[:, no % PR, j, 0:NT], PTl[:, no % PR, j, 0:NT])
                        last = three(ps[:NT, 5, 0:HD], a, (vh[:, s, :], vl[:, s, :]), s == 0, s == i)
                    last.then_inc(pv_done, 1)

            def finish(e, i):
                z = e * T + i
                pe.wait_ge(y_out, z + 1)
                g = yt_at[e, i]
                bank = ring(g)
                for m in range(2):
                    last = nc.tensor.transpose(bank[:, m * NT:(m + 1) * NT], Y[:, z % 2, m * 128:(m + 1) * 128], ident[:NT, :NT])
                last.then_inc(tr_done, 1)

            def output(e, i):
                z = e * T + i
                g = yt_at[e, i]
                n = e * WT + 6
                pe.wait_ge(split, n + 2)
                pe.wait_ge(tr_hi, g + 1)
                pe.wait_ge(tr_lo, g + 1)
                for h in range(2):
                    if z:
                        pe.wait_ge(o_out, 2 * z + h - 1)
                    for m in range(2):
                        a = (YTh[:, z % 2, m, 0:NT], YTl[:, z % 2, m, 0:NT])
                        b = [w[:, (n + m) % WR, h * 384:(h + 1) * 384] for w in (wh, wl)]
                        last = three(ps[:NT, 6 + h, 0:384], a, b, m == 0, m == 1)
                    last.then_inc(o_done, 1)

            for e in range(E_ATT):
                project(e)
                scores(e, 0)
                for i in range(T):
                    turn(e, i)
                    if i >= 1:
                        finish(e, i - 1)
                    if i + 1 < T:
                        scores(e, i + 1)
                    values(e, i)
                    if i >= 1:
                        output(e, i - 1)
                finish(e, T - 1)
                output(e, T - 1)

        @block.scalar
        def _(act):
            act.wait_ge(wg1_loaded, 16)
            nc.scalar.activation(g1h[:], wg1[:], ACT.Copy).then_inc(gsplit, 1)
            act.wait_ge(bg1_loaded, 16)
            for g, (n0, nn) in enumerate(CHUNKS):
                act.wait_ge(g1_done, g + 1)
                nc.scalar.activation(g1[:, n0:n0 + nn], ps[:32, 3 + g, 0:nn], ACT.Relu, bias=bg1[:]).then_inc(g1_out, 1)
            act.wait_ge(loaded, 16 * 7)
            def gate_exps():
                act.wait_ge(e_in, 1)
                nc.scalar.activation(p[:], lg[:], ACT.Exp).then_inc(e_out, 1)
                act.wait_ge(e_in, 2)
                nc.scalar.activation(lg[:], p[:], ACT.Exp).then_inc(e_out, 1)

            def turned_hi(item):
                g = order.index(item)
                act.wait_ge(tr_done, g + 1)
                bank = ps[:, 3 + g % 2, :]
                if item[0] == "P":
                    _, e, i, q, n, no = item
                    if no >= PR:
                        act.wait_ge(pv_done, no - PR + 1)
                    nc.scalar.activation(PTh[:, no % PR, 0:n, 0:NT], bank[:NT, 0:n * NT].rearrange("p (j n) -> p j n", j=n),
                                         ACT.Copy).then_inc(tr_hi, 1)
                else:
                    _, e, i = item
                    z = e * T + i
                    if z >= 2:
                        act.wait_ge(o_done, 2 * (z - 1))
                    nc.scalar.activation(YTh[:, z % 2, :, 0:NT], bank[:, 0:2 * NT].rearrange("p (j n) -> p j n", j=2),
                                         ACT.Copy).then_inc(tr_hi, 1)

            def exps(e, i):
                z = e * T + i
                act.wait_ge(m_done, z + 1)
                if i >= 2:
                    act.wait_ge(tr_done, yt_at[e, i - 2])
                for q, n in blocks(i):
                    last = nc.scalar.activation(E[:NT, z % 2, q * 500:q * 500 + n * NT], ps[:NT, q, 0:n * NT], ACT.Exp,
                                                bias=mx[:, z % 2, 4:5], scale=SCALE, accum_out=rs[:, z % 2, q:q + 1])
                last.then_inc(x_done, 1)

            for e in range(E_ATT):
                for m in range(4):
                    for g, (n0, nn) in enumerate(CHUNKS):
                        i = e * PJ + 3 * m + g
                        bank = ps[:, i % 3, 0:nn]
                        bias = bqk[:, (m // 2) * K + 2 * e + m % 2:(m // 2) * K + 2 * e + m % 2 + 1]
                        act.wait_ge(pj_done, i + 1)
                        if e == 0 and m < 2:
                            if m == 1 and g == 0:
                                act.wait_ge(conv_done, 1)
                            nc.scalar.activation(E[:, 0, n0:n0 + nn], bank, ACT.Identity, bias=bias).then_inc(pj_hi, 1)
                        else:
                            nc.scalar.activation(qkh[:, m, n0:n0 + nn], bank, ACT.Identity, bias=bias).then_inc(pj_hi, 1)
                    if e == 0 and m < 2:
                        act.wait_ge(conv_done, m + 1)
                        nc.scalar.activation(qkh[:, m, 0:N], E[:, 1, :], ACT.Copy).then_inc(conv_in, 1)
                if e == 0:
                    gate_exps()
                for t in range(T):
                    i = e * PJ + 12 + t
                    act.wait_ge(pj_done, i + 1)
                    nc.scalar.activation(vh[:, t, :], ps[:NT, i % 3, 0:HD], ACT.Copy).then_inc(pj_hi, 1)
                exps(e, 0)
                for i in range(T):
                    for q, n in blocks(i):
                        turned_hi(order[pt_at[e, i, q][0]])
                    if i >= 1:
                        turned_hi(order[yt_at[e, i - 1]])
                    if i + 1 < T:
                        exps(e, i + 1)
                turned_hi(order[yt_at[e, T - 1]])

        @block.vector
        def _(dve):
            n_link = [0]

            def link(ins_):
                n_link[0] += 1
                ins_.then_inc(v, 1)
                dve.wait_ge(v, n_link[0])

            def each(a, m=E_ATT):
                return a.unsqueeze(2).broadcast_to([NT, T, m])

            for a in (qkh, qkl):
                nc.vector.memset(a[:, :, N:N + 2].bitcast(F32), 0.0)
            dve.wait_ge(gsplit, 1)
            nc.vector.tensor_tensor(g1l[:], wg1[:], g1h[:].bitcast(F32), ALU.subtract).then_inc(gsplit, 1)
            dve.wait_ge(loaded, 16 * 7)

            def gate():
                dve.wait_ge(g2_done, 1)
                link(nc.vector.tensor_tensor(lg[:], ps[:NT, 6, 0:T * E_ATT].rearrange("p (t e) -> p t e", t=T), bg2[:].unsqueeze(1).broadcast_to([NT, T, E_ATT]), ALU.add))
                link(nc.vector.tensor_reduce(mg[:], lg[:], AX.X, ALU.max))
                nc.vector.tensor_tensor(lg[:], lg[:], each(mg[:]), ALU.subtract).then_inc(e_in, 1)
                dve.wait_ge(e_out, 1)
                link(nc.vector.tensor_reduce(mg[:], p[:], AX.X, ALU.add))
                link(nc.vector.reciprocal(mg[:], mg[:]))
                nc.vector.tensor_tensor(p[:], p[:], each(mg[:]), ALU.mult).then_inc(e_in, 1)
                dve.wait_ge(e_out, 2)
                for e in range(E_ATT):
                    a, b = [x for x in range(E_ATT) if x != e]
                    link(nc.vector.tensor_tensor(c1[:], p[:, :, a], p[:, :, e], ALU.is_ge if a < e else ALU.is_gt))
                    link(nc.vector.tensor_tensor(c2[:], p[:, :, b], p[:, :, e], ALU.is_ge if b < e else ALU.is_gt))
                    link(nc.vector.tensor_tensor(c1[:], c1[:], c2[:], ALU.mult))
                    link(nc.vector.tensor_scalar(c1[:], c1[:], -1.0, 1.0, ALU.mult, ALU.add))
                    link(nc.vector.tensor_tensor(we[:, :, e], lg[:, :, e], c1[:], ALU.mult))
                link(nc.vector.tensor_reduce(mg[:], we[:], AX.X, ALU.add))
                link(nc.vector.reciprocal(mg[:], mg[:]))
                link(nc.vector.tensor_tensor(we[:], we[:], each(mg[:]), ALU.mult))

            def convolve(m):
                q, qc = E[:, 0, :], E[:, 1, :]
                dve.wait_ge(pj_hi, 3 * m + 3)
                if m == 0:
                    dve.wait_ge(g2_done, 1)
                if m:
                    dve.wait_ge(conv_in, 1)
                    dve.wait_ge(pj_lo, 3)
                link(nc.vector.tensor_scalar(qc, q, cw[:, m, 1:2], cb[:, m:m + 1], ALU.mult, ALU.add))
                link(nc.vector.scalar_tensor_tensor(qc[:, 1:N], q[:, 0:N - 1], cw[:, m, 0:1], qc[:, 1:N], ALU.mult, ALU.add))
                nc.vector.scalar_tensor_tensor(qc[:, 0:N - 1], q[:, 1:N], cw[:, m, 2:3], qc[:, 0:N - 1], ALU.mult,
                                               ALU.add).then_inc(conv_done, 1)
                dve.wait_ge(conv_in, m + 1)
                nc.vector.tensor_tensor(qkl[:, m, 0:N], qc, qkh[:, m, 0:N].bitcast(F32), ALU.subtract).then_inc(pj_lo, 3)

            def maxima(e, i):
                z = e * T + i
                dve.wait_ge(s_done, z + 1)
                nq = len(blocks(i))
                for q, m in blocks(i):
                    last = nc.vector.tensor_reduce(mx[:, z % 2, q:q + 1], ps[:NT, q, 0:m * NT], AX.X, ALU.max)
                link(last)
                src = mx[:, z % 2, 0:1]
                if nq > 1:
                    link(nc.vector.tensor_reduce(mx[:, z % 2, 3:4], mx[:, z % 2, 0:nq], AX.X, ALU.max))
                    src = mx[:, z % 2, 3:4]
                nc.vector.tensor_scalar(mx[:, z % 2, 4:5], src, -SCALE, None, ALU.mult).then_inc(m_done, 1)

            def turned_lo(item):
                g = order.index(item)
                dve.wait_ge(tr_hi, g + 1)
                bank = ps[:, 3 + g % 2, :]
                if item[0] == "P":
                    _, e, i, q, n, no = item
                    nc.vector.tensor_tensor(PTl[:, no % PR, 0:n, 0:NT], bank[:NT, 0:n * NT].rearrange("p (j n) -> p j n", j=n),
                                            PTh[:, no % PR, 0:n, 0:NT].bitcast(F32), ALU.subtract).then_inc(tr_lo, 1)
                else:
                    _, e, i = item
                    z = e * T + i
                    nc.vector.tensor_tensor(YTl[:, z % 2, :, 0:NT], bank[:, 0:2 * NT].rearrange("p (j n) -> p j n", j=2),
                                            YTh[:, z % 2, :, 0:NT].bitcast(F32), ALU.subtract).then_inc(tr_lo, 1)

            def gate_scale(e, i):
                z = e * T + i
                nq = len(blocks(i))
                dve.wait_ge(x_done, z + 1)
                if z:
                    dve.wait_ge(y_out, z)
                nc.vector.tensor_scalar(wbv[:], bv[:, e, :], we[:, i, e:e + 1], None, ALU.mult)
                src = rs[:, z % 2, 0:1]
                if nq > 1:
                    link(nc.vector.tensor_reduce(rs[:, z % 2, 3:4], rs[:, z % 2, 0:nq], AX.X, ALU.add))
                    src = rs[:, z % 2, 3:4]
                link(nc.vector.reciprocal(rs[:, z % 2, 4:5], src))
                link(nc.vector.tensor_tensor(rs[:, z % 2, 4:5], rs[:, z % 2, 4:5], we[:, i, e:e + 1], ALU.mult))

            def outputs(e, i):
                z = e * T + i
                dve.wait_ge(pv_done, pt_at[e, i, len(blocks(i)) - 1][1] + 1)
                if i >= 2:
                    dve.wait_ge(tr_done, yt_at[e, i - 2] + 1)
                nc.vector.scalar_tensor_tensor(Y[:, z % 2, :], ps[:NT, 5, 0:HD], rs[:, z % 2, 4:5], wbv[:],
                                               ALU.mult, ALU.add).then_inc(y_out, 1)

            def add_output(e, i):
                z = e * T + i
                if z == 0:
                    dve.wait_ge(biased, T)
                for h in range(2):
                    dve.wait_ge(o_done, 2 * z + h + 1)
                    nc.vector.tensor_tensor(X[:, i, h * 384:(h + 1) * 384], X[:, i, h * 384:(h + 1) * 384], ps[:NT, 6 + h, 0:384],
                                            ALU.add).then_inc(o_out, 1)

            for e in range(E_ATT):
                for m in range(4):
                    if e == 0 and m < 2:
                        convolve(m)
                        continue
                    for g, (n0, nn) in enumerate(CHUNKS):
                        i = e * PJ + 3 * m + g
                        b = (m // 2) * K + 2 * e + m % 2
                        dve.wait_ge(pj_hi, i + 1)
                        nc.vector.scalar_tensor_tensor(qkl[:, m, n0:n0 + nn], ps[:, i % 3, 0:nn], bqk[:, b:b + 1],
                                                       qkh[:, m, n0:n0 + nn].bitcast(F32), ALU.add, ALU.subtract).then_inc(pj_lo, 1)
                if e == 0:
                    gate()
                for t in range(T):
                    i = e * PJ + 12 + t
                    dve.wait_ge(pj_hi, i + 1)
                    nc.vector.tensor_tensor(vl[:, t, :], ps[:NT, i % 3, 0:HD], vh[:, t, :].bitcast(F32), ALU.subtract).then_inc(pj_lo, 1)
                maxima(e, 0)
                for i in range(T):
                    gate_scale(e, i)
                    for q, n in blocks(i):
                        turned_lo(order[pt_at[e, i, q][0]])
                    if i >= 1:
                        turned_lo(order[yt_at[e, i - 1]])
                    if i + 1 < T:
                        maxima(e, i + 1)
                    outputs(e, i)
                    if i >= 1:
                        add_output(e, i - 1)
                turned_lo(order[yt_at[e, T - 1]])
                add_output(e, T - 1)


def transpose_split(nc, name, src, hi, lo, ident, ps):
    with ExitStack() as c:
        turned = new_sem(nc, c, name + "_turned")
        hi_out = new_sem(nc, c, name + "_hi_out")
        lo_out = new_sem(nc, c, name + "_lo_out")
        block = c.enter_context(nc.Block(no_gpsimd_drain=True))
        groups = [(t, h) for t in range(T) for h in range(2)]

        @block.tensor
        def _(pe):
            for g, (t, h) in enumerate(groups):
                if g >= BANKS:
                    pe.wait_ge(lo_out, g - BANKS + 1)
                for j in range(3):
                    k = 3 * h + j
                    last = nc.tensor.transpose(ps[:, g % BANKS, j * NT:(j + 1) * NT],
                                               src[:, t, k * 128:(k + 1) * 128], ident[:NT, :NT])
                last.then_inc(turned, 1)

        def place(g, dst):
            t, h = groups[g]
            return (dst[:, 3 * h:3 * h + 3, t * NT:(t + 1) * NT],
                    ps[:, g % BANKS, 0:3 * NT].rearrange("p (j n) -> p j n", j=3))

        @block.scalar
        def _(act):
            for g in range(len(groups)):
                act.wait_ge(turned, g + 1)
                dst, bank = place(g, hi)
                nc.scalar.activation(dst, bank, ACT.Copy).then_inc(hi_out, 1)

        @block.vector
        def _(dve):
            for g in range(len(groups)):
                dve.wait_ge(hi_out, g + 1)
                dst, bank = place(g, lo)
                nc.vector.tensor_tensor(dst, bank, place(g, hi)[0].bitcast(F32), ALU.subtract).then_inc(lo_out, 1)


def program(nc, ins, out):
    with ExitStack() as c:
        X = c.enter_context(nc.sbuf_tensor("X", [NT, T, D], F32))
        ident = c.enter_context(nc.sbuf_tensor("ident", [128, 128], F32))
        stat = c.enter_context(nc.sbuf_tensor("stat", [NT, T, 4], F32))
        eps = c.enter_context(nc.sbuf_tensor("eps", [128, 2], F32))
        ps = c.enter_context(nc.psum_tensor("ps", [128, BANKS, 512], F32))
        normd = nc.dram_tensor("normd", [N, D], F32).ap()
        eo = nc.dram_tensor("eo", [E_MOE * CAP, D], F32).ap()
        with ExitStack() as s:
            loaded = new_sem(nc, s, "x_loaded")
            made = new_sem(nc, s, "consts_made")
            block = s.enter_context(nc.Block(no_gpsimd_drain=True))

            @block.sync
            def _(sp):
                sp.dma_start(X[:], ins["x"].rearrange("(t p) d -> p t d", p=NT)).then_inc(loaded, 16)
                sp.wait_ge(loaded, 16)

            @block.gpsimd
            def _(pool):
                nc.gpsimd.memset(eps[:, 0:1], 1e-5)
                nc.gpsimd.memset(eps[:, 1:2], 1e-6)
                nc.gpsimd.memset(ident[:], 0.0).then_inc(made, 1)
                pool.wait_ge(made, 1)
                nc.gpsimd.affine_select(out=ident[:], in_=ident[:], compare_op=ALU.not_equal, fill=1.0,
                                        base=0, pattern=[[-1, 128]], channel_multiplier=1).then_inc(made, 1)
                pool.wait_ge(made, 2)
        first = ExitStack()
        A = first.enter_context(nc.sbuf_tensor("A", [128, T * 8 * 97], F32))
        XT = A[:, 0:K * N].rearrange("p (k n) -> p k n", k=K)
        ald = nc.dram_tensor("ald", [16, N], F32).ap()

        def by_node(area, width=D):
            return area[:NT, 0:T * width].rearrange("p (t d) -> p t d", t=T)

        with ExitStack() as graph:
            CT = graph.enter_context(nc.sbuf_tensor("CT", [NT, T, N], F32))
            with ExitStack() as early:
                ones = early.enter_context(nc.sbuf_tensor("ones", [128, 128], F32))
                cst = {"ident": ident, "ones": ones}
                moe = {n: early.enter_context(nc.sbuf_tensor("moe_" + n, [NT, T], F32)) for n in ("rp", "ka", "kb")}
                moe["slot"] = early.enter_context(nc.sbuf_tensor("moe_slot", [NT, T], I32))
                moe["tok"] = early.enter_context(nc.sbuf_tensor("moe_tok", [128, E_MOE // 2], I32))
                with ExitStack() as s:
                    XN = s.enter_context(nc.sbuf_tensor("XN0", [NT, T, D], F32))
                    layernorm(nc, "ln0", X, XN, stat, eps[:NT, 0:1])
                    transpose_nodes(nc, "t0", XN, XT, ident, ps)
                with ExitStack() as s:
                    MT = s.enter_context(nc.sbuf_tensor("MT", [NT, T, N], F32))
                    dense_graph(nc, ins, cst, MT, CT, ps)
                    low_rank_and_gcn(nc, ins, XT, MT, X, cst, stat, ones, ps)
                with ExitStack() as s:
                    XN = s.enter_context(nc.sbuf_tensor("XN1", [NT, T, D], F32))
                    layernorm(nc, "ln1", X, XN, stat, eps[:NT, 0:1])
                    route(nc, ins, cst, X, XN, XT, stat, eps[:NT, 1:2], moe, ps, normd)
                    experts(nc, ins, cst, X, XN, XT, moe, ps, normd, eo)
            B = graph.enter_context(nc.sbuf_tensor("B", [128, T * 8 * 97], F32))
            MN = graph.enter_context(nc.sbuf_tensor("MN", [NT, T, N], BF16))
            layernorm(nc, "ln2", X, by_node(B), stat, eps[:NT, 0:1])
            transpose_nodes(nc, "t2", by_node(B), XT, ident, ps)
            hx = B[:NT].rearrange("p (t h c) -> p t h c", t=T, h=8)
            O1 = by_node(A)
            with ExitStack() as s:
                al = s.enter_context(nc.sbuf_tensor("al1", [NT, T, 16], F32))
                gat_project(nc, "h1_", ins, ("L1_gnn_W1", "L1_gnn_a_src1", "L1_gnn_a_dst1"), XT, hx, al, 8, MN, CT, ident, ps, True)
                gat_attention(nc, "g1_", ins, hx, al, 8, MN, CT, ident, ps, ald, O1, False)
                elu_and_bias(nc, ins, O1, X)
            h1T = B[:, 0:K * N].rearrange("p (k n) -> p k n", k=K)
            transpose_nodes(nc, "t3", O1, h1T, ident, ps)
            hx = by_node(A, D + 1).unsqueeze(2)
            with ExitStack() as s:
                al = s.enter_context(nc.sbuf_tensor("al2", [NT, T, 2], F32))
                gat_project(nc, "h2_", ins, ("L1_gnn_W2", "L1_gnn_a_src2", "L1_gnn_a_dst2"), h1T, hx, al, 1, MN, CT, ident, ps, False)
                gat_attention(nc, "g2_", ins, hx, al, 1, MN, CT, ident, ps, ald, X, True)
        first.close()
        late = ExitStack()
        xh, xl = (late.enter_context(nc.sbuf_tensor(n, [128, K, N], F32R)) for n in ("xh", "xl"))
        with ExitStack() as s:
            XN = s.enter_context(nc.sbuf_tensor("XN3", [NT, T, D], F32))
            layernorm(nc, "ln3", X, XN, stat, eps[:NT, 0:1])
            transpose_split(nc, "t4", XN, xh, xl, ident, ps)
        expert_attention(nc, ins, (xh, xl), X, ident, ps, out)
        late.close()


_INS = ['x', 'src', 'dst', 'edge_weight', 'L0_gnn_Wd', 'L0_gnn_bd', 'L0_gnn_Wu', 'L0_gnn_bu', 'L0_gnn_W1',
        'L0_gnn_b1', 'L0_gnn_W2', 'L0_gnn_b2', 'L0_ffn_ln_w', 'L0_ffn_w_router', 'L0_ffn_wi', 'L0_ffn_wo',
        'L1_gnn_W1', 'L1_gnn_a_src1', 'L1_gnn_a_dst1', 'L1_gnn_b1', 'L1_gnn_W2', 'L1_gnn_a_src2',
        'L1_gnn_a_dst2', 'L1_gnn_b2', 'L1_ffn_Wqk', 'L1_ffn_bqk', 'L1_ffn_Wv', 'L1_ffn_bv', 'L1_ffn_conv_w',
        'L1_ffn_conv_b', 'L1_ffn_glob', 'L1_ffn_pos_bias', 'L1_ffn_Wg1', 'L1_ffn_bg1', 'L1_ffn_Wg2',
        'L1_ffn_bg2', 'L1_ffn_Wp', 'L1_ffn_bp']


def kernel(**inputs):
    import numpy as _np
    import concourse.bacc as _bacc
    from concourse import mybir as _mybir
    from concourse.bass_utils import run_bass_kernel_spmd as _run

    nc = _bacc.Bacc("TRN2", target_bir_lowering=False, num_devices=1)
    arrays, args = {}, {}
    for name in _INS:
        a = _np.ascontiguousarray(inputs[name])
        arrays[f"in_{name}_dram"] = a
        args[name] = nc.dram_tensor(f"in_{name}_dram", a.shape, _mybir.dt.from_np(a.dtype), kind="ExternalInput").ap()
    out = nc.dram_tensor("out_0_dram", (1250, 768), _mybir.dt.from_np(_np.dtype("float32")), kind="ExternalOutput").ap()
    program(nc, args, out)
    r = _run(nc, [arrays], core_ids=[0])
    return r.results[0]["out_0_dram"]
```
